# Optimizing a Trainium2 kernel written in Bass

```python
import numpy as np
import jax
import jax.numpy as jnp

def _softmax(x, axis=-1):
    return jax.nn.softmax(x, axis=axis)

def _gelu(x):
    return jax.nn.gelu(x, approximate=True)

def _silu(x):
    return jax.nn.silu(x)

def _sigmoid(x):
    return jax.nn.sigmoid(x)

def _layernorm(x, axis=-1, eps=1e-05):
    m = jnp.mean(x, axis=axis, keepdims=True)
    v = jnp.var(x, axis=axis, keepdims=True)
    return (x - m) / jnp.sqrt(v + eps)

def _scatter_add(tgt, idx, src, axis=0):
    return tgt.at[idx].add(src)

def _segment_sum(src, seg, n):
    return jax.ops.segment_sum(src, seg, n)
kernel_name = 'mk_sandwich_d1_jaxref_r4_9863d5'

def setup_inputs(seed: int=0):
    np.random.seed(seed)
    _w = jnp.asarray

    def _L0_attn_setup():
        import jax, jax.numpy as jnp
        import numpy as np
        HIDDEN = 1024
        N_HEADS = 32
        N_KV = 8
        HEAD_DIM = HIDDEN // N_HEADS
        Q_PER_KV = N_HEADS // N_KV
        SEQ = 512
        ROPE_BASE = 1000000.0
        POS_SCALE = 1.0
        SM_SCALE = 1.0 / HEAD_DIM
        BLOCK = 64
        LOCAL_BLOCKS = 16
        VERT_STRIDE = 8

        def _blocksparse_mask(seq_len):
            nb = seq_len // BLOCK
            qb = np.arange(nb)[:, None]
            kb = np.arange(nb)[None, :]
            bmask = (kb <= qb) & ((qb - kb < LOCAL_BLOCKS) | ((kb + 1) % VERT_STRIDE == 0))
            emask = np.kron(bmask, np.ones((BLOCK, BLOCK), dtype=bool))
            i = np.arange(seq_len)
            emask &= i[:, None] >= i[None, :]
            return jnp.asarray(emask)

        def _rope(x, cos, sin):
            x1, x2 = jnp.split(x, 2, axis=-1)
            rot = jnp.concatenate([-x2, x1], axis=-1)
            return x * cos[None, :, None, :] + rot * sin[None, :, None, :]
        key = jax.random.key(seed)
        k1, k2, k3, k4, k5 = jax.random.split(key, 5)
        qkv_out = (N_HEADS + 2 * N_KV) * HEAD_DIM
        return {'hidden_states': jax.random.normal(k1, (1, SEQ, HIDDEN), dtype=jnp.float32), 'w_qkv': jax.random.normal(k2, (qkv_out, HIDDEN), dtype=jnp.float32) * 0.02, 'b_qkv': jnp.zeros((qkv_out,), dtype=jnp.float32), 'w_dense': jax.random.normal(k3, (HIDDEN, HIDDEN), dtype=jnp.float32) * 0.02, 'b_dense': jnp.zeros((HIDDEN,), dtype=jnp.float32)}
    _L0_attn_in = _L0_attn_setup()

    def _L0_ffn_setup():
        import jax, jax.numpy as jnp
        import numpy as np
        NUM_EXPERTS = 8
        TOP_K = 2
        RANK = 16
        LORA_ALPHA = 32
        SCALING = LORA_ALPHA / RANK
        key = jax.random.key(seed)
        ks = jax.random.split(key, 6)
        B, S, D_IN, D_OUT = (4, 512, 1024, 1024)
        x = jax.random.normal(ks[0], (B, S, D_IN), dtype=jnp.float32)
        W_base = jax.random.normal(ks[1], (D_OUT, D_IN), dtype=jnp.float32) * 0.02
        b_base = jax.random.normal(ks[2], (D_OUT,), dtype=jnp.float32) * 0.02
        W_router = jax.random.normal(ks[3], (NUM_EXPERTS, D_IN), dtype=jnp.float32) * 0.02
        A = jax.random.normal(ks[4], (NUM_EXPERTS, RANK, D_IN), dtype=jnp.float32) * 0.02
        Bm = jax.random.normal(ks[5], (D_OUT, RANK), dtype=jnp.float32) * 0.02
        Bm = jnp.broadcast_to(Bm, (NUM_EXPERTS, D_OUT, RANK)) * jnp.arange(1, NUM_EXPERTS + 1, dtype=jnp.float32)[:, None, None] * 0.2
        return {'x': x, 'W_base': W_base, 'b_base': b_base, 'W_router': W_router, 'A': A, 'B': Bm}
    _L0_ffn_in = _L0_ffn_setup()
    _d = {'L0_attn_hidden_states': _L0_attn_in['hidden_states'], 'L0_attn_w_qkv': _L0_attn_in['w_qkv'], 'L0_attn_b_qkv': _L0_attn_in['b_qkv'], 'L0_attn_w_dense': _L0_attn_in['w_dense'], 'L0_attn_b_dense': _L0_attn_in['b_dense'], 'L0_ffn_W_base': _L0_ffn_in['W_base'], 'L0_ffn_b_base': _L0_ffn_in['b_base'], 'L0_ffn_W_router': _L0_ffn_in['W_router'], 'L0_ffn_A': _L0_ffn_in['A'], 'L0_ffn_B': _L0_ffn_in['B']}
    _x0 = _d['L0_attn_hidden_states']
    _d['L0_attn_hidden_states'] = jax.random.normal(jax.random.fold_in(jax.random.key(seed), 1), (2, 2048, 1024), dtype=_x0.dtype)
    del _x0
    return _d

def reference(L0_attn_hidden_states, L0_attn_w_qkv, L0_attn_b_qkv, L0_attn_w_dense, L0_attn_b_dense, L0_ffn_W_base, L0_ffn_b_base, L0_ffn_W_router, L0_ffn_A, L0_ffn_B):

    def _L0_attn_ref(hidden_states, w_qkv, b_qkv, w_dense, b_dense):
        import jax, jax.numpy as jnp
        import numpy as np
        HIDDEN = 1024
        N_HEADS = 32
        N_KV = 8
        HEAD_DIM = HIDDEN // N_HEADS
        Q_PER_KV = N_HEADS // N_KV
        SEQ = 512
        ROPE_BASE = 1000000.0
        POS_SCALE = 1.0
        SM_SCALE = 1.0 / HEAD_DIM
        BLOCK = 64
        LOCAL_BLOCKS = 16
        VERT_STRIDE = 8

        def _blocksparse_mask(seq_len):
            nb = seq_len // BLOCK
            qb = np.arange(nb)[:, None]
            kb = np.arange(nb)[None, :]
            bmask = (kb <= qb) & ((qb - kb < LOCAL_BLOCKS) | ((kb + 1) % VERT_STRIDE == 0))
            emask = np.kron(bmask, np.ones((BLOCK, BLOCK), dtype=bool))
            i = np.arange(seq_len)
            emask &= i[:, None] >= i[None, :]
            return jnp.asarray(emask)

        def _rope(x, cos, sin):
            x1, x2 = jnp.split(x, 2, axis=-1)
            rot = jnp.concatenate([-x2, x1], axis=-1)
            return x * cos[None, :, None, :] + rot * sin[None, :, None, :]
        B, S, _ = hidden_states.shape
        qkv = jnp.einsum('bsh,oh->bso', hidden_states, w_qkv) + b_qkv
        qkv = qkv.reshape(B, S, N_KV, Q_PER_KV + 2, HEAD_DIM)
        q = qkv[:, :, :, :Q_PER_KV].reshape(B, S, N_HEADS, HEAD_DIM)
        k = qkv[:, :, :, Q_PER_KV]
        v = qkv[:, :, :, Q_PER_KV + 1]
        inv_freq = 1.0 / ROPE_BASE ** (jnp.arange(0, HEAD_DIM, 2, dtype=jnp.float32) / HEAD_DIM)
        t = jnp.arange(S, dtype=jnp.float32) * POS_SCALE
        freqs = jnp.outer(t, inv_freq)
        emb = jnp.concatenate([freqs, freqs], axis=-1)
        cos, sin = (jnp.cos(emb), jnp.sin(emb))
        q = _rope(q, cos, sin)
        k = _rope(k, cos, sin)
        k = jnp.repeat(k, Q_PER_KV, axis=2)
        v = jnp.repeat(v, Q_PER_KV, axis=2)
        mask = _blocksparse_mask(S)
        scores = jnp.einsum('bqhd,bkhd->bhqk', q, k) * SM_SCALE
        scores = jnp.where(mask[None, None], scores, jnp.finfo(scores.dtype).min)
        probs = jax.nn.softmax(scores, axis=-1)
        ctx = jnp.einsum('bhqk,bkhd->bqhd', probs, v).reshape(B, S, HIDDEN)
        out = jnp.einsum('bsh,oh->bso', ctx, w_dense) + b_dense
        return out

    def _L0_ffn_ref(x, W_base, b_base, W_router, A, B):
        import jax, jax.numpy as jnp
        import numpy as np
        NUM_EXPERTS = 8
        TOP_K = 2
        RANK = 16
        LORA_ALPHA = 32
        SCALING = LORA_ALPHA / RANK
        bs, seq, d_in = x.shape
        T = bs * seq
        xf = x.reshape(T, d_in)
        base = xf @ W_base.T + b_base
        logits = xf @ W_router.T
        rw, sel = jax.lax.top_k(logits, TOP_K)
        rw = jax.nn.softmax(rw, axis=-1)
        onehot = jax.nn.one_hot(sel, NUM_EXPERTS, dtype=rw.dtype)
        w = jnp.einsum('tk,tke->te', rw, onehot)
        h = jnp.einsum('td,erd->ter', xf, A)
        lora = jnp.einsum('ter,te,eor->to', h, w, B) * SCALING
        return (base + lora).reshape(bs, seq, -1)
    x = L0_attn_hidden_states
    x = x + _layernorm(_L0_attn_ref(_layernorm(x, axis=-1), L0_attn_w_qkv, L0_attn_b_qkv, L0_attn_w_dense, L0_attn_b_dense), axis=-1)
    x = x + _layernorm(_L0_ffn_ref(_layernorm(x, axis=-1), L0_ffn_W_base, L0_ffn_b_base, L0_ffn_W_router, L0_ffn_A, L0_ffn_B), axis=-1)
    return x

_drawn_inputs = setup_inputs


def setup_inputs(seed=0):
    import zlib

    import numpy as np

    out = dict(_drawn_inputs(seed))
    spreads = {'L0_attn_b_qkv': (0.0, 0.1), 'L0_attn_b_dense': (0.0, 0.1)}
    factors = {'L0_ffn_b_base': 3.226}
    for name, (base, spread) in spreads.items():
        noise = np.random.default_rng([zlib.crc32(name.encode()), seed]).standard_normal(out[name].shape)
        drawn = base * np.exp(spread * noise) if base else spread * noise
        out[name] = jnp.asarray(drawn.astype(out[name].dtype))
    for name, factor in factors.items():
        out[name] = (out[name] * factor).astype(out[name].dtype)
    return out
```

```python
from contextlib import ExitStack

import numpy as np

import concourse.bass as bass
from concourse import mybir

F32 = mybir.dt.float32
F32R = mybir.dt.float32r
BF16 = mybir.dt.bfloat16
ALU = mybir.AluOpType
ACT = mybir.ActivationFunctionType
AX = mybir.AxisListType

P = 128
BATCH, SEQ, HID = 2, 2048, 1024
HEADS, GROUPS = 32, 8
HD = HID // HEADS
QPG = HEADS // GROUPS
EXPERTS, RANK = 8, 16
ER = EXPERTS * RANK
KC = HID // P
TG = 512
NTG = BATCH * SEQ // TG
TPG = TG // P
UPB = SEQ // TG
QK_TILES = GROUPS + GROUPS * HD // P
BLOCK, LOCAL, VERT = 64, 16, 8
BPT = P // BLOCK
LT = LOCAL // BPT
EPS = 1e-5
SM_SCALE = 1.0 / HD
NEG = -1.0e30
CREDIT = 16


def max_segments(tile):
    end = (tile + 1) * P
    if tile < LT:
        start, pieces = 0, []
        while end - start > 0:
            width = (end - start) % 512 or 512
            pieces.append((start, width))
            start += width
        return pieces
    start = (tile - LT) * P + BLOCK
    return [(start, BLOCK)] + [(start + BLOCK + i * 512, 512) for i in range(2)]


def has_vertical(tile):
    return tile > (VERT - 1) // BPT + LT


def edge_is_vertical(tile):
    return (BPT * (tile - LT) + 2) % VERT == 0


def steps_of(unit):
    first = unit * TPG
    last = first + TPG - 1
    steps = []
    for key in range(0, last + 1):
        lo = max(key, first)
        full = min(key + LT - 1, last)
        start = (lo - first) * P
        mid = max(full - first + 1, 0) * P if full >= lo else start
        end = mid
        if first <= key + LT <= last:
            end = mid + (P if edge_is_vertical(key + LT) else BLOCK)
        if (BPT * key + 2) % VERT == 0 and has_vertical(last) and key + LT < last:
            end = TG
        if end > start:
            steps.append((key, start, mid, end))
    steps.sort(key=lambda s: (s[0] != first, s[0]))
    assert steps[0][1] == 0 and steps[0][2] == TG
    return steps


def project(nc, x, w_qk, b_qk, w_v, b_v, rope, ident, q_hi, q_lo, k_hi, k_lo, v_out):
    with ExitStack() as ctx:
        sb = lambda name, shape, dt=F32: ctx.enter_context(nc.sbuf_tensor(name, shape, dt))
        ps = lambda name: ctx.enter_context(nc.psum_tensor(name, [P, 512], F32))
        sem = lambda name: ctx.enter_context(nc.semaphore(name))

        wqk = sb("wqk", [P, KC, QK_TILES * P])
        wv = sb("wv", [P, KC, GROUPS * HD])
        bqk = sb("bqk", [P, QK_TILES])
        bv = sb("bv", [P, GROUPS * HD])
        idn = sb("idn_p", [P, P])
        xin = sb("xin", [P, TPG, HID])
        stats = sb("stats_p", [P, TPG, 2, 6])
        mean_var = sb("mean_var_p", [P, TPG, 2])
        var_eps = sb("var_eps_p", [P, TPG])
        minus_half = sb("minus_half_p", [P, TPG])
        rstd = sb("rstd_p", [P, TPG])
        xn = [sb(f"xn{i}", [P, HID]) for i in range(2)]
        x_t = [sb(f"x_t{i}", [P, KC, TG]) for i in range(2)]
        cos_sin = [sb(f"cos_sin{i}", [P, 2, TG]) for i in range(2)]
        raw = [sb(f"raw{i}", [P, TG]) for i in range(2)]
        swapped = [sb(f"swapped{i}", [P, TG]) for i in range(2)]
        with_cos = [sb(f"with_cos{i}", [P, TG]) for i in range(2)]
        with_sin = [sb(f"with_sin{i}", [P, TG]) for i in range(2)]
        turned = [sb(f"turned{i}", [P, TG]) for i in range(2)]
        hi = [sb(f"hi{i}", [P, TG], F32R) for i in range(2)]
        lo = [sb(f"lo{i}", [P, TG], F32R) for i in range(2)]
        v_sb = [sb(f"v_sb{i}", [P, GROUPS * HD]) for i in range(2)]
        ps_t = [ps(f"ps_t{i}") for i in range(2)]
        ps_qk = [ps(f"ps_qk{i}") for i in range(4)]
        ps_v = [ps(f"ps_v{i}") for i in range(2)]

        passed = sem("passed_p")
        weights_in = sem("weights_in")
        consts_in = sem("consts_in")
        wv_in = sem("wv_in")
        x_in = [sem(f"x_in{t}") for t in range(TPG)]
        rope_in = [sem(f"rope_in{i}") for i in range(2)]
        stats_done = sem("stats_done")
        aggr_done = sem("aggr_done")
        eps_done = sem("eps_done")
        rstd_done = sem("rstd_done")
        xn_done = sem("xn_done")
        tr_done = sem("tr_done")
        xt_done = sem("xt_done")
        qk_done = sem("qk_done")
        raw_done = sem("raw_done")
        swap_done = sem("swap_done")
        cos_done = sem("cos_done")
        sin_done = sem("sin_done")
        turned_done = sem("turned_done")
        hi_done = sem("hi_done")
        lo_done = sem("lo_done")
        vps_done = sem("vps_done")
        v_done = sem("v_done")
        qk_stored = [sem(f"qk_stored{i}") for i in range(2)]
        v_stored = [sem(f"v_stored{i}") for i in range(2)]

        def x_tile(n, t):
            return x[bass.ds((n * TPG + t) * P, P), :]

        def table_loads(n, j):
            return (n - j) * 8 + 16

        NORM_AT = [1, 3, 5, 7]
        MOVE_AT = [2, 4, 6, 8]
        LAST = NTG - 1

        def loop_groups(eng, body):
            with eng.Fori(0, NTG // 2 - 1) as i:
                for j in range(2):
                    body(i * 2 + j, j, False)
            for j in range(2):
                body(NTG - 2 + j, j, j == 1)

        block = ctx.enter_context(nc.Block())

        @block.sync
        def _(sp):
            for i in range(2):
                sp.sem_inc(qk_stored[i], CREDIT * 4)
                sp.sem_inc(v_stored[i], CREDIT)
            sp.dma_start(idn[:], ident).then_inc(consts_in, 16)
            for t in range(TPG):
                sp.dma_start(xin[:, t, :], x_tile(0, t)).then_inc(x_in[t], 16)
            sp.dma_start(bqk[:], b_qk).then_inc(consts_in, 16)
            sp.dma_start(bv[:], b_v.partition_broadcast(P)).then_inc(consts_in, 16)
            for k in range(KC):
                sp.dma_start(wqk[:, k, :], w_qk[k * P:(k + 1) * P, :]).then_inc(weights_in, 16)
            sp.dma_start(cos_sin[0][:], rope[0]).then_inc(rope_in[0], 16)
            sp.dma_start(wv[:], w_v.rearrange("(k p) n -> p k n", p=P)).then_inc(wv_in, 16)
            for t in range(TPG):
                sp.wait_ge(xn_done, t + 1)
                sp.dma_start(xin[:, t, :], x_tile(1, t)).then_inc(x_in[t], 16)

            def body(n, j, last):
                if not last:
                    sp.dma_start(cos_sin[1 - j][:], rope[bass.ds(n + 1, 1)].rearrange("o p a s -> (o p) a s")
                                 ).then_inc(rope_in[1 - j], 16)
                for r in range(QK_TILES):
                    m = n * QK_TILES + r
                    sp.wait_ge(lo_done, m + 1 + CREDIT)
                    for part, (dq, dk) in ((hi, (q_hi, k_hi)), (lo, (q_lo, k_lo))):
                        if r < GROUPS:
                            dst = dq[bass.ds(n * GROUPS + r, 1)].rearrange("o p s -> (o p) s")
                        else:
                            dst = dk[bass.ds(n * 2 + (r - GROUPS), 1)].rearrange("o p s -> (o p) s")
                        sp.dma_start(dst.bitcast(F32), part[r % 2][:].bitcast(F32)
                                     ).then_inc(qk_stored[r % 2], 16)
                    if r in MOVE_AT and not last and not (isinstance(n, int) and n + 2 > LAST):
                        t = MOVE_AT.index(r)
                        sp.wait_ge(xn_done, (n + 1) * TPG + t + 1)
                        sp.dma_start(xin[:, t, :], x_tile(n + 2, t)).then_inc(x_in[t], 16)
                for t in range(TPG):
                    sp.wait_ge(v_done, n * TPG + t + 1 + CREDIT)
                    sp.dma_start(v_out[bass.ds((n * TPG + t) * P, P), :], v_sb[t % 2][:]
                                 ).then_inc(v_stored[t % 2], 16)

            loop_groups(sp, body)
            for i in range(2):
                sp.wait_ge(qk_stored[i], CREDIT * 4 + NTG * QK_TILES * 16)
                sp.wait_ge(v_stored[i], CREDIT + NTG * TPG // 2 * 16)

        @block.gpsimd
        def _(pool):
            pool.sem_inc(sin_done, CREDIT)
            pool.memset(minus_half[:], -0.5).then_inc(rstd_done, 1)

            def group_rstd(n):
                pool.wait_ge(eps_done, n + 1)
                if isinstance(n, int) and n == 0:
                    pool.wait_ge(rstd_done, 1)
                pool.tensor_tensor(rstd[:], var_eps[:], minus_half[:], ALU.pow).then_inc(rstd_done, 1)

            group_rstd(0)

            def body(n, j, last):
                pool.wait_ge(rope_in[j], table_loads(n, j))
                if not last:
                    group_rstd(n + 1)
                for r in range(QK_TILES):
                    m = n * QK_TILES + r
                    pool.wait_ge(swap_done, m + 1)
                    pool.wait_ge(turned_done, m - 1 + CREDIT)
                    pool.tensor_tensor(with_sin[r % 2][:], swapped[r % 2][:], cos_sin[j][:, 1, :],
                                       ALU.mult).then_inc(sin_done, 1)

            loop_groups(pool, body)

        @block.scalar
        def _(act):
            act.sem_inc(raw_done, CREDIT)
            act.sem_inc(xt_done, CREDIT)

            def move(n, t, buf):
                for half in range(2):
                    act.wait_ge(tr_done, (n * TPG + t) * 2 + half + 1)
                    act.activation(x_t[buf][:, half * 4:half * 4 + 4, t * P:(t + 1) * P],
                                   ps_t[half][:].rearrange("p (k s) -> p k s", k=4),
                                   ACT.Copy).then_inc(xt_done, 1)

            act.wait_ge(consts_in, 48)
            for t in range(TPG):
                move(0, t, 0)

            def body(n, j, last):
                def split_hi(r):
                    m = n * QK_TILES + r
                    act.wait_ge(turned_done, m + 1 + CREDIT)
                    act.wait_ge(qk_stored[r % 2], (n * (QK_TILES // 2) + r // 2) * 32 + CREDIT * 4)
                    act.activation(hi[r % 2][:], turned[r % 2][:], ACT.Copy,
                                   scale=SM_SCALE if r < GROUPS else 1.0).then_inc(hi_done, 1)

                for r in range(QK_TILES + 2):
                    if r < QK_TILES:
                        m = n * QK_TILES + r
                        act.wait_ge(qk_done, m + 1)
                        act.wait_ge(cos_done, m - 1 + CREDIT)
                        act.activation(raw[r % 2][:], ps_qk[(j * QK_TILES + r) % 4][:], ACT.Identity,
                                       bias=bqk[:, r:r + 1]).then_inc(raw_done, 1)
                    if r >= 2:
                        split_hi(r - 2)
                    if r in MOVE_AT and not last:
                        move(n + 1, MOVE_AT.index(r), 1 - j)

            loop_groups(act, body)

        @block.vector
        def _(dve):
            dve.sem_inc(turned_done, CREDIT)
            dve.sem_inc(lo_done, CREDIT)
            dve.sem_inc(cos_done, CREDIT)
            dve.sem_inc(v_done, CREDIT)

            def group_stats(n):
                for t in range(TPG):
                    dve.wait_ge(x_in[t], (n + 1) * 16)
                    for half in range(2):
                        last = dve.bn_stats(stats[:, t, half, :], xin[:, t, half * 512:(half + 1) * 512])
                    last.then_inc(stats_done, 1)
                for t in range(TPG):
                    dve.wait_ge(stats_done, n * TPG + t + 1)
                    dve.sem_inc(passed, 1)
                    last = dve.bn_aggr(mean_var[:, t, :], stats[:, t].rearrange("p a b -> p (a b)"))
                last.then_inc(aggr_done, 1)
                dve.wait_ge(aggr_done, n + 1)
                dve.tensor_scalar(var_eps[:], mean_var[:, :, 1], EPS, None, ALU.add).then_inc(eps_done, 1)

            def normalise(n, t):
                if t == 0:
                    dve.wait_ge(rstd_done, n + 2)
                if not (isinstance(n, int) and n == 0 and t < 2):
                    dve.wait_ge(tr_done, (n * TPG + t - 1) * 2)
                dve.tensor_scalar(xn[t % 2][:], xin[:, t, :], mean_var[:, t, 0:1], rstd[:, t:t + 1],
                                  ALU.subtract, ALU.mult).then_inc(xn_done, 1)

            group_stats(0)
            for t in range(TPG):
                normalise(0, t)
            dve.wait_ge(consts_in, 48)

            def body(n, j, last):
                dve.wait_ge(rope_in[j], table_loads(n, j))
                if not last:
                    group_stats(n + 1)
                for r in range(QK_TILES + 3):
                    if r < QK_TILES:
                        m = n * QK_TILES + r
                        dve.wait_ge(raw_done, m + 1 + CREDIT)
                        dve.wait_ge(sin_done, m - 1 + CREDIT)
                        dve.sem_inc(passed, 1)
                        dve.stream_shuffle(swapped[r % 2][:], raw[r % 2][:],
                                           [(i + HD // 2) % HD for i in range(HD)]).then_inc(swap_done, 1)
                        dve.wait_ge(turned_done, m - 1 + CREDIT)
                        dve.tensor_tensor(with_cos[r % 2][:], raw[r % 2][:], cos_sin[j][:, 0, :],
                                          ALU.mult).then_inc(cos_done, 1)
                    if r >= 3:
                        q = r - 3
                        dve.wait_ge(hi_done, n * QK_TILES + q + 1)
                        dve.scalar_tensor_tensor(lo[q % 2][:], turned[q % 2][:],
                                                 SM_SCALE if q < GROUPS else 1.0,
                                                 hi[q % 2][:].bitcast(F32), op0=ALU.mult,
                                                 op1=ALU.subtract).then_inc(lo_done, 1)
                    if 1 <= r <= QK_TILES:
                        m = n * QK_TILES + r - 1
                        dve.wait_ge(cos_done, m + 1 + CREDIT)
                        dve.wait_ge(sin_done, m + 1 + CREDIT)
                        dve.wait_ge(lo_done, m - 1 + CREDIT)
                        dve.tensor_tensor(turned[(r - 1) % 2][:], with_cos[(r - 1) % 2][:],
                                          with_sin[(r - 1) % 2][:], ALU.add).then_inc(turned_done, 1)
                    if r in NORM_AT and not last:
                        normalise(n + 1, NORM_AT.index(r))
                for t in range(TPG):
                    dve.wait_ge(vps_done, n * TPG + t + 1)
                    dve.wait_ge(v_stored[t % 2], (n * 2 + t // 2) * 16 + CREDIT)
                    dve.tensor_tensor(v_sb[t % 2][:], ps_v[t % 2][:, 0:GROUPS * HD], bv[:],
                                      ALU.add).then_inc(v_done, 1)

            loop_groups(dve, body)

        @block.tensor
        def _(pe):
            def transposes(n, t):
                pe.wait_ge(xn_done, n * TPG + t + 1)
                for half in range(2):
                    pe.wait_ge(xt_done, (n * TPG + t - 1) * 2 + half + 1 + CREDIT)
                    for c in range(4):
                        k = half * 4 + c
                        last = pe.transpose(ps_t[half][:, c * P:(c + 1) * P],
                                            xn[t % 2][:, k * P:(k + 1) * P], idn[:])
                    last.then_inc(tr_done, 1)

            pe.wait_ge(consts_in, 48)
            for t in range(TPG):
                transposes(0, t)
            pe.wait_ge(weights_in, KC * 16)
            pe.wait_ge(wv_in, 16)

            def body(n, j, last):
                pe.wait_ge(xt_done, (n + 1) * TPG * 2 + CREDIT)
                for r in range(QK_TILES):
                    m = n * QK_TILES + r
                    pe.wait_ge(raw_done, m - 3 + CREDIT)
                    for k in range(KC):
                        mm = pe.matmul(ps_qk[(j * QK_TILES + r) % 4][:], wqk[:, k, r * P:(r + 1) * P],
                                       x_t[j][:, k, :], start=(k == 0), stop=(k == KC - 1))
                    mm.then_inc(qk_done, 1)
                    if r in MOVE_AT and not last:
                        transposes(n + 1, MOVE_AT.index(r))
                for t in range(TPG):
                    pe.wait_ge(v_done, n * TPG + t - 1 + CREDIT)
                    for k in range(KC):
                        mm = pe.matmul(ps_v[t % 2][:, 0:GROUPS * HD], x_t[j][:, k, t * P:(t + 1) * P],
                                       wv[:, k, :], start=(k == 0), stop=(k == KC - 1))
                    mm.then_inc(vps_done, 1)

            loop_groups(pe, body)


def attend(nc, masks, ident, q_hi, q_lo, k_hi, k_lo, v_in, o_out, sum_out, finish_weights):
    STEPS = [steps_of(u) for u in range(UPB)]
    NS = [len(s) for s in STEPS]
    CHUNKS = [[(tl, h, c) for h in range(QPG) for tl in range(TPG)
               for c in range(len(max_segments(u * TPG + tl)))] for u in range(UPB)]
    NCH = [len(c) for c in CHUNKS]
    UNITS = 2 * UPB
    step0 = [sum(NS[w % UPB] for w in range(u)) for u in range(UNITS + 1)]
    chunk0 = [sum(NCH[w % UPB] for w in range(u)) for u in range(UNITS + 1)]
    fixes = [[s for s in STEPS[u] if s[0] >= u * TPG or s[3] > s[2]] for u in range(UPB)]
    fix0 = [sum(len(fixes[w % UPB]) * QPG for w in range(u)) for u in range(UNITS + 1)]
    BODY_STEPS, BODY_CHUNKS, BODY_FIXES = step0[-1], chunk0[-1], fix0[-1]
    assert BODY_STEPS % 2 == 0 and all(n % 2 == 0 for n in NCH)
    BODIES = GROUPS // 2

    with ExitStack() as ctx:
        sb = lambda name, shape, dt=F32: ctx.enter_context(nc.sbuf_tensor(name, shape, dt))
        ps = lambda name: ctx.enter_context(nc.psum_tensor(name, [P, 512], F32))
        sem = lambda name: ctx.enter_context(nc.semaphore(name))

        kp = [sb(f"kp{i}", [P, SEQ], F32R) for i in range(2)]
        qp = [sb(f"qp{i}", [P, QPG, TG], F32R) for i in range(4)]
        v1 = [sb(f"v1_{i}", [P, SEQ // P, 2 * HD]) for i in range(2)]
        probs = [[sb(f"probs{i}_{h}", [P, TG]) for h in range(QPG)] for i in range(2)]
        part_max = sb("part_max", [P, QPG * TPG, 3])
        neg_max = [sb(f"neg_max{i}", [P, QPG * TPG]) for i in range(2)]
        max_row = [sb(f"max_row{i}", [QPG * TPG, P], F32R) for i in range(2)]
        o_sb = [sb(f"o_sb{i}", [P, 2, TG]) for i in range(2)]
        idn = sb("idn_a", [P, P])
        idn_bf = sb("idn_bf", [P, P], BF16)
        mask_f = sb("mask_f", [P, P + BLOCK])
        mask_bf = sb("mask_bf", [P, P + BLOCK], BF16)
        ps_max = [ps(f"ps_max{i}") for i in range(2)]
        ps_s = [ps(f"ps_s{h}") for h in range(QPG)]
        ps_o = [ps(f"ps_o{i}") for i in range(2)]

        passed = sem("passed_a")
        consts_in = sem("consts_in_a")
        consts_bf = sem("consts_bf")
        ones_set = sem("ones_set")
        q_in = [sem(f"q_in{i}") for i in range(4)]
        k_in = [sem(f"k_in{i}") for i in range(2)]
        v_in_s = [sem(f"v_in{i}") for i in range(2)]
        row_in = sem("row_in")
        chunk_done = sem("chunk_done")
        reduced = sem("reduced")
        neg_done = sem("neg_done")
        rowt_done = sem("rowt_done")
        row_done = sem("row_done")
        scores_done = sem("scores_done")
        exp_done = sem("exp_done")
        fix_done = sem("fix_done")
        pv_done = sem("pv_done")
        o_done = sem("o_done")
        o_stored = [sem(f"o_stored{i}") for i in range(2)]
        weights3_in = sem("weights3_in")

        block = ctx.enter_context(nc.Block())

        def load_q(sp, b, g, u):
            buf = u % 4
            blk = (b * UPB + u % UPB) * GROUPS + g + u // UPB
            for part, src in ((0, q_hi), (1, q_hi), (2, q_lo)):
                sp.dma_start(qp[buf][part * HD:(part + 1) * HD].bitcast(F32),
                             src[bass.ds(blk, 1)].rearrange("o (h d) s -> (o d) h s", h=QPG).bitcast(F32)
                             ).then_inc(q_in[buf], 16)

        def load_kv(sp, b, g, j):
            for part, src in ((0, k_hi), (1, k_lo), (2, k_hi)):
                sp.dma_start(kp[j][part * HD:(part + 1) * HD].rearrange("d (n s) -> d n s", n=UPB).bitcast(F32),
                             src.rearrange("(n g) d s -> n g d s", g=GROUPS)[bass.ds(b * UPB, UPB), bass.ds(g + j, 1)]
                             .rearrange("n o d s -> (o d) n s").bitcast(F32)
                             ).then_inc(k_in[j], 16)
            sp.dma_start(v1[j][:, :, 0:HD],
                         v_in[bass.ds(b * SEQ, SEQ), bass.ds((g + j) * HD, HD)].rearrange("(t p) d -> p t d", p=P)
                         ).then_inc(v_in_s[j], 16)

        def row_step(u):
            return NS[u % UPB] - 2

        def chunks_by(u):
            total, steps = NCH[(u + 1) % UPB], max(row_step(u) - 1, 1)
            return [total * (s + 1) // steps - total * s // steps if s < steps else 0
                    for s in range(NS[u % UPB])]

        def bank_width(tile, seg):
            width = max_segments(tile)[seg][1]
            return width + BLOCK if seg == 0 and has_vertical(tile) else width

        def loop_bodies(eng, before, body):
            with eng.Fori(0, BATCH) as b:
                before(b)
                with eng.Fori(0, BODIES - 1) as i:
                    body(b, i, b * BODIES + i, False)
                body(b, BODIES - 1, b * BODIES + (BODIES - 1), True)

        @block.sync
        def _(sp):
            sp.sem_inc(row_in, CREDIT * 2)
            for i in range(2):
                sp.sem_inc(o_stored[i], CREDIT)
            sp.dma_start(idn[:], ident).then_inc(consts_in, 16)
            sp.dma_start(mask_f[:], masks).then_inc(consts_in, 16)
            def put_row(u, n):
                sp.wait_ge(row_done, n + 1 + CREDIT)
                sp.dma_start(qp[u % 4][3 * HD:3 * HD + 1].bitcast(F32), max_row[u % 2][:].bitcast(F32)
                             ).then_inc(row_in, 16)

            def before(b):
                sp.wait_ge(pv_done, b * (BODIES * BODY_STEPS) + CREDIT)
                load_kv(sp, b, 0, 0)
                for u in range(3):
                    load_q(sp, b, 0, u)
                load_kv(sp, b, 0, 1)
                put_row(0, b * (BODIES * UNITS))

            def body(b, i, n, last):
                g = i * 2
                for u in range(UNITS):
                    if not (last and u + 3 >= UNITS):
                        sp.wait_ge(scores_done, (n * BODY_STEPS + step0[u]) * QPG + CREDIT)
                        if u + 3 < UNITS:
                            load_q(sp, b, g, u + 3)
                        else:
                            load_q(sp, b, g + 2, u + 3 - UNITS)
                    if u == UPB and not last:
                        sp.wait_ge(pv_done, n * BODY_STEPS + step0[UPB] + CREDIT)
                        load_kv(sp, b, g + 2, 0)
                    if u > 0:
                        store_o(b, g, n, u - 1)
                    if not (last and u + 1 == UNITS):
                        put_row((u + 1) % UNITS, n * UNITS + u + 1)
                store_o(b, g, n, UNITS - 1)
                if not last:
                    load_kv(sp, b, g + 2, 1)

            def store_o(b, g, n, u):
                sp.wait_ge(o_done, n * UNITS + u + 1 + CREDIT)
                blk = (b * UPB + u % UPB) * GROUPS + g + u // UPB
                for hh in range(2):
                    for dst, first, size in ((o_out, 0, HD), (sum_out, HD, 1)):
                        sp.dma_start(dst[bass.ds(blk, 1)].rearrange("o (i h d) s -> h (o d) i s", i=2, h=2)[hh],
                                     o_sb[u % 2][hh * 2 * HD + first:hh * 2 * HD + first + size]
                                     ).then_inc(o_stored[u % 2], 16)

            loop_bodies(sp, before, body)
            for i in range(2):
                sp.wait_ge(o_stored[i], CREDIT + BATCH * BODIES * UNITS // 2 * 64)

        @block.gpsimd
        def _(pool):
            for j in range(2):
                pool.memset(v1[j][:, :, HD:2 * HD], 1.0).then_inc(ones_set, 1)

            def body(b, i, n, last):
                for u in range(UNITS):
                    f = 0
                    for s, (key, start, mid, end) in enumerate(STEPS[u % UPB]):
                        step = step0[u] + s
                        if (key, start, mid, end) not in fixes[u % UPB]:
                            continue
                        for h in range(QPG):
                            pool.wait_ge(exp_done, (n * BODY_STEPS + step) * QPG + h + 1)
                            pool.sem_inc(passed, 1)
                            p = probs[step % 2][h]
                            if key >= (u % UPB) * TPG:
                                pool.affine_select(out=p[:, start:start + P], in_=p[:, start:start + P],
                                                   compare_op=ALU.is_ge, fill=0.0, base=0,
                                                   pattern=[[1, P]], channel_multiplier=-1
                                                   ).then_inc(fix_done, 1)
                            else:
                                pool.affine_select(out=p[:, mid:end], in_=p[:, mid:end],
                                                   compare_op=ALU.is_ge, fill=0.0, base=-BLOCK,
                                                   pattern=[[0, end - mid]], channel_multiplier=1
                                                   ).then_inc(fix_done, 1)

            loop_bodies(pool, lambda b: None, body)

        @block.scalar
        def _(act):
            act.sem_inc(row_done, CREDIT)
            act.sem_inc(o_done, CREDIT)
            for dst, src in finish_weights:
                act.dma_start(dst, src).then_inc(weights3_in, 16)

            def row(u, n):
                act.wait_ge(rowt_done, n + 1)
                act.wait_ge(row_in, (n - 1) * 16 + CREDIT * 2)
                act.activation(max_row[u % 2][:], ps_max[0][0:QPG * TPG, 0:P], ACT.Copy
                               ).then_inc(row_done, 1)

            def out(u, n):
                act.wait_ge(pv_done, step_end(u, n) + CREDIT)
                act.wait_ge(o_stored[u % 2], out_loads(u, n) + CREDIT)
                for i in range(2):
                    last = act.activation(o_sb[u % 2][:, i, :], ps_o[i][:], ACT.Copy)
                last.then_inc(o_done, 1)

            def step_end(u, n):
                return n * BODY_STEPS + step0[u + 1]

            def out_loads(u, n):
                return (n * (UNITS // 2) + u // 2) * 64

            def before(b):
                row(0, b * (BODIES * UNITS))

            def body(b, i, n, last):
                for u in range(UNITS):
                    steps = STEPS[u % UPB]
                    row_at = row_step(u)
                    for s, (key, start, mid, end) in enumerate(steps):
                        step = step0[u] + s
                        act.wait_ge(pv_done, n * BODY_STEPS + step - 1 + CREDIT)
                        for h in range(QPG):
                            act.wait_ge(scores_done, (n * BODY_STEPS + step) * QPG + h + 1 + CREDIT)
                            act.activation(probs[step % 2][h][:, start:end], ps_s[h][:, start:end],
                                           ACT.Exp).then_inc(exp_done, 1)
                        if s == 0 and u > 0:
                            out(u - 1, n)
                        if s == row_at and not (last and u + 1 == UNITS):
                            row((u + 1) % UNITS, n * UNITS + u + 1)
                out(UNITS - 1, n)

            loop_bodies(act, before, body)
            act.wait_ge(weights3_in, 16 * len(finish_weights))

        @block.vector
        def _(dve):
            dve.sem_inc(reduced, CREDIT)
            dve.sem_inc(neg_done, CREDIT)
            dve.wait_ge(consts_in, 32)
            dve.tensor_copy(idn_bf[:], idn[:]).then_inc(consts_bf, 1)
            dve.tensor_copy(mask_bf[:], mask_f[:]).then_inc(consts_bf, 1)
            for j in range(2):
                dve.memset(kp[j][3 * HD:3 * HD + 1, :].bitcast(F32), 1.0).then_inc(ones_set, 1)

            def maxima(u, unit_n, chunk_n):
                dve.wait_ge(neg_done, unit_n + CREDIT)
                for c, (tl, h, seg) in enumerate(CHUNKS[u % UPB]):
                    width = bank_width((u % UPB) * TPG + tl, seg)
                    dve.wait_ge(chunk_done, chunk_n + c + 1)
                    last = dve.reduce_max(part_max[:, h * TPG + tl, seg:seg + 1],
                                          ps_max[c % 2][:, 0:width], AX.X)
                    last.then_inc(reduced, 1)
                n_seg = len(max_segments((u % UPB) * TPG))
                dve.wait_ge(reduced, chunk_n + NCH[u % UPB] + CREDIT)
                dve.wait_ge(row_done, unit_n - 1 + CREDIT)
                dve.tensor_reduce(neg_max[u % 2][:], part_max[:, :, 0:n_seg], AX.X, ALU.max,
                                  negate=True).then_inc(neg_done, 1)

            def before(b):
                maxima(0, b * (BODIES * UNITS), b * (BODIES * BODY_CHUNKS))

            def body(b, i, n, last):
                for u in range(UNITS):
                    if not (last and u + 1 == UNITS):
                        maxima((u + 1) % UNITS, n * UNITS + u + 1, n * BODY_CHUNKS + chunk0[u + 1])

            loop_bodies(dve, before, body)

        @block.tensor
        def _(pe):
            pe.sem_inc(scores_done, CREDIT)
            pe.sem_inc(pv_done, CREDIT)

            def chunk(u, c, unit_n, chunk_n):
                tl, h, seg = CHUNKS[u % UPB][c]
                tile = (u % UPB) * TPG + tl
                segs = max_segments(tile)
                start, width = segs[seg]
                k = kp[(u // UPB) % 2]
                bank = ps_max[c % 2]
                if c == 0:
                    pe.wait_ge(row_done, unit_n + CREDIT)
                pe.wait_ge(reduced, chunk_n + c - 1 + CREDIT)
                diag = seg == len(segs) - 1
                edge = tile >= LT and seg == 0 and not edge_is_vertical(tile)
                lhs = qp[u % 4][0:3 * HD, h, tl * P:(tl + 1) * P]
                if seg == 0 and has_vertical(tile):
                    vert = (VERT - 1) * BLOCK
                    step = start - vert
                    rhs = k[0:3 * HD, vert:vert + 2 * step].rearrange("p (a b) -> p a b", a=2)[:, :, 0:BLOCK]
                    mm = pe.matmul(bank[:, 0:2 * BLOCK], lhs, rhs, start=True, stop=not edge)
                    at = BLOCK
                else:
                    mm = pe.matmul(bank[:, 0:width], lhs, k[0:3 * HD, start:start + width],
                                   start=True, stop=not (edge or diag))
                    at = 0
                if edge:
                    mm = pe.matmul(bank[:, at:at + BLOCK], idn_bf[:], mask_bf[:, P:P + BLOCK],
                                   start=False, stop=True)
                if diag:
                    mm = pe.matmul(bank[:, width - P:width], idn_bf[:], mask_bf[:, 0:P],
                                   start=False, stop=True)
                mm.then_inc(chunk_done, 1)

            def turn_row(u, unit_n):
                pe.wait_ge(neg_done, unit_n + 1 + CREDIT)
                pe.transpose(ps_max[0][0:QPG * TPG, 0:P], neg_max[u % 2][:], idn[:]
                             ).then_inc(rowt_done, 1)

            def scores(u, s, n):
                key, start, mid, end = STEPS[u % UPB][s]
                k = kp[(u // UPB) % 2]
                for h in range(QPG):
                    pe.wait_ge(exp_done, exp_count(u, s, n) + h)
                    pe.matmul(ps_s[h][:, start:end], k[0:3 * HD + 1, key * P:(key + 1) * P],
                              qp[u % 4][0:3 * HD + 1, h, start:end], start=True, stop=True
                              ).then_inc(scores_done, 1)

            def exp_count(u, s, n):
                return (n * BODY_STEPS + step0[u] + s - 1) * QPG + 1

            def context(u, s, n):
                key, start, mid, end = STEPS[u % UPB][s]
                if (key, start, mid, end) in fixes[u % UPB]:
                    order = [x for x in STEPS[u % UPB][:s] if x in fixes[u % UPB]]
                    pe.wait_ge(fix_done, n * BODY_FIXES + fix0[u] + (len(order) + 1) * QPG)
                pe.wait_ge(exp_done, (n * BODY_STEPS + step0[u] + s + 1) * QPG)
                for h in range(QPG):
                    rows = slice((h % 2) * 2 * HD, (h % 2 + 1) * 2 * HD)
                    mm = pe.matmul(ps_o[h // 2][rows, start:end], v1[(u // UPB) % 2][:, key, :],
                                   probs[(step0[u] + s) % 2][h][:, start:end],
                                   start=(s == 0), stop=(s == NS[u % UPB] - 1), skip_group_check=True,
                                   tile_position=(0, (h % 2) * 2 * HD))
                mm.then_inc(pv_done, 1)

            pe.wait_ge(consts_bf, 2)
            pe.wait_ge(ones_set, 4)

            def before(b):
                pe.wait_ge(k_in[0], b * (BODIES * 48) + 48)
                pe.wait_ge(q_in[0], b * (BODIES * 96) + 48)
                for c in range(NCH[0]):
                    chunk(0, c, b * (BODIES * UNITS), b * (BODIES * BODY_CHUNKS))
                turn_row(0, b * (BODIES * UNITS))
                pe.wait_ge(row_in, b * (BODIES * UNITS * 16) + 16 + CREDIT * 2)
                pe.wait_ge(v_in_s[0], b * (BODIES * 16) + 16)
                scores_first(b)

            def scores_first(b):
                key, start, mid, end = STEPS[0][0]
                for h in range(QPG):
                    pe.wait_ge(pv_done, b * (BODIES * BODY_STEPS) + CREDIT)
                    pe.matmul(ps_s[h][:, start:end], kp[0][0:3 * HD + 1, key * P:(key + 1) * P],
                              qp[0][0:3 * HD + 1, h, start:end], start=True, stop=True
                              ).then_inc(scores_done, 1)

            def body(b, i, n, last):
                for u in range(UNITS):
                    final = last and u + 1 == UNITS
                    plan = chunks_by(u)
                    c = 0
                    if not final:
                        w = (u + 1) % UNITS
                        body_of = n + (u + 1) // UNITS
                        pe.wait_ge(q_in[w % 4], body_of * 96 + (w // 4 + 1) * 48)
                        if w == UPB or w == 0:
                            pe.wait_ge(k_in[w // UPB], body_of * 48 + 48)
                            pe.wait_ge(v_in_s[w // UPB], body_of * 16 + 16)
                    for s in range(NS[u % UPB]):
                        if s + 1 < NS[u % UPB]:
                            scores(u, s + 1, n)
                        elif not final:
                            pe.wait_ge(row_in, (n * UNITS + u + 2) * 16 + CREDIT * 2)
                            scores((u + 1) % UNITS, 0, n) if u + 1 < UNITS else scores_next(n)
                        if not final:
                            for _ in range(plan[s]):
                                chunk(w, c, n * UNITS + u + 1, n * BODY_CHUNKS + chunk0[u + 1])
                                c += 1
                            if s == row_step(u):
                                turn_row(w, n * UNITS + u + 1)
                        if s == 0:
                            pe.wait_ge(o_done, n * UNITS + u + CREDIT)
                        context(u, s, n)

            def scores_next(n):
                key, start, mid, end = STEPS[0][0]
                for h in range(QPG):
                    pe.wait_ge(exp_done, ((n + 1) * BODY_STEPS - 1) * QPG + 1 + h)
                    pe.matmul(ps_s[h][:, start:end], kp[0][0:3 * HD + 1, key * P:(key + 1) * P],
                              qp[0][0:3 * HD + 1, h, start:end], start=True, stop=True
                              ).then_inc(scores_done, 1)

            loop_bodies(pe, before, body)


def finish(nc, weights, x, b_dense, b_base, rev_index, ident, o_in, sum_in, inv_dram, out):
    w_dense, w_base, w_ra, b_lora = weights
    with ExitStack() as ctx:
        sb = lambda name, shape, dt=F32: ctx.enter_context(nc.sbuf_tensor(name, shape, dt))
        ps = lambda name, width=512: ctx.enter_context(nc.psum_tensor(name, [P, width], F32))
        sem = lambda name: ctx.enter_context(nc.semaphore(name))
        two = lambda name, shape: [sb(f"{name}{i}", shape) for i in range(2)]

        idn = sb("idn_f", [P, P])
        bd, bb = sb("bd", [P, HID]), sb("bb", [P, HID])
        rev = sb("rev", [P, EXPERTS])
        minus_half = sb("minus_half_f", [P, 1])
        ctx_t, inv, xt = two("ctx_t", [P, KC, P]), two("inv", [P, KC, P]), two("x_res", [P, HID])
        a_sb, y_sb, x1 = two("a_sb", [P, HID]), two("y_sb", [P, HID]), two("x1_", [P, HID])
        xn2, x2_t = two("xn2_", [P, HID]), two("x2_t", [P, KC, P])
        f_sb, z_sb, out_sb = two("f_sb", [P, HID]), two("z_sb", [P, HID]), two("out_sb", [P, HID])
        stats = [two(f"stats{k}_", [P, 2, 6]) for k in range(3)]
        mean_var = [two(f"mean_var{k}_", [P, 2]) for k in range(3)]
        var_eps = [two(f"var_eps{k}_", [P, 1]) for k in range(3)]
        rstd = [two(f"rstd{k}_", [P, 1]) for k in range(3)]
        shift = [two(f"shift{k}_", [P, 1]) for k in range(3)]
        logits, top, first, second = (two(f"{k}_", [P, EXPERTS]) for k in ("logits", "top", "first", "second"))
        score, best = two("score", [P, EXPERTS]), two("best", [P, 1])
        gap, expo, half, w1, w2 = (two(f"{k}_", [P, 1]) for k in ("gap", "expo", "half", "w1", "w2"))
        comb, hw, hw_t = two("comb", [P, EXPERTS]), two("hw", [P, ER]), two("hw_t", [P, P])
        ps_d, ps_f = ps("ps_d", HID), ps("ps_f", HID)
        ps_x = [ps(f"ps_x{i}") for i in range(2)]
        ps_ra, ps_h = ps("ps_ra"), ps("ps_h")

        passed = sem("passed_f")
        consts_in = sem("consts_in_f")
        sums_in = sem("sums_in")
        sums_inv = sem("sums_inv")
        inv_kept = sem("inv_kept")
        half_set = sem("half_set")
        o_loaded = [sem(f"o_loaded{i}") for i in range(2)]
        inv_loaded = [sem(f"inv_loaded{i}") for i in range(2)]
        x_loaded = [sem(f"x_loaded{i}") for i in range(2)]
        out_stored = [sem(f"out_stored{i}") for i in range(2)]
        ctx_done = sem("ctx_done")
        dense_done = sem("dense_done")
        a_done = sem("a_done")
        eps_done = [sem(f"eps_done{k}") for k in range(3)]
        rstd_done = [sem(f"rstd_done{k}") for k in range(3)]
        shift_done = [sem(f"shift_done{k}") for k in range(3)]
        y_done = sem("y_done")
        x1_done = sem("x1_done")
        xn2_done = sem("xn2_done")
        x2_turned = sem("x2_turned")
        x2_moved = sem("x2_moved")
        ra_done = sem("ra_done")
        gap_done = sem("gap_done")
        expo_done = sem("expo_done")
        hw_done = sem("hw_done")
        hwt_turned = sem("hwt_turned")
        hwt_done = sem("hwt_done")
        ffn_done = sem("ffn_done")
        f_done = sem("f_done")
        z_done = sem("z_done")
        out_done = sem("out_done")
        chain = sem("chain")
        chain_first = sem("chain_first")

        NT = NTG * TPG

        def loop_tiles(eng, body):
            with eng.Fori(0, NTG - 1) as n:
                for t in range(TPG):
                    body(n, t, NT)
            for t in range(TPG):
                body(NTG - 1, t, TPG - 1 - t)

        block = ctx.enter_context(nc.Block())

        @block.sync
        def _(sp):
            sp.dma_start(inv[0][:].rearrange("p k s -> p (k s)"),
                         sum_in.rearrange("b h s -> (b h s)").rearrange("(p n) -> p n", p=P)
                         ).then_inc(sums_in, 16)
            sp.dma_start(idn[:], ident).then_inc(consts_in, 16)
            sp.dma_start(bd[:], b_dense.partition_broadcast(P)).then_inc(consts_in, 16)
            sp.dma_start(bb[:], b_base.partition_broadcast(P)).then_inc(consts_in, 16)
            sp.dma_start(rev[:], rev_index.partition_broadcast(P)).then_inc(consts_in, 16)
            sp.wait_ge(sums_inv, 1)
            sp.dma_start(inv_dram.rearrange("b h s -> (b h s)").rearrange("(p n) -> p n", p=P),
                         inv[1][:].rearrange("p k s -> p (k s)")).then_inc(inv_kept, 16)
            sp.wait_ge(inv_kept, 16)

            def load(n, t):
                n, t = n + t // TPG, t % TPG
                i = t % 2
                cols = slice(t * P, (t + 1) * P)
                sp.dma_start(ctx_t[i][:], o_in[bass.ds(n * GROUPS, GROUPS), :, cols].rearrange("g p s -> p g s")
                             ).then_inc(o_loaded[i], 16)
                for h in range(QPG):
                    sp.dma_start(inv[i][h * HD:(h + 1) * HD],
                                 inv_dram[bass.ds(n * GROUPS, GROUPS), h, cols].partition_broadcast(HD)
                                 ).then_inc(inv_loaded[i], 16)
                sp.dma_start(xt[i][:], x[bass.ds((n * TPG + t) * P, P), :]).then_inc(x_loaded[i], 16)

            load(0, 0)
            load(0, 1)

            def body(n, t, rest):
                if rest >= 2:
                    sp.wait_ge(dense_done, n * TPG + t + 1)
                    sp.wait_ge(x1_done, n * TPG + t + 1)
                    load(n, t + 2)
                sp.wait_ge(out_done, n * TPG + t + 1 + CREDIT)
                sp.dma_start(out[bass.ds((n * TPG + t) * P, P), :], out_sb[t % 2][:]
                             ).then_inc(out_stored[t % 2], 16)

            loop_tiles(sp, body)
            for i in range(2):
                sp.wait_ge(out_stored[i], CREDIT * 2 + NT // 2 * 16)

        @block.gpsimd
        def _(pool):
            for i in range(2):
                pool.sem_inc(out_stored[i], CREDIT * 2)
            pool.memset(minus_half[:], -0.5).then_inc(half_set, 1)
            pool.wait_ge(half_set, 1)

            def root(k, n, t):
                n, i = n + t // TPG, t % 2
                pool.wait_ge(eps_done[k], n * TPG + t % TPG + 1)
                pool.tensor_tensor(rstd[k][i][:], var_eps[k][i][:], minus_half[:], ALU.pow
                                   ).then_inc(rstd_done[k], 1)

            root(0, 0, 0)
            root(1, 0, 0)

            def body(n, t, rest):
                if rest >= 1:
                    root(0, n, t + 1)
                    root(1, n, t + 1)
                root(2, n, t)
                pool.wait_ge(z_done, n * TPG + t + 1 + CREDIT)
                pool.wait_ge(out_stored[t % 2], (n * 2 + t // 2) * 16 + CREDIT * 2)
                pool.tensor_tensor(out_sb[t % 2][:], z_sb[t % 2][:], x1[t % 2][:], ALU.add
                                   ).then_inc(out_done, 1)

            loop_tiles(pool, body)

        @block.scalar
        def _(act):
            act.sem_inc(x2_moved, CREDIT)
            act.sem_inc(hwt_done, CREDIT)

            def affine(k, src, dst, n, t, done):
                n, i = n + t // TPG, t % 2
                act.wait_ge(shift_done[k], n * TPG + t % TPG + 1)
                act.activation(dst[i][:], src[i][:], ACT.Identity, bias=shift[k][i][:],
                               scale=rstd[k][i][:]).then_inc(done, 1)

            affine(0, a_sb, y_sb, 0, 0, y_done)

            def body(n, t, rest):
                i = t % 2
                for half_ in range(2):
                    act.wait_ge(x2_turned, (n * TPG + t) * 2 + half_ + 1)
                    act.activation(x2_t[i][:, half_ * 4:half_ * 4 + 4, :],
                                   ps_x[half_][:].rearrange("p (k s) -> p k s", k=4), ACT.Copy
                                   ).then_inc(x2_moved, 1)
                act.wait_ge(gap_done, n * TPG + t + 1)
                act.activation(expo[i][:], gap[i][:], ACT.Exp).then_inc(expo_done, 1)
                act.wait_ge(hwt_turned, n * TPG + t + 1)
                act.activation(hw_t[i][:], ps_h[:, 0:P], ACT.Copy).then_inc(hwt_done, 1)
                if rest >= 1:
                    affine(0, a_sb, y_sb, n, t + 1, y_done)
                act.wait_ge(out_done, n * TPG + t - 1 + CREDIT)
                affine(2, f_sb, z_sb, n, t, z_done)

            loop_tiles(act, body)

        @block.vector
        def _(dve):
            dve.sem_inc(a_done, CREDIT)
            dve.sem_inc(f_done, CREDIT)
            dve.sem_inc(out_done, CREDIT)
            count = [0]

            def link(ins, n):
                ins.then_inc(chain if n is not None else chain_first, 1)
                count[0] += 1
                if n is None:
                    dve.wait_ge(chain_first, count[0])
                else:
                    dve.wait_ge(chain, n * LINKS_PER_BODY + count[0])

            def norm_stats(k, src, i, n):
                dve.bn_stats(stats[k][i][:, 0, :], src[:, 0:512])
                link(dve.bn_stats(stats[k][i][:, 1, :], src[:, 512:1024]), n)
                dve.sem_inc(passed, 1)
                link(dve.bn_aggr(mean_var[k][i][:], stats[k][i][:].rearrange("p a b -> p (a b)")), n)
                dve.tensor_scalar(var_eps[k][i][:], mean_var[k][i][:, 1:2], EPS, None, ALU.add
                                  ).then_inc(eps_done[k], 1)

            def norm_shift(k, i, tile):
                dve.wait_ge(rstd_done[k], tile + 1)
                dve.scalar_tensor_tensor(shift[k][i][:], mean_var[k][i][:, 0:1], -1.0, rstd[k][i][:],
                                         op0=ALU.mult, op1=ALU.mult).then_inc(shift_done[k], 1)

            def divide(n, t):
                n, t = n + t // TPG, t % TPG
                i = t % 2
                dve.wait_ge(o_loaded[i], (n * 2 + t // 2 + 1) * 16)
                dve.wait_ge(inv_loaded[i], (n * 2 + t // 2 + 1) * 64)
                dve.tensor_tensor(ctx_t[i][:], ctx_t[i][:], inv[i][:], ALU.mult).then_inc(ctx_done, 1)

            def evacuate_dense(n, t):
                n, t = n + t // TPG, t % TPG
                dve.wait_ge(dense_done, n * TPG + t + 1)
                dve.tensor_tensor(a_sb[t % 2][:], ps_d[:], bd[:], ALU.add).then_inc(a_done, 1)

            def attention_norms(n, t, links):
                n, t = n + t // TPG, t % TPG
                i, tile = t % 2, n * TPG + t
                dve.wait_ge(a_done, tile + 1 + CREDIT)
                norm_stats(0, a_sb[i], i, links)
                norm_shift(0, i, tile)
                dve.wait_ge(y_done, tile + 1)
                dve.wait_ge(x_loaded[i], (n * 2 + t // 2 + 1) * 16)
                dve.wait_ge(out_done, tile - 1 + CREDIT)
                dve.tensor_tensor(x1[i][:], y_sb[i][:], xt[i][:], ALU.add).then_inc(x1_done, 1)
                dve.wait_ge(x1_done, tile + 1)
                norm_stats(1, x1[i], i, links)
                dve.wait_ge(rstd_done[1], tile + 1)
                dve.tensor_scalar(xn2[i][:], x1[i][:], mean_var[1][i][:, 0:1], rstd[1][i][:],
                                  ALU.subtract, ALU.mult).then_inc(xn2_done, 1)

            def router(n, t):
                i = t % 2
                dve.wait_ge(ra_done, n * TPG + t + 1)
                link(dve.tensor_copy(logits[i][:], ps_ra[:, 0:EXPERTS]), n)
                dve.sem_inc(passed, 1)
                link(dve.max(top[i][:], logits[i][:]), n)

                def one_hot(dst, values, value):
                    link(dve.scalar_tensor_tensor(score[i][:], values, value, rev[:],
                                                  op0=ALU.is_equal, op1=ALU.mult), n)
                    link(dve.reduce_max(best[i][:], score[i][:], AX.X), n)
                    link(dve.tensor_scalar(dst[i][:], score[i][:], best[i][:], None, ALU.is_equal), n)

                one_hot(first, logits[i][:], top[i][:, 0:1])
                link(dve.scalar_tensor_tensor(logits[i][:], first[i][:], -3.0e38, logits[i][:],
                                              op0=ALU.mult, op1=ALU.add), n)
                one_hot(second, logits[i][:], top[i][:, 1:2])
                dve.tensor_tensor(gap[i][:], top[i][:, 1:2], top[i][:, 0:1], ALU.subtract
                                  ).then_inc(gap_done, 1)
                dve.wait_ge(expo_done, n * TPG + t + 1)
                link(dve.tensor_scalar(half[i][:], expo[i][:], 1.0, 0.5, ALU.add, ALU.mult), n)
                link(dve.reciprocal(w1[i][:], half[i][:]), n)
                link(dve.tensor_tensor(w2[i][:], w1[i][:], expo[i][:], ALU.mult), n)
                link(dve.tensor_scalar(comb[i][:], first[i][:], w1[i][:], None, ALU.mult), n)
                link(dve.scalar_tensor_tensor(comb[i][:], second[i][:], w2[i][:], comb[i][:],
                                              op0=ALU.mult, op1=ALU.add), n)
                dve.tensor_tensor(hw[i][:].rearrange("p (e r) -> p e r", r=RANK),
                                  ps_ra[:, EXPERTS:EXPERTS + ER].rearrange("p (e r) -> p e r", r=RANK),
                                  comb[i][:].unsqueeze(2).to_broadcast([P, EXPERTS, RANK]),
                                  ALU.mult).then_inc(hw_done, 1)

            def ffn_norm(n, t):
                i, tile = t % 2, n * TPG + t
                dve.wait_ge(ffn_done, tile + 1)
                dve.wait_ge(z_done, tile - 1 + CREDIT)
                dve.tensor_tensor(f_sb[i][:], ps_f[:], bb[:], ALU.add).then_inc(f_done, 1)
                dve.wait_ge(f_done, tile + 1 + CREDIT)
                norm_stats(2, f_sb[i], i, n)
                norm_shift(2, i, tile)

            LINKS_PER_BODY = TPG * (3 * 2 + 14)
            dve.sem_inc(z_done, CREDIT)
            dve.wait_ge(sums_in, 16)
            dve.reciprocal(inv[1][:], inv[0][:]).then_inc(sums_inv, 1)
            dve.wait_ge(consts_in, 64)
            divide(0, 0)
            divide(0, 1)
            evacuate_dense(0, 0)
            attention_norms(0, 0, None)

            def body(n, t, rest):
                if t == 0:
                    count[0] = 0
                router(n, t)
                if rest >= 1:
                    evacuate_dense(n, t + 1)
                if rest >= 2:
                    divide(n, t + 2)
                if rest >= 1:
                    attention_norms(n, t + 1, n)
                ffn_norm(n, t)
                assert t < TPG - 1 or rest == 0 or count[0] == LINKS_PER_BODY, count

            loop_tiles(dve, body)

        @block.tensor
        def _(pe):
            def dense(n, t):
                n, t = n + t // TPG, t % TPG
                i, tile = t % 2, n * TPG + t
                pe.wait_ge(ctx_done, tile + 1)
                pe.wait_ge(a_done, tile + CREDIT)
                for half_ in range(2):
                    for k in range(KC):
                        mm = pe.matmul(ps_d[:, half_ * 512:(half_ + 1) * 512], ctx_t[i][:, k, :],
                                       w_dense[:, k, half_ * 512:(half_ + 1) * 512],
                                       start=(k == 0), stop=(k == KC - 1))
                mm.then_inc(dense_done, 1)

            pe.wait_ge(consts_in, 64)
            dense(0, 0)

            def body(n, t, rest):
                i, tile = t % 2, n * TPG + t
                if rest >= 1:
                    dense(n, t + 1)
                pe.wait_ge(xn2_done, tile + 1)
                for half_ in range(2):
                    pe.wait_ge(x2_moved, (tile - 1) * 2 + half_ + 1 + CREDIT)
                    for c in range(4):
                        k = half_ * 4 + c
                        mm = pe.transpose(ps_x[half_][:, c * P:(c + 1) * P],
                                          xn2[i][:, k * P:(k + 1) * P], idn[:])
                    mm.then_inc(x2_turned, 1)
                pe.wait_ge(x2_moved, tile * 2 + 2 + CREDIT)
                for k in range(KC):
                    mm = pe.matmul(ps_ra[:, 0:EXPERTS + ER], x2_t[i][:, k, :], w_ra[:, k, :],
                                   start=(k == 0), stop=(k == KC - 1))
                mm.then_inc(ra_done, 1)
                pe.wait_ge(f_done, tile + CREDIT)
                for half_ in range(2):
                    for k in range(KC):
                        pe.matmul(ps_f[:, half_ * 512:(half_ + 1) * 512], x2_t[i][:, k, :],
                                  w_base[:, k, half_ * 512:(half_ + 1) * 512],
                                  start=(k == 0), stop=False)
                pe.wait_ge(hw_done, tile + 1)
                pe.transpose(ps_h[:, 0:P], hw[i][:], idn[:]).then_inc(hwt_turned, 1)
                pe.wait_ge(hwt_done, tile + 1 + CREDIT)
                for half_ in range(2):
                    mm = pe.matmul(ps_f[:, half_ * 512:(half_ + 1) * 512], hw_t[i][:],
                                   b_lora[:, half_ * 512:(half_ + 1) * 512], start=False, stop=True)
                mm.then_inc(ffn_done, 1)

            loop_tiles(pe, body)


def build(nc, x, w_qk, b_qk, w_v, b_v, w_dense, b_dense, w_base, b_base, w_ra, b_lora, rope, ident,
          masks, rev_index, out):
    kept = lambda name, shape, dt: nc.dram_tensor(name, shape, dt, kind="Internal").ap()
    q_hi, q_lo = (kept(f"q_{k}", [NTG * GROUPS, QPG * HD, TG], F32R) for k in ("hi", "lo"))
    k_hi, k_lo = (kept(f"k_{k}", [NTG * GROUPS, HD, TG], F32R) for k in ("hi", "lo"))
    v_all = kept("v_all", [BATCH * SEQ, GROUPS * HD], F32)
    o_all = kept("o_all", [NTG * GROUPS, QPG * HD, TG], F32)
    sums = kept("sums", [NTG * GROUPS, QPG, TG], F32)
    inv_sums = kept("inv_sums", [NTG * GROUPS, QPG, TG], F32)
    k_tiles = [k.rearrange("(a g) d s -> a (g d) s", g=P // HD) for k in (k_hi, k_lo)]

    project(nc, x, w_qk, b_qk, w_v, b_v, rope, ident, q_hi, q_lo, k_tiles[0], k_tiles[1], v_all)
    with ExitStack() as ctx:
        sb = lambda name, shape: ctx.enter_context(nc.sbuf_tensor(name, shape, F32))
        wd, wb = sb("wd", [P, KC, HID]), sb("wb", [P, KC, HID])
        wra, bl = sb("wra", [P, KC, EXPERTS + ER]), sb("bl", [P, HID])
        loads = []
        for dst, src in ((wd, w_dense), (wb, w_base), (wra, w_ra)):
            loads += [(dst[:, k, :], src[k * P:(k + 1) * P, :]) for k in range(KC)]
        loads.append((bl[:], b_lora))
        attend(nc, masks, ident, q_hi, q_lo, k_hi, k_lo, v_all, o_all, sums, loads)
        finish(nc, (wd, wb, wra, bl), x, b_dense, b_base, rev_index, ident, o_all, sums, inv_sums, out)


def rope_table():
    half = np.arange(0, HD, 2, dtype=np.float32) / np.float32(HD)
    inv_freq = (np.float32(1.0) / np.power(np.float32(1000000.0), half)).astype(np.float32)
    freqs = np.outer(np.arange(SEQ, dtype=np.float32), inv_freq).astype(np.float32)
    emb = np.concatenate([freqs, freqs], axis=-1).astype(np.float64)
    cos, sin = np.cos(emb), np.sin(emb)
    sin[:, :HD // 2] *= -1.0
    table = np.stack([np.tile(cos.T, (P // HD, 1)), np.tile(sin.T, (P // HD, 1))], axis=1)
    table = table.reshape(P, 2, UPB, TG).transpose(2, 0, 1, 3)
    return np.ascontiguousarray(np.tile(table, (BATCH, 1, 1, 1)).astype(np.float32))


def kernel(L0_attn_hidden_states, L0_attn_w_qkv, L0_attn_b_qkv, L0_attn_w_dense, L0_attn_b_dense,
           L0_ffn_W_base, L0_ffn_b_base, L0_ffn_W_router, L0_ffn_A, L0_ffn_B):
    import concourse.bacc as bacc
    from concourse.bass_utils import run_bass_kernel_spmd

    arr = np.asarray
    w = arr(L0_attn_w_qkv).reshape(GROUPS, QPG + 2, HD, HID)
    b = arr(L0_attn_b_qkv).reshape(GROUPS, QPG + 2, HD)
    w_qk = np.concatenate([w[:, :QPG].reshape(-1, HID), w[:, QPG].reshape(-1, HID)]).T
    b_qk = np.concatenate([b[:, :QPG].reshape(-1), b[:, QPG].reshape(-1)]).reshape(QK_TILES, P).T
    lora_a = arr(L0_ffn_A).reshape(ER, HID)
    masks = np.zeros((P, P + BLOCK), np.float32)
    masks[:, :P][np.triu_indices(P, 1)] = NEG
    masks[P // 2:, P:] = NEG
    given = {
        "x": arr(L0_attn_hidden_states).reshape(BATCH * SEQ, HID),
        "w_qk": w_qk,
        "b_qk": b_qk,
        "w_v": w[:, QPG + 1].reshape(-1, HID).T,
        "b_v": b[:, QPG + 1].reshape(-1),
        "w_dense": arr(L0_attn_w_dense).T,
        "b_dense": arr(L0_attn_b_dense),
        "w_base": arr(L0_ffn_W_base).T,
        "b_base": arr(L0_ffn_b_base),
        "w_ra": np.concatenate([arr(L0_ffn_W_router), lora_a]).T,
        "b_lora": arr(L0_ffn_B).transpose(0, 2, 1).reshape(ER, HID),
        "rope": rope_table(),
        "ident": np.eye(P, dtype=np.float32),
        "masks": masks,
        "rev_index": np.arange(EXPERTS, 0, -1).astype(np.float32),
    }
    given = {k: np.ascontiguousarray(v) for k, v in given.items()}
    nc = bacc.Bacc("TRN2", target_bir_lowering=False, num_devices=1)
    aps = [nc.dram_tensor(f"{k}_dram", v.shape, F32, kind="ExternalInput").ap() for k, v in given.items()]
    out = nc.dram_tensor("out_dram", [BATCH * SEQ, HID], F32, kind="ExternalOutput").ap()
    build(nc, *aps, out)
    result = run_bass_kernel_spmd(nc, [{f"{k}_dram": v for k, v in given.items()}], core_ids=[0])
    return result.results[0]["out_dram"].reshape(BATCH, SEQ, HID)
```

```python
from contextlib import ExitStack

import numpy as np

import concourse.bass as bass
from concourse import mybir

F32 = mybir.dt.float32
F32R = mybir.dt.float32r
BF16 = mybir.dt.bfloat16
ALU = mybir.AluOpType
ACT = mybir.ActivationFunctionType
AX = mybir.AxisListType

P = 128
BATCH, SEQ, HID = 2, 2048, 1024
HEADS, GROUPS = 32, 8
HD = HID // HEADS
QPG = HEADS // GROUPS
EXPERTS, RANK = 8, 16
ER = EXPERTS * RANK
KC = HID // P
TG = 512
NTG = BATCH * SEQ // TG
TPG = TG // P
UPB = SEQ // TG
QK_TILES = GROUPS + GROUPS * HD // P
BLOCK, LOCAL, VERT = 64, 16, 8
BPT = P // BLOCK
LT = LOCAL // BPT
EPS = 1e-5
SM_SCALE = 1.0 / HD
NEG = -1.0e30
CREDIT = 16


def max_segments(tile):
    end = (tile + 1) * P
    if tile < LT:
        start, pieces = 0, []
        while end - start > 0:
            width = (end - start) % 512 or 512
            pieces.append((start, width))
            start += width
        return pieces
    start = (tile - LT) * P + BLOCK
    return [(start, BLOCK)] + [(start + BLOCK + i * 512, 512) for i in range(2)]


def has_vertical(tile):
    return tile > (VERT - 1) // BPT + LT


def edge_is_vertical(tile):
    return (BPT * (tile - LT) + 2) % VERT == 0


def steps_of(unit):
    first = unit * TPG
    last = first + TPG - 1
    steps = []
    for key in range(0, last + 1):
        lo = max(key, first)
        full = min(key + LT - 1, last)
        start = (lo - first) * P
        mid = max(full - first + 1, 0) * P if full >= lo else start
        end = mid
        if first <= key + LT <= last:
            end = mid + (P if edge_is_vertical(key + LT) else BLOCK)
        if (BPT * key + 2) % VERT == 0 and has_vertical(last) and key + LT < last:
            end = TG
        if end > start:
            steps.append((key, start, mid, end))
    steps.sort(key=lambda s: (s[0] != first, s[0]))
    assert steps[0][1] == 0 and steps[0][2] == TG
    return steps


def project(nc, x, w_qk, b_qk, w_v, b_v, rope, ident, q_hi, q_lo, k_hi, k_lo, v_out):
    with ExitStack() as ctx:
        sb = lambda name, shape, dt=F32: ctx.enter_context(nc.sbuf_tensor(name, shape, dt))
        ps = lambda name: ctx.enter_context(nc.psum_tensor(name, [P, 512], F32))
        sem = lambda name: ctx.enter_context(nc.semaphore(name))

        wqk = sb("wqk", [P, KC, QK_TILES * P])
        wv = sb("wv", [P, KC, GROUPS * HD])
        bqk = sb("bqk", [P, QK_TILES])
        bv = sb("bv", [P, GROUPS * HD])
        idn = sb("idn_p", [P, P])
        xin = sb("xin", [P, TPG, HID])
        stats = sb("stats_p", [P, TPG, 2, 6])
        mean_var = sb("mean_var_p", [P, TPG, 2])
        var_eps = sb("var_eps_p", [P, TPG])
        minus_half = sb("minus_half_p", [P, TPG])
        rstd = sb("rstd_p", [P, TPG])
        xn = [sb(f"xn{i}", [P, HID]) for i in range(2)]
        x_t = [sb(f"x_t{i}", [P, KC, TG]) for i in range(2)]
        cos_sin = [sb(f"cos_sin{i}", [P, 2, TG]) for i in range(2)]
        raw = [sb(f"raw{i}", [P, TG]) for i in range(2)]
        swapped = [sb(f"swapped{i}", [P, TG]) for i in range(2)]
        with_cos = [sb(f"with_cos{i}", [P, TG]) for i in range(2)]
        with_sin = [sb(f"with_sin{i}", [P, TG]) for i in range(2)]
        turned = [sb(f"turned{i}", [P, TG]) for i in range(2)]
        hi = [sb(f"hi{i}", [P, TG], F32R) for i in range(2)]
        lo = [sb(f"lo{i}", [P, TG], F32R) for i in range(2)]
        v_sb = [sb(f"v_sb{i}", [P, GROUPS * HD]) for i in range(2)]
        ps_t = [ps(f"ps_t{i}") for i in range(2)]
        ps_qk = [ps(f"ps_qk{i}") for i in range(4)]
        ps_v = [ps(f"ps_v{i}") for i in range(2)]

        passed = sem("passed_p")
        weights_in = sem("weights_in")
        consts_in = sem("consts_in")
        wv_in = sem("wv_in")
        x_in = [sem(f"x_in{t}") for t in range(TPG)]
        rope_in = [sem(f"rope_in{i}") for i in range(2)]
        stats_done = sem("stats_done")
        aggr_done = sem("aggr_done")
        eps_done = sem("eps_done")
        rstd_done = sem("rstd_done")
        xn_done = sem("xn_done")
        tr_done = sem("tr_done")
        xt_done = sem("xt_done")
        qk_done = sem("qk_done")
        raw_done = sem("raw_done")
        swap_done = sem("swap_done")
        cos_done = sem("cos_done")
        sin_done = sem("sin_done")
        turned_done = sem("turned_done")
        hi_done = sem("hi_done")
        lo_done = sem("lo_done")
        vps_done = sem("vps_done")
        v_done = sem("v_done")
        qk_stored = [sem(f"qk_stored{i}") for i in range(2)]
        v_stored = [sem(f"v_stored{i}") for i in range(2)]

        def x_tile(n, t):
            return x[bass.ds((n * TPG + t) * P, P), :]

        def table_loads(n, j):
            return (n - j) * 8 + 16

        NORM_AT = [1, 3, 5, 7]
        MOVE_AT = [2, 4, 6, 8]
        LAST = NTG - 1

        def loop_groups(eng, body):
            with eng.Fori(0, NTG // 2 - 1) as i:
                for j in range(2):
                    body(i * 2 + j, j, False)
            for j in range(2):
                body(NTG - 2 + j, j, j == 1)

        block = ctx.enter_context(nc.Block())

        @block.sync
        def _(sp):
            for i in range(2):
                sp.sem_inc(qk_stored[i], CREDIT * 4)
                sp.sem_inc(v_stored[i], CREDIT)
            sp.dma_start(idn[:], ident).then_inc(consts_in, 16)
            for t in range(TPG):
                sp.dma_start(xin[:, t, :], x_tile(0, t)).then_inc(x_in[t], 16)
            sp.dma_start(bqk[:], b_qk).then_inc(consts_in, 16)
            sp.dma_start(bv[:], b_v.partition_broadcast(P)).then_inc(consts_in, 16)
            for k in range(KC):
                sp.dma_start(wqk[:, k, :], w_qk[k * P:(k + 1) * P, :]).then_inc(weights_in, 16)
            sp.dma_start(cos_sin[0][:], rope[0]).then_inc(rope_in[0], 16)
            sp.dma_start(wv[:], w_v.rearrange("(k p) n -> p k n", p=P)).then_inc(wv_in, 16)
            for t in range(TPG):
                sp.wait_ge(xn_done, t + 1)
                sp.dma_start(xin[:, t, :], x_tile(1, t)).then_inc(x_in[t], 16)

            def body(n, j, last):
                if not last:
                    sp.dma_start(cos_sin[1 - j][:], rope[bass.ds(n + 1, 1)].rearrange("o p a s -> (o p) a s")
                                 ).then_inc(rope_in[1 - j], 16)
                for r in range(QK_TILES):
                    m = n * QK_TILES + r
                    sp.wait_ge(lo_done, m + 1 + CREDIT)
                    for part, (dq, dk) in ((hi, (q_hi, k_hi)), (lo, (q_lo, k_lo))):
                        if r < GROUPS:
                            dst = dq[bass.ds(n * GROUPS + r, 1)].rearrange("o p s -> (o p) s")
                        else:
                            dst = dk[bass.ds(n * 2 + (r - GROUPS), 1)].rearrange("o p s -> (o p) s")
                        sp.dma_start(dst.bitcast(F32), part[r % 2][:].bitcast(F32)
                                     ).then_inc(qk_stored[r % 2], 16)
                    if r in MOVE_AT and not last and not (isinstance(n, int) and n + 2 > LAST):
                        t = MOVE_AT.index(r)
                        sp.wait_ge(xn_done, (n + 1) * TPG + t + 1)
                        sp.dma_start(xin[:, t, :], x_tile(n + 2, t)).then_inc(x_in[t], 16)
                for t in range(TPG):
                    sp.wait_ge(v_done, n * TPG + t + 1 + CREDIT)
                    sp.dma_start(v_out[bass.ds((n * TPG + t) * P, P), :], v_sb[t % 2][:]
                                 ).then_inc(v_stored[t % 2], 16)

            loop_groups(sp, body)
            for i in range(2):
                sp.wait_ge(qk_stored[i], CREDIT * 4 + NTG * QK_TILES * 16)
                sp.wait_ge(v_stored[i], CREDIT + NTG * TPG // 2 * 16)

        @block.gpsimd
        def _(pool):
            pool.sem_inc(sin_done, CREDIT)
            pool.memset(minus_half[:], -0.5).then_inc(rstd_done, 1)

            def group_rstd(n):
                pool.wait_ge(eps_done, n + 1)
                if isinstance(n, int) and n == 0:
                    pool.wait_ge(rstd_done, 1)
                pool.tensor_tensor(rstd[:], var_eps[:], minus_half[:], ALU.pow).then_inc(rstd_done, 1)

            group_rstd(0)

            def body(n, j, last):
                pool.wait_ge(rope_in[j], table_loads(n, j))
                if not last:
                    group_rstd(n + 1)
                for r in range(QK_TILES):
                    m = n * QK_TILES + r
                    pool.wait_ge(swap_done, m + 1)
                    pool.wait_ge(turned_done, m - 1 + CREDIT)
                    pool.tensor_tensor(with_sin[r % 2][:], swapped[r % 2][:], cos_sin[j][:, 1, :],
                                       ALU.mult).then_inc(sin_done, 1)

            loop_groups(pool, body)

        @block.scalar
        def _(act):
            act.sem_inc(raw_done, CREDIT)
            act.sem_inc(xt_done, CREDIT)

            def move(n, t, buf):
                for half in range(2):
                    act.wait_ge(tr_done, (n * TPG + t) * 2 + half + 1)
                    act.activation(x_t[buf][:, half * 4:half * 4 + 4, t * P:(t + 1) * P],
                                   ps_t[half][:].rearrange("p (k s) -> p k s", k=4),
                                   ACT.Copy).then_inc(xt_done, 1)

            act.wait_ge(consts_in, 48)
            for t in range(TPG):
                move(0, t, 0)

            def body(n, j, last):
                def split_hi(r):
                    m = n * QK_TILES + r
                    act.wait_ge(turned_done, m + 1 + CREDIT)
                    act.wait_ge(qk_stored[r % 2], (n * (QK_TILES // 2) + r // 2) * 32 + CREDIT * 4)
                    act.activation(hi[r % 2][:], turned[r % 2][:], ACT.Copy,
                                   scale=SM_SCALE if r < GROUPS else 1.0).then_inc(hi_done, 1)

                for r in range(QK_TILES + 2):
                    if r < QK_TILES:
                        m = n * QK_TILES + r
                        act.wait_ge(qk_done, m + 1)
                        act.wait_ge(cos_done, m - 1 + CREDIT)
                        act.activation(raw[r % 2][:], ps_qk[(j * QK_TILES + r) % 4][:], ACT.Identity,
                                       bias=bqk[:, r:r + 1]).then_inc(raw_done, 1)
                    if r >= 2:
                        split_hi(r - 2)
                    if r in MOVE_AT and not last:
                        move(n + 1, MOVE_AT.index(r), 1 - j)

            loop_groups(act, body)

        @block.vector
        def _(dve):
            dve.sem_inc(turned_done, CREDIT)
            dve.sem_inc(lo_done, CREDIT)
            dve.sem_inc(cos_done, CREDIT)
            dve.sem_inc(v_done, CREDIT)

            def group_stats(n):
                for t in range(TPG):
                    dve.wait_ge(x_in[t], (n + 1) * 16)
                    for half in range(2):
                        last = dve.bn_stats(stats[:, t, half, :], xin[:, t, half * 512:(half + 1) * 512])
                    last.then_inc(stats_done, 1)
                for t in range(TPG):
                    dve.wait_ge(stats_done, n * TPG + t + 1)
                    dve.sem_inc(passed, 1)
                    last = dve.bn_aggr(mean_var[:, t, :], stats[:, t].rearrange("p a b -> p (a b)"))
                last.then_inc(aggr_done, 1)
                dve.wait_ge(aggr_done, n + 1)
                dve.tensor_scalar(var_eps[:], mean_var[:, :, 1], EPS, None, ALU.add).then_inc(eps_done, 1)

            def normalise(n, t):
                if t == 0:
                    dve.wait_ge(rstd_done, n + 2)
                if not (isinstance(n, int) and n == 0 and t < 2):
                    dve.wait_ge(tr_done, (n * TPG + t - 1) * 2)
                dve.tensor_scalar(xn[t % 2][:], xin[:, t, :], mean_var[:, t, 0:1], rstd[:, t:t + 1],
                                  ALU.subtract, ALU.mult).then_inc(xn_done, 1)

            group_stats(0)
            for t in range(TPG):
                normalise(0, t)
            dve.wait_ge(consts_in, 48)

            def body(n, j, last):
                dve.wait_ge(rope_in[j], table_loads(n, j))
                if not last:
                    group_stats(n + 1)
                for r in range(QK_TILES + 3):
                    if r < QK_TILES:
                        m = n * QK_TILES + r
                        dve.wait_ge(raw_done, m + 1 + CREDIT)
                        dve.wait_ge(sin_done, m - 1 + CREDIT)
                        dve.sem_inc(passed, 1)
                        dve.stream_shuffle(swapped[r % 2][:], raw[r % 2][:],
                                           [(i + HD // 2) % HD for i in range(HD)]).then_inc(swap_done, 1)
                        dve.wait_ge(turned_done, m - 1 + CREDIT)
                        dve.tensor_tensor(with_cos[r % 2][:], raw[r % 2][:], cos_sin[j][:, 0, :],
                                          ALU.mult).then_inc(cos_done, 1)
                    if r >= 3:
                        q = r - 3
                        dve.wait_ge(hi_done, n * QK_TILES + q + 1)
                        dve.scalar_tensor_tensor(lo[q % 2][:], turned[q % 2][:],
                                                 SM_SCALE if q < GROUPS else 1.0,
                                                 hi[q % 2][:].bitcast(F32), op0=ALU.mult,
                                                 op1=ALU.subtract).then_inc(lo_done, 1)
                    if 1 <= r <= QK_TILES:
                        m = n * QK_TILES + r - 1
                        dve.wait_ge(cos_done, m + 1 + CREDIT)
                        dve.wait_ge(sin_done, m + 1 + CREDIT)
                        dve.wait_ge(lo_done, m - 1 + CREDIT)
                        dve.tensor_tensor(turned[(r - 1) % 2][:], with_cos[(r - 1) % 2][:],
                                          with_sin[(r - 1) % 2][:], ALU.add).then_inc(turned_done, 1)
                    if r in NORM_AT and not last:
                        normalise(n + 1, NORM_AT.index(r))
                for t in range(TPG):
                    dve.wait_ge(vps_done, n * TPG + t + 1)
                    dve.wait_ge(v_stored[t % 2], (n * 2 + t // 2) * 16 + CREDIT)
                    dve.tensor_tensor(v_sb[t % 2][:], ps_v[t % 2][:, 0:GROUPS * HD], bv[:],
                                      ALU.add).then_inc(v_done, 1)

            loop_groups(dve, body)

        @block.tensor
        def _(pe):
            def transposes(n, t):
                pe.wait_ge(xn_done, n * TPG + t + 1)
                for half in range(2):
                    pe.wait_ge(xt_done, (n * TPG + t - 1) * 2 + half + 1 + CREDIT)
                    for c in range(4):
                        k = half * 4 + c
                        last = pe.transpose(ps_t[half][:, c * P:(c + 1) * P],
                                            xn[t % 2][:, k * P:(k + 1) * P], idn[:])
                    last.then_inc(tr_done, 1)

            pe.wait_ge(consts_in, 48)
            for t in range(TPG):
                transposes(0, t)
            pe.wait_ge(weights_in, KC * 16)
            pe.wait_ge(wv_in, 16)

            def body(n, j, last):
                pe.wait_ge(xt_done, (n + 1) * TPG * 2 + CREDIT)
                for r in range(QK_TILES):
                    m = n * QK_TILES + r
                    pe.wait_ge(raw_done, m - 3 + CREDIT)
                    for k in range(KC):
                        mm = pe.matmul(ps_qk[(j * QK_TILES + r) % 4][:], wqk[:, k, r * P:(r + 1) * P],
                                       x_t[j][:, k, :], start=(k == 0), stop=(k == KC - 1))
                    mm.then_inc(qk_done, 1)
                    if r in MOVE_AT and not last:
                        transposes(n + 1, MOVE_AT.index(r))
                for t in range(TPG):
                    pe.wait_ge(v_done, n * TPG + t - 1 + CREDIT)
                    for k in range(KC):
                        mm = pe.matmul(ps_v[t % 2][:, 0:GROUPS * HD], x_t[j][:, k, t * P:(t + 1) * P],
                                       wv[:, k, :], start=(k == 0), stop=(k == KC - 1))
                    mm.then_inc(vps_done, 1)

            loop_groups(pe, body)


def attend(nc, masks, ident, q_hi, q_lo, k_hi, k_lo, v_in, o_out, sum_out, finish_weights):
    STEPS = [steps_of(u) for u in range(UPB)]
    NS = [len(s) for s in STEPS]
    CHUNKS = [[(tl, h, c) for h in range(QPG) for tl in range(TPG)
               for c in range(len(max_segments(u * TPG + tl)))] for u in range(UPB)]
    NCH = [len(c) for c in CHUNKS]
    UNITS = 2 * UPB
    step0 = [sum(NS[w % UPB] for w in range(u)) for u in range(UNITS + 1)]
    chunk0 = [sum(NCH[w % UPB] for w in range(u)) for u in range(UNITS + 1)]
    fixes = [[s for s in STEPS[u] if s[0] >= u * TPG or s[3] > s[2]] for u in range(UPB)]
    fix0 = [sum(len(fixes[w % UPB]) * QPG for w in range(u)) for u in range(UNITS + 1)]
    BODY_STEPS, BODY_CHUNKS, BODY_FIXES = step0[-1], chunk0[-1], fix0[-1]
    assert BODY_STEPS % 2 == 0 and all(n % 2 == 0 for n in NCH)
    BODIES = BATCH * GROUPS // 2

    with ExitStack() as ctx:
        sb = lambda name, shape, dt=F32: ctx.enter_context(nc.sbuf_tensor(name, shape, dt))
        ps = lambda name: ctx.enter_context(nc.psum_tensor(name, [P, 512], F32))
        sem = lambda name: ctx.enter_context(nc.semaphore(name))

        kp = [sb(f"kp{i}", [P, SEQ], F32R) for i in range(2)]
        qp = [sb(f"qp{i}", [P, QPG, TG], F32R) for i in range(4)]
        v1 = [sb(f"v1_{i}", [P, SEQ // P, 2 * HD]) for i in range(2)]
        probs = [[sb(f"probs{i}_{h}", [P, TG]) for h in range(QPG)] for i in range(2)]
        part_max = sb("part_max", [P, QPG * TPG, 3])
        neg_max = [sb(f"neg_max{i}", [P, QPG * TPG]) for i in range(2)]
        max_row = [sb(f"max_row{i}", [QPG * TPG, P], F32R) for i in range(2)]
        o_sb = [sb(f"o_sb{i}", [P, 2, TG]) for i in range(2)]
        idn = sb("idn_a", [P, P])
        idn_bf = sb("idn_bf", [P, P], BF16)
        mask_f = sb("mask_f", [P, P + BLOCK])
        mask_bf = sb("mask_bf", [P, P + BLOCK], BF16)
        ps_max = [ps(f"ps_max{i}") for i in range(2)]
        ps_s = [ps(f"ps_s{h}") for h in range(QPG)]
        ps_o = [ps(f"ps_o{i}") for i in range(2)]

        passed = sem("passed_a")
        consts_in = sem("consts_in_a")
        consts_bf = sem("consts_bf")
        ones_set = sem("ones_set")
        q_in = [sem(f"q_in{i}") for i in range(4)]
        k_in = [sem(f"k_in{i}") for i in range(2)]
        v_in_s = [sem(f"v_in{i}") for i in range(2)]
        row_in = [sem(f"row_in{i}") for i in range(2)]
        chunk_done = sem("chunk_done")
        reduced = sem("reduced")
        neg_done = sem("neg_done")
        rowt_done = sem("rowt_done")
        row_done = sem("row_done")
        scores_done = sem("scores_done")
        exp_done = sem("exp_done")
        fix_done = sem("fix_done")
        pv_done = sem("pv_done")
        o_done = sem("o_done")
        o_stored = [sem(f"o_stored{i}") for i in range(2)]
        weights3_in = sem("weights3_in")

        block = ctx.enter_context(nc.Block())

        def body_groups(n):
            b = n >> 2
            if not isinstance(n, int):
                b.max_val = BATCH - 1
            return b, (n & 3) * 2

        def load_q(sp, n, u):
            b, g = body_groups(n)
            blk = (b * UPB + u % UPB) * GROUPS + g + u // UPB
            for part, src in ((0, q_hi), (1, q_hi), (2, q_lo)):
                sp.dma_start(qp[u % 4][part * HD:(part + 1) * HD].bitcast(F32),
                             src[bass.ds(blk, 1)].rearrange("o (h d) s -> (o d) h s", h=QPG).bitcast(F32)
                             ).then_inc(q_in[u % 4], 16)

        def load_kv(sp, n, j):
            b, g = body_groups(n)
            for part, src in ((0, k_hi), (1, k_lo), (2, k_hi)):
                sp.dma_start(kp[j][part * HD:(part + 1) * HD].rearrange("d (n s) -> d n s", n=UPB).bitcast(F32),
                             src.rearrange("(n g) d s -> n g d s", g=GROUPS)[bass.ds(b * UPB, UPB), bass.ds(g + j, 1)]
                             .rearrange("n o d s -> (o d) n s").bitcast(F32)
                             ).then_inc(k_in[j], 16)
            sp.dma_start(v1[j][:, :, 0:HD],
                         v_in[bass.ds(b * SEQ, SEQ), bass.ds((g + j) * HD, HD)].rearrange("(t p) d -> p t d", p=P)
                         ).then_inc(v_in_s[j], 16)

        EARLY = 4
        HEAD = EARLY + 12
        STREAM = [[(2, EARLY, HEAD)], [(1, HEAD, NCH[2])], [(1, 0, NCH[3])],
                  [(1, 0, NCH[0]), (2, 0, NCH[1]), (3, 0, EARLY)]]
        ROWS = [[], [(1, NCH[2] - HEAD)], [(1, NCH[3])],
                [(1, NCH[0] + EARLY), (2, NCH[0] + NCH[1] + EARLY)]]

        def plan_of(v):
            stream = [(ahead, c) for ahead, a, z in STREAM[v] for c in range(a, z)]
            steps = NS[v] if not ROWS[v] else NS[v] - 2
            weight = [end - start for _, start, _, end in STEPS[v][:steps]]
            rows, done, slots = {}, 0, []
            left = list(ROWS[v])
            for s in range(NS[v]):
                if left and s < NS[v] - 1 and done >= left[0][1] and s not in rows:
                    rows[s] = left.pop(0)[0]
                upto = len(stream) * sum(weight[:s + 1]) // sum(weight)
                take = stream[done:upto - upto % 2]
                done += len(take)
                slots.append([take[i * len(take) // 4:(i + 1) * len(take) // 4] for i in range(4)])
            assert done == len(stream) and not left, (v, done, left)
            return slots, rows

        PLANS = [plan_of(v) for v in range(UPB)]

        def bank_width(tile, seg):
            width = max_segments(tile)[seg][1]
            return width + BLOCK if seg == 0 and has_vertical(tile) else width

        def first_chunk(u):
            return u // UNITS * BODY_CHUNKS + chunk0[u % UNITS]

        def loop_bodies(eng, body):
            with eng.Fori(0, BODIES - 1) as n:
                body(n, False)
            body(BODIES - 1, True)

        @block.sync
        def _(sp):
            for i in range(2):
                sp.sem_inc(row_in[i], CREDIT)
                sp.sem_inc(o_stored[i], CREDIT)
            sp.dma_start(idn[:], ident).then_inc(consts_in, 16)
            sp.dma_start(mask_f[:], masks).then_inc(consts_in, 16)

            def put_row(u, n):
                sp.wait_ge(row_done, n * UNITS + u + 1 + CREDIT)
                sp.dma_start(qp[u % 4][3 * HD:3 * HD + 1].bitcast(F32), max_row[u % 2][:].bitcast(F32)
                             ).then_inc(row_in[u % 2], 16)

            def store_o(n, u):
                sp.wait_ge(o_done, (n * UNITS + u + 1) * 2 + CREDIT)
                b, g = body_groups(n)
                blk = (b * UPB + u % UPB) * GROUPS + g + u // UPB
                for hh in range(2):
                    for dst, first, size in ((o_out, 0, HD), (sum_out, HD, 1)):
                        sp.dma_start(dst[bass.ds(blk, 1)].rearrange("o (i h d) s -> h (o d) i s", i=2, h=2)[hh],
                                     o_sb[u % 2][hh * 2 * HD + first:hh * 2 * HD + first + size]
                                     ).then_inc(o_stored[u % 2], 16)

            load_kv(sp, 0, 0)
            for u in range(3):
                load_q(sp, 0, u)
            load_kv(sp, 0, 1)
            put_row(0, 0)
            put_row(1, 0)

            def body(n, last):
                for u in range(UNITS):
                    if not (last and u + 3 >= UNITS):
                        sp.wait_ge(scores_done, (n * BODY_STEPS + step0[u]) * QPG + CREDIT)
                        load_q(sp, n + (u + 3) // UNITS, (u + 3) % UNITS)
                    if u == UPB and not last:
                        sp.wait_ge(pv_done, n * BODY_STEPS + step0[UPB] + CREDIT)
                        load_kv(sp, n + 1, 0)
                    if u > 0:
                        store_o(n, u - 1)
                    if not (last and u + 1 == UNITS):
                        for ahead, _ in ROWS[u % UPB]:
                            put_row(u + ahead, n)
                store_o(n, UNITS - 1)
                if not last:
                    load_kv(sp, n + 1, 1)

            loop_bodies(sp, body)
            for i in range(2):
                sp.wait_ge(o_stored[i], CREDIT + BODIES * UNITS // 2 * 64)

        @block.gpsimd
        def _(pool):
            for j in range(2):
                pool.memset(v1[j][:, :, HD:2 * HD], 1.0).then_inc(ones_set, 1)

            def body(n, last):
                for u in range(UNITS):
                    for s, (key, start, mid, end) in enumerate(STEPS[u % UPB]):
                        step = step0[u] + s
                        if (key, start, mid, end) not in fixes[u % UPB]:
                            continue
                        for h in range(QPG):
                            pool.wait_ge(exp_done, (n * BODY_STEPS + step) * QPG + h + 1)
                            pool.sem_inc(passed, 1)
                            p = probs[step % 2][h]
                            if key >= (u % UPB) * TPG:
                                pool.affine_select(out=p[:, start:start + P], in_=p[:, start:start + P],
                                                   compare_op=ALU.is_ge, fill=0.0, base=0,
                                                   pattern=[[1, P]], channel_multiplier=-1
                                                   ).then_inc(fix_done, 1)
                            else:
                                pool.affine_select(out=p[:, mid:end], in_=p[:, mid:end],
                                                   compare_op=ALU.is_ge, fill=0.0, base=-BLOCK,
                                                   pattern=[[0, end - mid]], channel_multiplier=1
                                                   ).then_inc(fix_done, 1)

            loop_bodies(pool, body)

        @block.scalar
        def _(act):
            act.sem_inc(row_done, CREDIT)
            act.sem_inc(o_done, CREDIT)
            for dst, src in finish_weights:
                act.dma_start(dst, src).then_inc(weights3_in, 16)

            def row(u, n):
                act.wait_ge(rowt_done, n * UNITS + u + 1)
                act.wait_ge(row_in[u % 2], (n * (UNITS // 2) + u // 2) * 16 + CREDIT)
                act.activation(max_row[u % 2][:], ps_max[0][0:QPG * TPG, 0:P], ACT.Copy
                               ).then_inc(row_done, 1)

            def out(u, n):
                act.wait_ge(pv_done, n * BODY_STEPS + step0[u + 1] + CREDIT)
                act.wait_ge(o_stored[u % 2], (n * (UNITS // 2) + u // 2) * 64 + CREDIT)
                for i in range(2):
                    act.activation(o_sb[u % 2][:, i, :], ps_o[i][:], ACT.Copy).then_inc(o_done, 1)

            row(0, 0)
            row(1, 0)

            def body(n, last):
                for u in range(UNITS):
                    final = last and u + 1 == UNITS
                    for s, (key, start, mid, end) in enumerate(STEPS[u % UPB]):
                        step = step0[u] + s
                        act.wait_ge(pv_done, n * BODY_STEPS + step - 1 + CREDIT)
                        for h in range(QPG):
                            act.wait_ge(scores_done, (n * BODY_STEPS + step) * QPG + h + 1 + CREDIT)
                            act.activation(probs[step % 2][h][:, start:end], ps_s[h][:, start:end],
                                           ACT.Exp).then_inc(exp_done, 1)
                            if h == 0 and s - 1 in PLANS[u % UPB][1] and not final:
                                row(u + PLANS[u % UPB][1][s - 1], n)
                        if s == 0 and u > 0:
                            out(u - 1, n)
                out(UNITS - 1, n)

            loop_bodies(act, body)
            act.wait_ge(weights3_in, 16 * len(finish_weights))

        @block.vector
        def _(dve):
            dve.sem_inc(reduced, CREDIT)
            dve.sem_inc(neg_done, CREDIT)
            dve.wait_ge(consts_in, 32)
            dve.tensor_copy(idn_bf[:], idn[:]).then_inc(consts_bf, 1)
            dve.tensor_copy(mask_bf[:], mask_f[:]).then_inc(consts_bf, 1)
            for j in range(2):
                dve.memset(kp[j][3 * HD:3 * HD + 1, :].bitcast(F32), 1.0).then_inc(ones_set, 1)

            def maxima(u, n, a, z):
                if a == 0:
                    dve.wait_ge(neg_done, n * UNITS + u + CREDIT)
                chunk_n = n * BODY_CHUNKS + first_chunk(u)
                for c in range(a, z):
                    tl, h, seg = CHUNKS[u % UPB][c]
                    width = bank_width((u % UPB) * TPG + tl, seg)
                    dve.wait_ge(chunk_done, chunk_n + c + 1)
                    dve.reduce_max(part_max[:, h * TPG + tl, seg:seg + 1], ps_max[c % 2][:, 0:width],
                                   AX.X).then_inc(reduced, 1)
                if z == NCH[u % UPB]:
                    n_seg = len(max_segments((u % UPB) * TPG))
                    dve.wait_ge(reduced, chunk_n + z + CREDIT)
                    dve.wait_ge(row_done, n * UNITS + u - 1 + CREDIT)
                    dve.tensor_reduce(neg_max[u % 2][:], part_max[:, :, 0:n_seg], AX.X, ALU.max,
                                      negate=True).then_inc(neg_done, 1)

            maxima(0, 0, 0, NCH[0])
            maxima(1, 0, 0, NCH[1])
            maxima(2, 0, 0, EARLY)

            def body(n, last):
                for u in range(UNITS):
                    if not (last and u + 1 == UNITS):
                        for ahead, a, z in STREAM[u % UPB]:
                            maxima(u + ahead, n, a, z)

            loop_bodies(dve, body)

        @block.tensor
        def _(pe):
            pe.sem_inc(scores_done, CREDIT)
            pe.sem_inc(pv_done, CREDIT)

            def chunk(u, c, n, row_unit=None):
                tl, h, seg = CHUNKS[u % UPB][c]
                tile = (u % UPB) * TPG + tl
                segs = max_segments(tile)
                start, width = segs[seg]
                k = kp[(u // UPB) % 2]
                bank = ps_max[c % 2]
                if c == 0:
                    pe.wait_ge(q_in[u % 4], n * 96 + (u // 4 + 1) * 48)
                    if u % UPB == 0:
                        pe.wait_ge(k_in[(u // UPB) % 2], n * 48 + (u // UNITS + 1) * 48)
                if row_unit is not None:
                    pe.wait_ge(row_done, n * UNITS + row_unit + 1 + CREDIT)
                pe.wait_ge(reduced, n * BODY_CHUNKS + first_chunk(u) + c - 1 + CREDIT)
                diag = seg == len(segs) - 1
                edge = tile >= LT and seg == 0 and not edge_is_vertical(tile)
                lhs = qp[u % 4][0:3 * HD, h, tl * P:(tl + 1) * P]
                if seg == 0 and has_vertical(tile):
                    vert = (VERT - 1) * BLOCK
                    step = start - vert
                    rhs = k[0:3 * HD, vert:vert + 2 * step].rearrange("p (a b) -> p a b", a=2)[:, :, 0:BLOCK]
                    mm = pe.matmul(bank[:, 0:2 * BLOCK], lhs, rhs, start=True, stop=not edge)
                    at = BLOCK
                else:
                    mm = pe.matmul(bank[:, 0:width], lhs, k[0:3 * HD, start:start + width],
                                   start=True, stop=not (edge or diag))
                    at = 0
                if edge:
                    mm = pe.matmul(bank[:, at:at + BLOCK], idn_bf[:], mask_bf[:, P:P + BLOCK],
                                   start=False, stop=True)
                if diag:
                    mm = pe.matmul(bank[:, width - P:width], idn_bf[:], mask_bf[:, 0:P],
                                   start=False, stop=True)
                mm.then_inc(chunk_done, 1)

            def turn_row(u, n, chunks):
                pe.wait_ge(neg_done, n * UNITS + u + 1 + CREDIT)
                pe.wait_ge(reduced, n * BODY_CHUNKS + chunks - 1 + CREDIT)
                pe.transpose(ps_max[0][0:QPG * TPG, 0:P], neg_max[u % 2][:], idn[:]
                             ).then_inc(rowt_done, 1)

            def scores(u, s, h, n):
                key, start, mid, end = STEPS[u % UPB][s]
                j, step = (u // UPB) % 2, u // UNITS * BODY_STEPS + step0[u % UNITS] + s
                if s == 0:
                    pe.wait_ge(row_in[u % 2], (n * (UNITS // 2) + u // 2 + 1) * 16 + CREDIT)
                if step > 0:
                    pe.wait_ge(exp_done, (n * BODY_STEPS + step - 1) * QPG + h + 1)
                pe.matmul(ps_s[h][:, start:end], kp[j][0:3 * HD + 1, key * P:(key + 1) * P],
                          qp[u % 4][0:3 * HD + 1, h, start:end], start=True, stop=True
                          ).then_inc(scores_done, 1)

            def context(u, s, h, n):
                key, start, mid, end = STEPS[u % UPB][s]
                if (key, start, mid, end) in fixes[u % UPB]:
                    before = len([x for x in STEPS[u % UPB][:s] if x in fixes[u % UPB]])
                    pe.wait_ge(fix_done, n * BODY_FIXES + fix0[u] + before * QPG + h + 1)
                pe.wait_ge(exp_done, (n * BODY_STEPS + step0[u] + s) * QPG + h + 1)
                if s == 0:
                    if u % UPB == 0:
                        pe.wait_ge(v_in_s[u // UPB], n * 16 + 16)
                    pe.wait_ge(o_done, (n * UNITS + u - 1) * 2 + h // 2 + 1 + CREDIT)
                rows = slice((h % 2) * 2 * HD, (h % 2 + 1) * 2 * HD)
                mm = pe.matmul(ps_o[h // 2][rows, start:end], v1[(u // UPB) % 2][:, key, :],
                               probs[(step0[u] + s) % 2][h][:, start:end],
                               start=(s == 0), stop=(s == NS[u % UPB] - 1), skip_group_check=True,
                               tile_position=(0, (h % 2) * 2 * HD))
                if h == QPG - 1:
                    mm.then_inc(pv_done, 1)

            pe.wait_ge(consts_bf, 2)
            pe.wait_ge(ones_set, 4)
            for c in range(NCH[0]):
                chunk(0, c, 0)
            for c in range(NCH[1]):
                if c == EARLY:
                    turn_row(0, 0, first_chunk(1) + c)
                chunk(1, c, 0, 0 if c == EARLY else None)
            for c in range(EARLY):
                chunk(2, c, 0)
            turn_row(1, 0, first_chunk(2) + EARLY)
            for h in range(QPG):
                scores(0, 0, h, 0)

            def body(n, last):
                row_unit = 1
                for u in range(UNITS):
                    final = last and u + 1 == UNITS
                    slots, rows = PLANS[u % UPB]
                    for s in range(NS[u % UPB]):
                        for slot in range(4):
                            for h in (slot // 2 * 2, slot // 2 * 2 + 1):
                                if slot % 2:
                                    context(u, s, h, n)
                                elif s + 1 < NS[u % UPB]:
                                    scores(u, s + 1, h, n)
                                elif not final:
                                    scores(u + 1, 0, h, n)
                            if final:
                                continue
                            if slot == 0 and s in rows:
                                row_unit = u + rows[s]
                                ahead, c = next(x for sl in plan_after(u, s) for x in sl)
                                turn_row(row_unit, n, first_chunk(u + ahead) + c)
                            for ahead, c in slots[s][slot]:
                                chunk(u + ahead, c, n, row_unit)
                                row_unit = None

            def plan_after(u, s):
                for later in range(UPB):
                    for step, slots in enumerate(PLANS[(u + later) % UPB][0]):
                        if later or step >= s:
                            for slot in slots:
                                yield [(later + ahead, c) for ahead, c in slot]

            loop_bodies(pe, body)


def finish(nc, weights, x, b_dense, b_base, rev_index, ident, o_in, sum_in, inv_dram, out):
    w_dense, w_base, w_ra, b_lora = weights
    with ExitStack() as ctx:
        sb = lambda name, shape, dt=F32: ctx.enter_context(nc.sbuf_tensor(name, shape, dt))
        ps = lambda name, width=512: ctx.enter_context(nc.psum_tensor(name, [P, width], F32))
        sem = lambda name: ctx.enter_context(nc.semaphore(name))
        two = lambda name, shape: [sb(f"{name}{i}", shape) for i in range(2)]

        idn = sb("idn_f", [P, P])
        bd, bb = sb("bd", [P, HID]), sb("bb", [P, HID])
        rev = sb("rev", [P, EXPERTS])
        minus_half = sb("minus_half_f", [P, 1])
        ctx_t, inv, xt = two("ctx_t", [P, KC, P]), two("inv", [P, KC, P]), two("x_res", [P, HID])
        a_sb, y_sb, x1 = two("a_sb", [P, HID]), two("y_sb", [P, HID]), two("x1_", [P, HID])
        xn2, x2_t = two("xn2_", [P, HID]), two("x2_t", [P, KC, P])
        f_sb, z_sb, out_sb = two("f_sb", [P, HID]), two("z_sb", [P, HID]), two("out_sb", [P, HID])
        stats = [two(f"stats{k}_", [P, 2, 6]) for k in range(3)]
        mean_var = [two(f"mean_var{k}_", [P, 2]) for k in range(3)]
        var_eps = [two(f"var_eps{k}_", [P, 1]) for k in range(3)]
        rstd = [two(f"rstd{k}_", [P, 1]) for k in range(3)]
        shift = [two(f"shift{k}_", [P, 1]) for k in range(3)]
        logits, top, first, second = (two(f"{k}_", [P, EXPERTS]) for k in ("logits", "top", "first", "second"))
        score, best = two("score", [P, EXPERTS]), two("best", [P, 1])
        gap, expo, half, w1, w2 = (two(f"{k}_", [P, 1]) for k in ("gap", "expo", "half", "w1", "w2"))
        comb, hw, hw_t = two("comb", [P, EXPERTS]), two("hw", [P, ER]), two("hw_t", [P, P])
        ps_d, ps_f = ps("ps_d", HID), ps("ps_f", HID)
        ps_x = [ps(f"ps_x{i}") for i in range(2)]
        ps_ra, ps_h = ps("ps_ra"), ps("ps_h")

        passed = sem("passed_f")
        consts_in = sem("consts_in_f")
        sums_in = sem("sums_in")
        sums_inv = sem("sums_inv")
        inv_kept = sem("inv_kept")
        half_set = sem("half_set")
        o_loaded = [sem(f"o_loaded{i}") for i in range(2)]
        inv_loaded = [sem(f"inv_loaded{i}") for i in range(2)]
        x_loaded = [sem(f"x_loaded{i}") for i in range(2)]
        out_stored = [sem(f"out_stored{i}") for i in range(2)]
        ctx_done = sem("ctx_done")
        dense_done = sem("dense_done")
        a_done = sem("a_done")
        eps_done = [sem(f"eps_done{k}") for k in range(3)]
        rstd_done = [sem(f"rstd_done{k}") for k in range(3)]
        shift_done = [sem(f"shift_done{k}") for k in range(3)]
        y_done = sem("y_done")
        x1_done = sem("x1_done")
        xn2_done = sem("xn2_done")
        x2_turned = sem("x2_turned")
        x2_moved = sem("x2_moved")
        ra_done = sem("ra_done")
        gap_done = sem("gap_done")
        expo_done = sem("expo_done")
        hw_done = sem("hw_done")
        hwt_turned = sem("hwt_turned")
        hwt_done = sem("hwt_done")
        ffn_done = sem("ffn_done")
        f_done = sem("f_done")
        z_done = sem("z_done")
        out_done = sem("out_done")
        chain = sem("chain")
        chain_first = sem("chain_first")

        NT = NTG * TPG

        def loop_tiles(eng, body):
            with eng.Fori(0, NTG - 1) as n:
                for t in range(TPG):
                    body(n, t, NT)
            for t in range(TPG):
                body(NTG - 1, t, TPG - 1 - t)

        block = ctx.enter_context(nc.Block())

        @block.sync
        def _(sp):
            sp.dma_start(inv[0][:].rearrange("p k s -> p (k s)"),
                         sum_in.rearrange("b h s -> (b h s)").rearrange("(p n) -> p n", p=P)
                         ).then_inc(sums_in, 16)
            sp.dma_start(idn[:], ident).then_inc(consts_in, 16)
            sp.dma_start(bd[:], b_dense.partition_broadcast(P)).then_inc(consts_in, 16)
            sp.dma_start(bb[:], b_base.partition_broadcast(P)).then_inc(consts_in, 16)
            sp.dma_start(rev[:], rev_index.partition_broadcast(P)).then_inc(consts_in, 16)
            sp.wait_ge(sums_inv, 1)
            sp.dma_start(inv_dram.rearrange("b h s -> (b h s)").rearrange("(p n) -> p n", p=P),
                         inv[1][:].rearrange("p k s -> p (k s)")).then_inc(inv_kept, 16)
            sp.wait_ge(inv_kept, 16)

            def load(n, t):
                n, t = n + t // TPG, t % TPG
                i = t % 2
                cols = slice(t * P, (t + 1) * P)
                sp.dma_start(ctx_t[i][:], o_in[bass.ds(n * GROUPS, GROUPS), :, cols].rearrange("g p s -> p g s")
                             ).then_inc(o_loaded[i], 16)
                for h in range(QPG):
                    sp.dma_start(inv[i][h * HD:(h + 1) * HD],
                                 inv_dram[bass.ds(n * GROUPS, GROUPS), h, cols].partition_broadcast(HD)
                                 ).then_inc(inv_loaded[i], 16)
                sp.dma_start(xt[i][:], x[bass.ds((n * TPG + t) * P, P), :]).then_inc(x_loaded[i], 16)

            load(0, 0)
            load(0, 1)

            def body(n, t, rest):
                if rest >= 2:
                    sp.wait_ge(dense_done, n * TPG + t + 1)
                    sp.wait_ge(x1_done, n * TPG + t + 1)
                    load(n, t + 2)
                sp.wait_ge(out_done, n * TPG + t + 1 + CREDIT)
                sp.dma_start(out[bass.ds((n * TPG + t) * P, P), :], out_sb[t % 2][:]
                             ).then_inc(out_stored[t % 2], 16)

            loop_tiles(sp, body)
            for i in range(2):
                sp.wait_ge(out_stored[i], CREDIT * 2 + NT // 2 * 16)

        @block.gpsimd
        def _(pool):
            for i in range(2):
                pool.sem_inc(out_stored[i], CREDIT * 2)
            pool.memset(minus_half[:], -0.5).then_inc(half_set, 1)
            pool.wait_ge(half_set, 1)

            def root(k, n, t):
                n, i = n + t // TPG, t % 2
                pool.wait_ge(eps_done[k], n * TPG + t % TPG + 1)
                pool.tensor_tensor(rstd[k][i][:], var_eps[k][i][:], minus_half[:], ALU.pow
                                   ).then_inc(rstd_done[k], 1)

            root(0, 0, 0)
            root(1, 0, 0)

            def body(n, t, rest):
                if rest >= 1:
                    root(0, n, t + 1)
                    root(1, n, t + 1)
                root(2, n, t)
                pool.wait_ge(z_done, n * TPG + t + 1 + CREDIT)
                pool.wait_ge(out_stored[t % 2], (n * 2 + t // 2) * 16 + CREDIT * 2)
                pool.tensor_tensor(out_sb[t % 2][:], z_sb[t % 2][:], x1[t % 2][:], ALU.add
                                   ).then_inc(out_done, 1)

            loop_tiles(pool, body)

        @block.scalar
        def _(act):
            act.sem_inc(x2_moved, CREDIT)
            act.sem_inc(hwt_done, CREDIT)

            def affine(k, src, dst, n, t, done):
                n, i = n + t // TPG, t % 2
                act.wait_ge(shift_done[k], n * TPG + t % TPG + 1)
                act.activation(dst[i][:], src[i][:], ACT.Identity, bias=shift[k][i][:],
                               scale=rstd[k][i][:]).then_inc(done, 1)

            affine(0, a_sb, y_sb, 0, 0, y_done)

            def body(n, t, rest):
                i = t % 2
                for half_ in range(2):
                    act.wait_ge(x2_turned, (n * TPG + t) * 2 + half_ + 1)
                    act.activation(x2_t[i][:, half_ * 4:half_ * 4 + 4, :],
                                   ps_x[half_][:].rearrange("p (k s) -> p k s", k=4), ACT.Copy
                                   ).then_inc(x2_moved, 1)
                act.wait_ge(gap_done, n * TPG + t + 1)
                act.activation(expo[i][:], gap[i][:], ACT.Exp).then_inc(expo_done, 1)
                act.wait_ge(hwt_turned, n * TPG + t + 1)
                act.activation(hw_t[i][:], ps_h[:, 0:P], ACT.Copy).then_inc(hwt_done, 1)
                if rest >= 1:
                    affine(0, a_sb, y_sb, n, t + 1, y_done)
                act.wait_ge(out_done, n * TPG + t - 1 + CREDIT)
                affine(2, f_sb, z_sb, n, t, z_done)

            loop_tiles(act, body)

        @block.vector
        def _(dve):
            dve.sem_inc(a_done, CREDIT)
            dve.sem_inc(f_done, CREDIT)
            dve.sem_inc(out_done, CREDIT)
            count = [0]

            def link(ins, n):
                ins.then_inc(chain if n is not None else chain_first, 1)
                count[0] += 1
                if n is None:
                    dve.wait_ge(chain_first, count[0])
                else:
                    dve.wait_ge(chain, n * LINKS_PER_BODY + count[0])

            def norm_stats(k, src, i, n):
                dve.bn_stats(stats[k][i][:, 0, :], src[:, 0:512])
                link(dve.bn_stats(stats[k][i][:, 1, :], src[:, 512:1024]), n)
                dve.sem_inc(passed, 1)
                link(dve.bn_aggr(mean_var[k][i][:], stats[k][i][:].rearrange("p a b -> p (a b)")), n)
                dve.tensor_scalar(var_eps[k][i][:], mean_var[k][i][:, 1:2], EPS, None, ALU.add
                                  ).then_inc(eps_done[k], 1)

            def norm_shift(k, i, tile):
                dve.wait_ge(rstd_done[k], tile + 1)
                dve.scalar_tensor_tensor(shift[k][i][:], mean_var[k][i][:, 0:1], -1.0, rstd[k][i][:],
                                         op0=ALU.mult, op1=ALU.mult).then_inc(shift_done[k], 1)

            def divide(n, t):
                n, t = n + t // TPG, t % TPG
                i = t % 2
                dve.wait_ge(o_loaded[i], (n * 2 + t // 2 + 1) * 16)
                dve.wait_ge(inv_loaded[i], (n * 2 + t // 2 + 1) * 64)
                dve.tensor_tensor(ctx_t[i][:], ctx_t[i][:], inv[i][:], ALU.mult).then_inc(ctx_done, 1)

            def evacuate_dense(n, t):
                n, t = n + t // TPG, t % TPG
                dve.wait_ge(dense_done, n * TPG + t + 1)
                dve.tensor_tensor(a_sb[t % 2][:], ps_d[:], bd[:], ALU.add).then_inc(a_done, 1)

            def attention_norms(n, t, links):
                n, t = n + t // TPG, t % TPG
                i, tile = t % 2, n * TPG + t
                dve.wait_ge(a_done, tile + 1 + CREDIT)
                norm_stats(0, a_sb[i], i, links)
                norm_shift(0, i, tile)
                dve.wait_ge(y_done, tile + 1)
                dve.wait_ge(x_loaded[i], (n * 2 + t // 2 + 1) * 16)
                dve.wait_ge(out_done, tile - 1 + CREDIT)
                dve.tensor_tensor(x1[i][:], y_sb[i][:], xt[i][:], ALU.add).then_inc(x1_done, 1)
                dve.wait_ge(x1_done, tile + 1)
                norm_stats(1, x1[i], i, links)
                dve.wait_ge(rstd_done[1], tile + 1)
                dve.tensor_scalar(xn2[i][:], x1[i][:], mean_var[1][i][:, 0:1], rstd[1][i][:],
                                  ALU.subtract, ALU.mult).then_inc(xn2_done, 1)

            def router(n, t):
                i = t % 2
                dve.wait_ge(ra_done, n * TPG + t + 1)
                link(dve.tensor_copy(logits[i][:], ps_ra[:, 0:EXPERTS]), n)
                dve.sem_inc(passed, 1)
                link(dve.max(top[i][:], logits[i][:]), n)

                def one_hot(dst, values, value):
                    link(dve.scalar_tensor_tensor(score[i][:], values, value, rev[:],
                                                  op0=ALU.is_equal, op1=ALU.mult), n)
                    link(dve.reduce_max(best[i][:], score[i][:], AX.X), n)
                    link(dve.tensor_scalar(dst[i][:], score[i][:], best[i][:], None, ALU.is_equal), n)

                one_hot(first, logits[i][:], top[i][:, 0:1])
                link(dve.scalar_tensor_tensor(logits[i][:], first[i][:], -3.0e38, logits[i][:],
                                              op0=ALU.mult, op1=ALU.add), n)
                one_hot(second, logits[i][:], top[i][:, 1:2])
                dve.tensor_tensor(gap[i][:], top[i][:, 1:2], top[i][:, 0:1], ALU.subtract
                                  ).then_inc(gap_done, 1)
                dve.wait_ge(expo_done, n * TPG + t + 1)
                link(dve.tensor_scalar(half[i][:], expo[i][:], 1.0, 0.5, ALU.add, ALU.mult), n)
                link(dve.reciprocal(w1[i][:], half[i][:]), n)
                link(dve.tensor_tensor(w2[i][:], w1[i][:], expo[i][:], ALU.mult), n)
                link(dve.tensor_scalar(comb[i][:], first[i][:], w1[i][:], None, ALU.mult), n)
                link(dve.scalar_tensor_tensor(comb[i][:], second[i][:], w2[i][:], comb[i][:],
                                              op0=ALU.mult, op1=ALU.add), n)
                dve.tensor_tensor(hw[i][:].rearrange("p (e r) -> p e r", r=RANK),
                                  ps_ra[:, EXPERTS:EXPERTS + ER].rearrange("p (e r) -> p e r", r=RANK),
                                  comb[i][:].unsqueeze(2).to_broadcast([P, EXPERTS, RANK]),
                                  ALU.mult).then_inc(hw_done, 1)

            def ffn_norm(n, t):
                i, tile = t % 2, n * TPG + t
                dve.wait_ge(ffn_done, tile + 1)
                dve.wait_ge(z_done, tile - 1 + CREDIT)
                dve.tensor_tensor(f_sb[i][:], ps_f[:], bb[:], ALU.add).then_inc(f_done, 1)
                dve.wait_ge(f_done, tile + 1 + CREDIT)
                norm_stats(2, f_sb[i], i, n)
                norm_shift(2, i, tile)

            LINKS_PER_BODY = TPG * (3 * 2 + 14)
            dve.sem_inc(z_done, CREDIT)
            dve.wait_ge(sums_in, 16)
            dve.reciprocal(inv[1][:], inv[0][:]).then_inc(sums_inv, 1)
            dve.wait_ge(consts_in, 64)
            divide(0, 0)
            divide(0, 1)
            evacuate_dense(0, 0)
            attention_norms(0, 0, None)

            def body(n, t, rest):
                if t == 0:
                    count[0] = 0
                router(n, t)
                if rest >= 1:
                    evacuate_dense(n, t + 1)
                if rest >= 2:
                    divide(n, t + 2)
                if rest >= 1:
                    attention_norms(n, t + 1, n)
                ffn_norm(n, t)
                assert t < TPG - 1 or rest == 0 or count[0] == LINKS_PER_BODY, count

            loop_tiles(dve, body)

        @block.tensor
        def _(pe):
            def dense(n, t):
                n, t = n + t // TPG, t % TPG
                i, tile = t % 2, n * TPG + t
                pe.wait_ge(ctx_done, tile + 1)
                pe.wait_ge(a_done, tile + CREDIT)
                for half_ in range(2):
                    for k in range(KC):
                        mm = pe.matmul(ps_d[:, half_ * 512:(half_ + 1) * 512], ctx_t[i][:, k, :],
                                       w_dense[:, k, half_ * 512:(half_ + 1) * 512],
                                       start=(k == 0), stop=(k == KC - 1))
                mm.then_inc(dense_done, 1)

            pe.wait_ge(consts_in, 64)
            dense(0, 0)

            def body(n, t, rest):
                i, tile = t % 2, n * TPG + t
                if rest >= 1:
                    dense(n, t + 1)
                pe.wait_ge(xn2_done, tile + 1)
                for half_ in range(2):
                    pe.wait_ge(x2_moved, (tile - 1) * 2 + half_ + 1 + CREDIT)
                    for c in range(4):
                        k = half_ * 4 + c
                        mm = pe.transpose(ps_x[half_][:, c * P:(c + 1) * P],
                                          xn2[i][:, k * P:(k + 1) * P], idn[:])
                    mm.then_inc(x2_turned, 1)
                pe.wait_ge(x2_moved, tile * 2 + 2 + CREDIT)
                for k in range(KC):
                    mm = pe.matmul(ps_ra[:, 0:EXPERTS + ER], x2_t[i][:, k, :], w_ra[:, k, :],
                                   start=(k == 0), stop=(k == KC - 1))
                mm.then_inc(ra_done, 1)
                pe.wait_ge(f_done, tile + CREDIT)
                for half_ in range(2):
                    for k in range(KC):
                        pe.matmul(ps_f[:, half_ * 512:(half_ + 1) * 512], x2_t[i][:, k, :],
                                  w_base[:, k, half_ * 512:(half_ + 1) * 512],
                                  start=(k == 0), stop=False)
                pe.wait_ge(hw_done, tile + 1)
                pe.transpose(ps_h[:, 0:P], hw[i][:], idn[:]).then_inc(hwt_turned, 1)
                pe.wait_ge(hwt_done, tile + 1 + CREDIT)
                for half_ in range(2):
                    mm = pe.matmul(ps_f[:, half_ * 512:(half_ + 1) * 512], hw_t[i][:],
                                   b_lora[:, half_ * 512:(half_ + 1) * 512], start=False, stop=True)
                mm.then_inc(ffn_done, 1)

            loop_tiles(pe, body)


def build(nc, x, w_qk, b_qk, w_v, b_v, w_dense, b_dense, w_base, b_base, w_ra, b_lora, rope, ident,
          masks, rev_index, out):
    kept = lambda name, shape, dt: nc.dram_tensor(name, shape, dt, kind="Internal").ap()
    q_hi, q_lo = (kept(f"q_{k}", [NTG * GROUPS, QPG * HD, TG], F32R) for k in ("hi", "lo"))
    k_hi, k_lo = (kept(f"k_{k}", [NTG * GROUPS, HD, TG], F32R) for k in ("hi", "lo"))
    v_all = kept("v_all", [BATCH * SEQ, GROUPS * HD], F32)
    o_all = kept("o_all", [NTG * GROUPS, QPG * HD, TG], F32)
    sums = kept("sums", [NTG * GROUPS, QPG, TG], F32)
    inv_sums = kept("inv_sums", [NTG * GROUPS, QPG, TG], F32)
    k_tiles = [k.rearrange("(a g) d s -> a (g d) s", g=P // HD) for k in (k_hi, k_lo)]

    project(nc, x, w_qk, b_qk, w_v, b_v, rope, ident, q_hi, q_lo, k_tiles[0], k_tiles[1], v_all)
    with ExitStack() as ctx:
        sb = lambda name, shape: ctx.enter_context(nc.sbuf_tensor(name, shape, F32))
        wd, wb = sb("wd", [P, KC, HID]), sb("wb", [P, KC, HID])
        wra, bl = sb("wra", [P, KC, EXPERTS + ER]), sb("bl", [P, HID])
        loads = []
        for dst, src in ((wd, w_dense), (wb, w_base), (wra, w_ra)):
            loads += [(dst[:, k, :], src[k * P:(k + 1) * P, :]) for k in range(KC)]
        loads.append((bl[:], b_lora))
        attend(nc, masks, ident, q_hi, q_lo, k_hi, k_lo, v_all, o_all, sums, loads)
        finish(nc, (wd, wb, wra, bl), x, b_dense, b_base, rev_index, ident, o_all, sums, inv_sums, out)


def rope_table():
    half = np.arange(0, HD, 2, dtype=np.float32) / np.float32(HD)
    inv_freq = (np.float32(1.0) / np.power(np.float32(1000000.0), half)).astype(np.float32)
    freqs = np.outer(np.arange(SEQ, dtype=np.float32), inv_freq).astype(np.float32)
    emb = np.concatenate([freqs, freqs], axis=-1).astype(np.float64)
    cos, sin = np.cos(emb), np.sin(emb)
    sin[:, :HD // 2] *= -1.0
    table = np.stack([np.tile(cos.T, (P // HD, 1)), np.tile(sin.T, (P // HD, 1))], axis=1)
    table = table.reshape(P, 2, UPB, TG).transpose(2, 0, 1, 3)
    return np.ascontiguousarray(np.tile(table, (BATCH, 1, 1, 1)).astype(np.float32))


def kernel(L0_attn_hidden_states, L0_attn_w_qkv, L0_attn_b_qkv, L0_attn_w_dense, L0_attn_b_dense,
           L0_ffn_W_base, L0_ffn_b_base, L0_ffn_W_router, L0_ffn_A, L0_ffn_B):
    import concourse.bacc as bacc
    from concourse.bass_utils import run_bass_kernel_spmd

    arr = np.asarray
    w = arr(L0_attn_w_qkv).reshape(GROUPS, QPG + 2, HD, HID)
    b = arr(L0_attn_b_qkv).reshape(GROUPS, QPG + 2, HD)
    w_qk = np.concatenate([w[:, :QPG].reshape(-1, HID), w[:, QPG].reshape(-1, HID)]).T
    b_qk = np.concatenate([b[:, :QPG].reshape(-1), b[:, QPG].reshape(-1)]).reshape(QK_TILES, P).T
    lora_a = arr(L0_ffn_A).reshape(ER, HID)
    masks = np.zeros((P, P + BLOCK), np.float32)
    masks[:, :P][np.triu_indices(P, 1)] = NEG
    masks[P // 2:, P:] = NEG
    given = {
        "x": arr(L0_attn_hidden_states).reshape(BATCH * SEQ, HID),
        "w_qk": w_qk,
        "b_qk": b_qk,
        "w_v": w[:, QPG + 1].reshape(-1, HID).T,
        "b_v": b[:, QPG + 1].reshape(-1),
        "w_dense": arr(L0_attn_w_dense).T,
        "b_dense": arr(L0_attn_b_dense),
        "w_base": arr(L0_ffn_W_base).T,
        "b_base": arr(L0_ffn_b_base),
        "w_ra": np.concatenate([arr(L0_ffn_W_router), lora_a]).T,
        "b_lora": arr(L0_ffn_B).transpose(0, 2, 1).reshape(ER, HID),
        "rope": rope_table(),
        "ident": np.eye(P, dtype=np.float32),
        "masks": masks,
        "rev_index": np.arange(EXPERTS, 0, -1).astype(np.float32),
    }
    given = {k: np.ascontiguousarray(v) for k, v in given.items()}
    nc = bacc.Bacc("TRN2", target_bir_lowering=False, num_devices=1)
    aps = [nc.dram_tensor(f"{k}_dram", v.shape, F32, kind="ExternalInput").ap() for k, v in given.items()]
    out = nc.dram_tensor("out_dram", [BATCH * SEQ, HID], F32, kind="ExternalOutput").ap()
    build(nc, *aps, out)
    result = run_bass_kernel_spmd(nc, [{f"{k}_dram": v for k, v in given.items()}], core_ids=[0])
    return result.results[0]["out_dram"].reshape(BATCH, SEQ, HID)
```

```python
from contextlib import ExitStack

import numpy as np

import concourse.bass as bass
from concourse import mybir

F32 = mybir.dt.float32
F32R = mybir.dt.float32r
BF16 = mybir.dt.bfloat16
ALU = mybir.AluOpType
ACT = mybir.ActivationFunctionType
AX = mybir.AxisListType

P = 128
BATCH, SEQ, HID = 2, 2048, 1024
HEADS, GROUPS = 32, 8
HD = HID // HEADS
QPG = HEADS // GROUPS
EXPERTS, RANK = 8, 16
ER = EXPERTS * RANK
KC = HID // P
TG = 512
NTG = BATCH * SEQ // TG
TPG = TG // P
UPB = SEQ // TG
QK_TILES = GROUPS + GROUPS * HD // P
BLOCK, LOCAL, VERT = 64, 16, 8
BPT = P // BLOCK
LT = LOCAL // BPT
RA = EXPERTS + ER
HALF_COLS = 388
HEAD_COLS = 2 * HALF_COLS
RA_COLS = RA + HID - HEAD_COLS
WA = RA + HID
EPS = 1e-5
SM_SCALE = 1.0 / HD
NEG = -1.0e30
CREDIT = 16


def max_segments(tile):
    end = (tile + 1) * P
    if tile < LT:
        start, pieces = 0, []
        while end - start > 0:
            width = (end - start) % 512 or 512
            pieces.append((start, width))
            start += width
        return pieces
    start = (tile - LT) * P + BLOCK
    return [(start, BLOCK)] + [(start + BLOCK + i * 512, 512) for i in range(2)]


def has_vertical(tile):
    return tile > (VERT - 1) // BPT + LT


def edge_is_vertical(tile):
    return (BPT * (tile - LT) + 2) % VERT == 0


def steps_of(unit):
    first = unit * TPG
    last = first + TPG - 1
    steps = []
    for key in range(0, last + 1):
        lo = max(key, first)
        full = min(key + LT - 1, last)
        start = (lo - first) * P
        mid = max(full - first + 1, 0) * P if full >= lo else start
        end = mid
        if first <= key + LT <= last:
            end = mid + (P if edge_is_vertical(key + LT) else BLOCK)
        if (BPT * key + 2) % VERT == 0 and has_vertical(last) and key + LT < last:
            end = TG
        if end > start:
            steps.append((key, start, mid, end))
    steps.sort(key=lambda s: (s[0] != first, s[0]))
    assert steps[0][1] == 0 and steps[0][2] == TG
    return steps


def bank_width(tile, seg):
    width = max_segments(tile)[seg][1]
    return width + BLOCK if seg == 0 and has_vertical(tile) else width


SLOTS = 6


def interleave(steps, chunks):
    LEAD, MARGIN, FIXED_STEP, FIXED_CHUNK = 0.44, 0.017, 150, 60
    places, now = [], 0
    for u in range(UPB):
        for s, (_, start, _, end) in enumerate(steps[u]):
            span = end - start + FIXED_STEP
            places += [(now + span * slot / SLOTS, u, s, slot) for slot in range(SLOTS)]
            now += span
    cost = [bank_width(u * TPG + tl, seg) + FIXED_CHUNK for u in range(UPB) for tl, _, seg in chunks[u]]
    order = [(u, c) for u in range(UPB) for c in range(len(chunks[u]))]
    slots = [[[[] for _ in range(SLOTS)] for _ in steps[u]] for u in range(UPB)]
    rows = [{} for _ in range(UPB)]
    both = [(time - now, u, s, slot, True) for time, u, s, slot in places] + [(*p, False) for p in places]
    first, spent, at = [], 0, -1
    taken = []

    for (u, c), width in zip(order, cost):
        time = (spent / sum(cost) - LEAD) * now
        spent += width
        at = next(i for i, p in enumerate(both) if i > at and p[0] >= time and i not in taken)
        _, pu, ps, slot, wrap = both[at]
        slots[pu][ps][slot].append((u + (UPB if wrap else 0), c))
        if c == len(chunks[u]) - 1:
            row = next(i for i, p in enumerate(both) if p[0] >= both[at][0] + MARGIN * now
                       and p[3] == 0 and p[2] + 1 < len(steps[p[1]]))
            taken += [row, row + 1]
            _, pu, ps, _, row_wrap = both[row]
            assert ps not in rows[pu]
            rows[pu][ps] = u + (UPB if row_wrap else 0)
        if wrap:
            first.append(("chunk", u, c))
    base = [sum(len(c) for c in chunks[:u]) for u in range(UPB)]
    base += [base[u] + sum(len(c) for c in chunks) for u in range(UPB)]
    for u in range(UPB):
        for s in rows[u]:
            later = [x for pu in range(u, UPB) for ps in range(s if pu == u else 0, len(steps[pu]))
                     for sl in slots[pu][ps] for x in sl]
            later = later or [(x[0] + UPB, x[1]) for x in slots[0][0][0]]
            unit, c = later[0]
            rows[u][s] = (rows[u][s], base[unit] + c)
    turned = sorted((r[0] - UPB, r[1] - base[UPB]) for row in rows for r in row.values() if r[0] >= UPB)
    for unit, count in reversed(turned):
        at = [i for i, e in enumerate(first) if e[0] == "chunk" and base[e[1]] + e[2] == count]
        first.insert(at[0] if at else len(first), ("row", unit, count))
    return slots, rows, first


def project(nc, x, w_qk, b_qk, w_v, b_v, rope, ident, q_hi, q_lo, k_hi, k_lo, v_out):
    with ExitStack() as ctx:
        sb = lambda name, shape, dt=F32: ctx.enter_context(nc.sbuf_tensor(name, shape, dt))
        ps = lambda name: ctx.enter_context(nc.psum_tensor(name, [P, 512], F32))
        sem = lambda name: ctx.enter_context(nc.semaphore(name))

        wqk_hi, wqk_lo = (sb(f"wqk_{k}", [P, KC, QK_TILES * P], F32R) for k in ("hi", "lo"))
        wv_hi, wv_lo = (sb(f"wv_{k}", [P, KC, GROUPS * HD], F32R) for k in ("hi", "lo"))
        bqk = sb("bqk", [P, QK_TILES])
        bv = sb("bv", [P, GROUPS * HD])
        idn = sb("idn_p", [P, P])
        xin = sb("xin", [P, TPG, HID])
        stats = sb("stats_p", [P, TPG, 2, 6])
        per_tile = sb("per_tile_p", [P, 5, TPG])
        mean_var = per_tile[:, 0:2, :].rearrange("p a t -> p (a t)").rearrange("p (t a) -> p t a", a=2)
        var_eps, minus_half, rstd = (per_tile[:, i, :] for i in (2, 3, 4))
        cos_sin = [sb(f"cos_sin{i}", [P, 2, TG]) for i in range(2)]
        raw = [sb(f"raw{i}", [P, TG]) for i in range(2)]
        swapped = [sb(f"swapped{i}", [P, TG]) for i in range(2)]
        with_cos = [sb(f"with_cos{i}", [P, TG]) for i in range(2)]
        hi = [sb(f"hi{i}", [P, TG], F32R) for i in range(2)]
        lo = [sb(f"lo{i}", [P, TG], F32R) for i in range(2)]
        v_sb = [sb(f"v_sb{i}", [P, GROUPS * HD]) for i in range(2)]
        ps_t = [ps(f"ps_t{i}") for i in range(2)]
        ps_qk = [ps(f"ps_qk{i}") for i in range(4)]
        ps_v = [ps(f"ps_v{i}") for i in range(2)]

        passed = sem("passed_p")
        weights_in = [sem(f"weights_in{i}") for i in range(QK_TILES // 2 + 1)]
        ident_in = sem("ident_in")
        consts_in = sem("consts_in")
        pool_split = sem("pool_split")
        dve_split = sem("dve_split")
        w_hi_done = sem("w_hi_done")
        x_in = [sem(f"x_in{t}") for t in range(TPG)]
        rope_in = [sem(f"rope_in{i}") for i in range(2)]
        stats_done = sem("stats_done")
        aggr_done = sem("aggr_done")
        eps_done = sem("eps_done")
        rstd_done = sem("rstd_done")
        xn_done = sem("xn_done")
        tr_done = sem("tr_done")
        xt_hi_done = sem("xt_hi_done")
        xt_done = sem("xt_done")
        qk_done = sem("qk_done")
        raw_done = sem("raw_done")
        swap_done = sem("swap_done")
        cos_done = sem("cos_done")
        sin_done = sem("sin_done")
        turned_done = sem("turned_done")
        hi_done = sem("hi_done")
        lo_done = sem("lo_done")
        vps_done = sem("vps_done")
        v_done = sem("v_done")
        qk_stored = [sem(f"qk_stored{i}") for i in range(2)]
        v_stored = [sem(f"v_stored{i}") for i in range(2)]

        def x_tile(n, t):
            return x[bass.ds((n * TPG + t) * P, P), :]

        def table_loads(n, j):
            return (n - j) * 8 + 16

        NORM_AT = [1, 3, 5, 7]
        LOW_AT = [3, 5, 7, 9]
        MOVE_AT = [2, 4, 6, 8]
        V_AT = [3, 6, 9, 9]
        V_OUT = [5, 8, 10, 11]
        V_STORE = [3, 6, 8, 9]
        LAST = NTG - 1
        V_BLOCK, POOL_SPLITS, DVE_SPLITS = 2, (0, 3), (1, 2, 4, 5)

        def loop_groups(eng, body):
            with eng.Fori(0, NTG // 2 - 1) as i:
                for j in range(2):
                    body(i * 2 + j, j, False)
            for j in range(2):
                body(NTG - 2 + j, j, j == 1)

        def group_stats(dve, n):
            for t in range(TPG):
                dve.wait_ge(x_in[t], (n + 1) * 16)
                for half in range(2):
                    last = dve.bn_stats(stats[:, t, half, :], xin[:, t, half * 512:(half + 1) * 512])
                last.then_inc(stats_done, 1)
            for t in range(TPG):
                dve.wait_ge(stats_done, n * TPG + t + 1)
                dve.sem_inc(passed, 1)
                last = dve.bn_aggr(mean_var[:, t, :], stats[:, t].rearrange("p a b -> p (a b)"))
            last.then_inc(aggr_done, 1)
            dve.wait_ge(aggr_done, n + 1)
            dve.tensor_scalar(var_eps, mean_var[:, :, 1], EPS, None, ALU.add).then_inc(eps_done, 1)

        def normalise(dve, n, t):
            if t == 0:
                dve.wait_ge(rstd_done, n + 2)
            dve.tensor_scalar(xin[:, t, :], xin[:, t, :], mean_var[:, t, 0:1], rstd[:, t:t + 1],
                              ALU.subtract, ALU.mult).then_inc(xn_done, 1)

        def group_rstd(pool, n):
            pool.wait_ge(eps_done, n + 1)
            if isinstance(n, int) and n == 0:
                pool.wait_ge(rstd_done, 1)
            pool.tensor_tensor(rstd, var_eps, minus_half, ALU.pow).then_inc(rstd_done, 1)

        wide = 2 * P
        blocks = [(w_qk[:, i * wide:(i + 1) * wide], wqk_hi[:, :, i * wide:(i + 1) * wide],
                   wqk_lo[:, :, i * wide:(i + 1) * wide]) for i in range(QK_TILES // 2)]
        assert GROUPS * HD == wide
        blocks.insert(V_BLOCK, (w_v, wv_hi[:], wv_lo[:]))
        with nc.sbuf_tensor("w_staged", [P, KC, 4 * wide], F32) as staged:
            stage = [staged[:, :, i % 4 * wide:(i % 4 + 1) * wide] for i in range(len(blocks))]
        xt_hi, xt_lo = ([sb(f"xt_{k}1", [P, KC, TG], F32R)] for k in ("hi", "lo"))
        xt_hi.insert(0, sb("xt_hi0", [P, KC, TG], F32R))
        xt_lo.insert(0, sb("xt_lo0", [P, KC, TG], F32R))

        def split_done(eng, i):
            if i in POOL_SPLITS:
                eng.wait_ge(pool_split, POOL_SPLITS.index(i) + 1)
            else:
                eng.wait_ge(dve_split, DVE_SPLITS.index(i) + 1)

        def staging_free(eng):
            eng.wait_ge(pool_split, len(POOL_SPLITS))
            eng.wait_ge(dve_split, len(DVE_SPLITS))

        def split_low(eng, i, done):
            eng.wait_ge(w_hi_done, i + 1)
            eng.tensor_tensor(blocks[i][2], stage[i], blocks[i][1].bitcast(F32), ALU.subtract).then_inc(done, 1)

        block = ctx.enter_context(nc.Block())

        @block.sync
        def _(sp):
            for i in range(2):
                sp.sem_inc(qk_stored[i], CREDIT * 4)
                sp.sem_inc(v_stored[i], CREDIT)
            sp.dma_start(idn[:], ident).then_inc(ident_in, 16)
            for t in range(TPG):
                sp.dma_start(xin[:, t, :], x_tile(0, t)).then_inc(x_in[t], 16)

            def stage_block(i):
                sp.dma_start(stage[i], blocks[i][0].rearrange("(k p) n -> p k n", p=P)
                             ).then_inc(weights_in[i], 16)

            for i in range(4):
                stage_block(i)
            sp.dma_start(bqk[:], b_qk).then_inc(consts_in, 16)
            sp.dma_start(bv[:], b_v.partition_broadcast(P)).then_inc(consts_in, 16)
            sp.dma_start(cos_sin[0][:], rope[0]).then_inc(rope_in[0], 16)
            for i in range(4, len(blocks)):
                split_done(sp, i - 4)
                stage_block(i)
            for t in range(TPG):
                sp.wait_ge(tr_done, (t + 1) * 2)
                sp.dma_start(xin[:, t, :], x_tile(1, t)).then_inc(x_in[t], 16)

            def body(n, j, last):
                if not last:
                    sp.dma_start(cos_sin[1 - j][:], rope[bass.ds(n + 1, 1)].rearrange("o p a s -> (o p) a s")
                                 ).then_inc(rope_in[1 - j], 16)
                for r in range(QK_TILES):
                    m = n * QK_TILES + r
                    sp.wait_ge(lo_done, m + 1 + CREDIT)
                    for part, (dq, dk) in ((hi, (q_hi, k_hi)), (lo, (q_lo, k_lo))):
                        if r < GROUPS:
                            dst = dq[bass.ds(n * GROUPS + r, 1)].rearrange("o p s -> (o p) s")
                        else:
                            dst = dk[bass.ds(n * 2 + (r - GROUPS), 1)].rearrange("o p s -> (o p) s")
                        sp.dma_start(dst.bitcast(F32), part[r % 2][:].bitcast(F32)
                                     ).then_inc(qk_stored[r % 2], 16)
                    if r in MOVE_AT and not last and not (isinstance(n, int) and n + 2 > LAST):
                        t = MOVE_AT.index(r)
                        sp.wait_ge(tr_done, ((n + 1) * TPG + t + 1) * 2)
                        sp.dma_start(xin[:, t, :], x_tile(n + 2, t)).then_inc(x_in[t], 16)
                    for t in (t for t in range(TPG) if V_STORE[t] == r):
                        sp.wait_ge(v_done, n * TPG + t + 1 + CREDIT)
                        sp.dma_start(v_out[bass.ds((n * TPG + t) * P, P), :], v_sb[t % 2][:]
                                     ).then_inc(v_stored[t % 2], 16)

            loop_groups(sp, body)
            for i in range(2):
                sp.wait_ge(qk_stored[i], CREDIT * 4 + NTG * QK_TILES * 16)
                sp.wait_ge(v_stored[i], CREDIT + NTG * TPG // 2 * 16)

        @block.gpsimd
        def _(pool):
            pool.sem_inc(sin_done, CREDIT)
            pool.memset(minus_half, -0.5).then_inc(rstd_done, 1)
            group_rstd(pool, 0)
            for i in POOL_SPLITS:
                split_low(pool, i, pool_split)
            def body(n, j, last):
                pool.wait_ge(rope_in[j], table_loads(n, j))
                if not last:
                    group_rstd(pool, n + 1)
                for r in range(QK_TILES):
                    m = n * QK_TILES + r
                    pool.wait_ge(swap_done, m + 1)
                    pool.tensor_tensor(swapped[r % 2][:], swapped[r % 2][:], cos_sin[j][:, 1, :],
                                       ALU.mult).then_inc(sin_done, 1)

            loop_groups(pool, body)

        @block.scalar
        def _(act):
            act.sem_inc(raw_done, CREDIT)

            def move(n, t, buf):
                for half in range(2):
                    act.wait_ge(tr_done, (n * TPG + t) * 2 + half + 1)
                    act.activation(xt_hi[buf][:, half * 4:half * 4 + 4, t * P:(t + 1) * P],
                                   ps_t[half][:].rearrange("p (k s) -> p k s", k=4),
                                   ACT.Copy).then_inc(xt_hi_done, 1)

            def split_high(i):
                act.wait_ge(weights_in[i], 16)
                act.activation(blocks[i][1], stage[i], ACT.Copy).then_inc(w_hi_done, 1)

            split_high(0)
            for t in range(TPG):
                move(0, t, 0)
            for i in range(1, len(blocks)):
                split_high(i)
            act.wait_ge(consts_in, 32)
            def body(n, j, last):
                def split_hi(r):
                    m = n * QK_TILES + r
                    act.wait_ge(turned_done, m + 1 + CREDIT)
                    act.wait_ge(qk_stored[r % 2], (n * (QK_TILES // 2) + r // 2) * 32 + CREDIT * 4)
                    act.activation(hi[r % 2][:], with_cos[r % 2][:], ACT.Copy,
                                   scale=SM_SCALE if r < GROUPS else 1.0).then_inc(hi_done, 1)

                for r in range(QK_TILES + 2):
                    if r < QK_TILES:
                        m = n * QK_TILES + r
                        act.wait_ge(qk_done, m + 1)
                        act.wait_ge(cos_done, m - 1 + CREDIT)
                        act.activation(raw[r % 2][:], ps_qk[(j * QK_TILES + r) % 4][:], ACT.Identity,
                                       bias=bqk[:, r:r + 1]).then_inc(raw_done, 1)
                    if r >= 2:
                        split_hi(r - 2)
                    if r in MOVE_AT and not last:
                        if r == MOVE_AT[0] and j == 0:
                            staging_free(act)
                        move(n + 1, MOVE_AT.index(r), 1 - j)

            loop_groups(act, body)

        @block.vector
        def _(dve):
            dve.sem_inc(turned_done, CREDIT)
            dve.sem_inc(lo_done, CREDIT)
            dve.sem_inc(cos_done, CREDIT)
            dve.sem_inc(v_done, CREDIT)
            dve.sem_inc(xt_done, CREDIT)

            def xt_low(n, t, buf):
                for half in range(2):
                    dve.wait_ge(xt_hi_done, (n * TPG + t) * 2 + half + 1)
                    at = (slice(None), slice(half * 4, half * 4 + 4), slice(t * P, (t + 1) * P))
                    dve.tensor_tensor(xt_lo[buf][at], ps_t[half][:].rearrange("p (k s) -> p k s", k=4),
                                      xt_hi[buf][at].bitcast(F32), ALU.subtract).then_inc(xt_done, 1)

            group_stats(dve, 0)
            for t in range(TPG):
                normalise(dve, 0, t)
            for t in range(TPG):
                xt_low(0, t, 0)
            for i in DVE_SPLITS:
                split_low(dve, i, dve_split)
            dve.wait_ge(consts_in, 32)
            dve.wait_ge(pool_split, len(POOL_SPLITS))

            def body(n, j, last):
                dve.wait_ge(rope_in[j], table_loads(n, j))
                if not last:
                    group_stats(dve, n + 1)
                for r in range(QK_TILES + 2):
                    if r < QK_TILES:
                        m = n * QK_TILES + r
                        dve.wait_ge(raw_done, m + 1 + CREDIT)
                        dve.wait_ge(turned_done, m - 1 + CREDIT)
                        dve.sem_inc(passed, 1)
                        dve.stream_shuffle(swapped[r % 2][:], raw[r % 2][:],
                                           [(i + HD // 2) % HD for i in range(HD)]).then_inc(swap_done, 1)
                    if r >= 2:
                        q = r - 2
                        dve.wait_ge(hi_done, n * QK_TILES + q + 1)
                        dve.wait_ge(qk_stored[q % 2], (n * (QK_TILES // 2) + q // 2) * 32 + CREDIT * 4)
                        dve.scalar_tensor_tensor(lo[q % 2][:], with_cos[q % 2][:],
                                                 SM_SCALE if q < GROUPS else 1.0,
                                                 hi[q % 2][:].bitcast(F32), op0=ALU.mult,
                                                 op1=ALU.subtract).then_inc(lo_done, 1)
                    if r < QK_TILES:
                        m = n * QK_TILES + r
                        dve.wait_ge(lo_done, m - 1 + CREDIT)
                        dve.tensor_tensor(with_cos[r % 2][:], raw[r % 2][:], cos_sin[j][:, 0, :],
                                          ALU.mult).then_inc(cos_done, 1)
                    if 1 <= r <= QK_TILES:
                        m = n * QK_TILES + r - 1
                        dve.wait_ge(cos_done, m + 1 + CREDIT)
                        dve.wait_ge(sin_done, m + 1 + CREDIT)
                        dve.tensor_tensor(with_cos[(r - 1) % 2][:], with_cos[(r - 1) % 2][:],
                                          swapped[(r - 1) % 2][:], ALU.add).then_inc(turned_done, 1)
                    if r in LOW_AT and not last:
                        xt_low(n + 1, LOW_AT.index(r), 1 - j)
                    if r in NORM_AT and not last:
                        normalise(dve, n + 1, NORM_AT.index(r))
                    if r in V_OUT:
                        t = V_OUT.index(r)
                        dve.wait_ge(vps_done, n * TPG + t + 1)
                        dve.wait_ge(v_stored[t % 2], (n * 2 + t // 2) * 16 + CREDIT)
                        dve.tensor_tensor(v_sb[t % 2][:], ps_v[t % 2][:, 0:GROUPS * HD], bv[:],
                                          ALU.add).then_inc(v_done, 1)

            loop_groups(dve, body)

        @block.tensor
        def _(pe):
            def transposes(n, t):
                pe.wait_ge(xn_done, n * TPG + t + 1)
                for half in range(2):
                    pe.wait_ge(xt_done, (n * TPG + t - 1) * 2 + half + 1 + CREDIT)
                    for c in range(4):
                        k = half * 4 + c
                        last = pe.transpose(ps_t[half][:, c * P:(c + 1) * P],
                                            xin[:, t, k * P:(k + 1) * P], idn[:])
                    last.then_inc(tr_done, 1)

            pe.wait_ge(ident_in, 16)
            for t in range(TPG):
                transposes(0, t)

            def body(n, j, last):
                pe.wait_ge(xt_done, (n + 1) * TPG * 2 + CREDIT)
                for r in range(QK_TILES):
                    m = n * QK_TILES + r
                    if r % 2 == 0:
                        split_done(pe, r // 2 + (r // 2 >= V_BLOCK))
                    pe.wait_ge(raw_done, m - 3 + CREDIT)
                    for k in range(KC):
                        for part, (w, x_t) in enumerate(((wqk_hi, xt_hi), (wqk_hi, xt_lo), (wqk_lo, xt_hi))):
                            mm = pe.matmul(ps_qk[(j * QK_TILES + r) % 4][:], w[:, k, r * P:(r + 1) * P],
                                           x_t[j][:, k, :], start=(k == 0 and part == 0),
                                           stop=(k == KC - 1 and part == 2))
                    mm.then_inc(qk_done, 1)
                    if r in MOVE_AT and not last:
                        transposes(n + 1, MOVE_AT.index(r))
                    for t in (t for t in range(TPG) if V_AT[t] == r):
                        if t == 0:
                            split_done(pe, V_BLOCK)
                        pe.wait_ge(v_done, n * TPG + t - 1 + CREDIT)
                        for k in range(KC):
                            for part, (w, x_t) in enumerate(((wv_hi, xt_hi), (wv_hi, xt_lo), (wv_lo, xt_hi))):
                                mm = pe.matmul(ps_v[t % 2][:, 0:GROUPS * HD],
                                               x_t[j][:, k, t * P:(t + 1) * P], w[:, k, :],
                                               start=(k == 0 and part == 0),
                                               stop=(k == KC - 1 and part == 2))
                        mm.then_inc(vps_done, 1)

            loop_groups(pe, body)


class Context:

    def __init__(self, nc, ctx, o_in, sum_in, inv_dram, wd):
        sb = lambda name, shape: ctx.enter_context(nc.sbuf_tensor(name, shape, F32))
        sem = lambda name: ctx.enter_context(nc.semaphore(name))
        self.o_in, self.inv_dram = o_in, inv_dram
        self.o = [sb(f"ctx_t{i}", [P, KC, P]) for i in range(2)]
        self.inv = [sb(f"inv{i}", [P, KC, P]) for i in range(2)]
        self.o_loaded = [sem(f"o_loaded{i}") for i in range(2)]
        self.inv_loaded = [sem(f"inv_loaded{i}") for i in range(2)]
        self.sums = sb("sums_sb", [P, TG])
        self.sums_in, self.inverted, self.inverse_kept = sem("sums_in"), sem("inverted"), sem("inverse_kept")
        self.ident = sb("ident_sb", [P, P])
        self.bd, self.bb = sb("bd", [P, HID]), sb("bb", [P, HID])
        self.b_lora = sb("b_lora", [P, HID])
        self.rev = sb("rev", [P, EXPERTS])
        self.consts_in = sem("consts3_in")
        self.wd = wd
        self.hi, self.lo = (ctx.enter_context(nc.sbuf_tensor(f"ctx_{k}", [P, KC, P], F32R)) for k in ("hi", "lo"))
        self.ps_d = ctx.enter_context(nc.psum_tensor("ps_d", [P, HID], F32))
        self.divided = sem("ctx_divided")
        self.hi_done = sem("ctx_hi_done")
        self.lo_done = sem("ctx_lo_done")
        self.dense_done = sem("dense_done")
        self.a_done = sem("a_done")
        flat = lambda t, b: (t[b * UPB * GROUPS:(b + 1) * UPB * GROUPS].rearrange("b h s -> (b h s)")
                             .rearrange("(p n) -> p n", p=P))
        self.sums_of = [flat(sum_in, b) for b in range(BATCH)]
        self.inverse_of = [flat(inv_dram, b) for b in range(BATCH)]

    def load(self, sp, n, t):
        n, t = n + t // TPG, t % TPG
        i = t % 2
        cols = slice(t * P, (t + 1) * P)
        sp.dma_start(self.o[i][:], self.o_in[bass.ds(n * GROUPS, GROUPS), :, cols].rearrange("g p s -> p g s")
                     ).then_inc(self.o_loaded[i], 16)
        for h in range(QPG):
            sp.dma_start(self.inv[i][h * HD:(h + 1) * HD],
                         self.inv_dram[bass.ds(n * GROUPS, GROUPS), h, cols].partition_broadcast(HD)
                         ).then_inc(self.inv_loaded[i], 16)


    def divide(self, dve, n, t):
        n, t = n + t // TPG, t % TPG
        i = t % 2
        dve.wait_ge(self.o_loaded[i], (n * 2 + t // 2 + 1) * 16)
        dve.wait_ge(self.inv_loaded[i], (n * 2 + t // 2 + 1) * 64)
        dve.tensor_tensor(self.o[i][:], self.o[i][:], self.inv[i][:], ALU.mult).then_inc(self.divided, 1)

    def high(self, act, n, t):
        n, i = n + t // TPG, t % 2
        act.wait_ge(self.divided, n * TPG + t % TPG + 1)
        if not (isinstance(n, int) and n == 0 and t == 0):
            act.wait_ge(self.dense_done, n * TPG + t % TPG)
        act.activation(self.hi[:], self.o[i][:], ACT.Copy).then_inc(self.hi_done, 1)

    def low(self, pool, n, t):
        n, i = n + t // TPG, t % 2
        pool.wait_ge(self.hi_done, n * TPG + t % TPG + 1)
        pool.tensor_tensor(self.lo[:], self.o[i][:], self.hi[:].bitcast(F32), ALU.subtract
                           ).then_inc(self.lo_done, 1)

    def dense(self, pe, n, t, a, z):
        n, t = n + t // TPG, t % TPG
        tile = n * TPG + t
        if a == 0:
            pe.wait_ge(self.lo_done, tile + 1)
            pe.wait_ge(self.a_done, tile + CREDIT)
        for half in range(2):
            first, end = max(a, half * 3 * KC), min(z, (half + 1) * 3 * KC)
            if first < end:
                cols = slice(half * 512, (half + 1) * 512)
                mm = products(pe, self.ps_d[:, cols], (self.hi, self.lo), self.wd, cols,
                              first - half * 3 * KC, end - half * 3 * KC, True)
        if z == 2 * 3 * KC:
            mm.then_inc(self.dense_done, 1)


def products(pe, bank, parts, weights, cols, a, z, last):
    for j in range(a, z):
        k, (x_part, w_part) = j // 3, ((0, 0), (0, 1), (1, 0))[j % 3]
        mm = pe.matmul(bank, parts[x_part][:, k, :], weights[w_part][:, k, cols],
                       start=(j == 0), stop=(last and j == 3 * KC - 1))
    return mm


def attend(nc, masks, ident, q_hi, q_lo, k_hi, k_lo, v_in, o_out, sum_out, w_dense, w_all, wd, wa,
           b_dense, b_base, b_lora, rev_index, context):
    assert BATCH * GROUPS // 2 == KC
    STEPS = [steps_of(u) for u in range(UPB)]
    NS = [len(s) for s in STEPS]
    CHUNKS = [[(tl, h, c) for h in range(QPG) for tl in range(TPG)
               for c in range(len(max_segments(u * TPG + tl)))] for u in range(UPB)]
    NCH = [len(c) for c in CHUNKS]
    UNITS = 2 * UPB
    step0 = [sum(NS[w % UPB] for w in range(u)) for u in range(UNITS + 1)]
    chunk0 = [sum(NCH[w % UPB] for w in range(u)) for u in range(UNITS + 1)]
    fixes = [[s for s in STEPS[u] if s[0] >= u * TPG or s[3] > s[2]] for u in range(UPB)]
    fix0 = [sum(len(fixes[w % UPB]) * QPG for w in range(u)) for u in range(UNITS + 1)]
    BODY_STEPS, BODY_CHUNKS, BODY_FIXES = step0[-1], chunk0[-1], fix0[-1]
    assert BODY_STEPS % 2 == 0 and all(n % 2 == 0 for n in NCH)
    BODIES = BATCH * GROUPS // 2

    with ExitStack() as ctx:
        sb = lambda name, shape, dt=F32: ctx.enter_context(nc.sbuf_tensor(name, shape, dt))
        ps = lambda name: ctx.enter_context(nc.psum_tensor(name, [P, 512], F32))
        sem = lambda name: ctx.enter_context(nc.semaphore(name))

        kp = [sb(f"kp{i}", [P, SEQ], F32R) for i in range(2)]
        qp = [sb(f"qp{i}", [P, QPG, TG], F32R) for i in range(4)]
        v1 = [sb(f"v1_{i}", [P, SEQ // P, 2 * HD]) for i in range(2)]
        probs = [[sb(f"probs{i}_{h}", [P, TG]) for h in range(QPG)] for i in range(2)]
        part_max = sb("part_max", [P, QPG * TPG, 3])
        neg_max = [sb(f"neg_max{i}", [P, QPG * TPG]) for i in range(2)]
        max_row = [sb(f"max_row{i}", [QPG * TPG, P], F32R) for i in range(2)]
        o_sb = [sb(f"o_sb{i}", [P, 2, TG]) for i in range(2)]
        staged_d, staged_a = sb("staged_d", [P, HID]), sb("staged_a", [P, WA])
        wa_sb = [sb(f"wa_sb_{k}", [P, WA], F32R) for k in ("hi", "lo")]
        idn = context.ident
        idn_bf = sb("idn_bf", [P, P], BF16)
        mask_f = sb("mask_f", [P, P + BLOCK])
        mask_bf = sb("mask_bf", [P, P + BLOCK], BF16)
        ps_max = [context.ps_d[:, i * 512:(i + 1) * 512] for i in range(2)]
        ps_s = [ps(f"ps_s{h}") for h in range(QPG)]
        ps_o = [ps(f"ps_o{i}") for i in range(2)]

        passed = sem("passed_a")
        consts_in = sem("consts_in_a")
        consts_bf = sem("consts_bf")
        ones_set = sem("ones_set")
        q_in = [sem(f"q_in{i}") for i in range(4)]
        k_in = [sem(f"k_in{i}") for i in range(2)]
        v_in_s = [sem(f"v_in{i}") for i in range(2)]
        row_in = [sem(f"row_in{i}") for i in range(2)]
        chunk_done = sem("chunk_done")
        reduced = sem("reduced")
        neg_done = sem("neg_done")
        rowt_done = sem("rowt_done")
        row_done = sem("row_done")
        scores_done = sem("scores_done")
        exp_done = sem("exp_done")
        fix_done = sem("fix_done")
        pv_done = sem("pv_done")
        o_done = sem("o_done")
        o_stored = [sem(f"o_stored{i}") for i in range(2)]
        w_staged = sem("w_staged")
        w_high = sem("w_high")
        w_low = sem("w_low")
        wa_stored = sem("wa_stored")

        block = ctx.enter_context(nc.Block())

        def body_groups(n):
            b = n >> 2
            if not isinstance(n, int):
                b.max_val = BATCH - 1
            return b, (n & 3) * 2

        def load_q(sp, n, u):
            b, g = body_groups(n)
            blk = (b * UPB + u % UPB) * GROUPS + g + u // UPB
            for part, src in ((0, q_hi), (1, q_hi), (2, q_lo)):
                sp.dma_start(qp[u % 4][part * HD:(part + 1) * HD].bitcast(F32),
                             src[bass.ds(blk, 1)].rearrange("o (h d) s -> (o d) h s", h=QPG).bitcast(F32)
                             ).then_inc(q_in[u % 4], 16)

        def load_k(sp, n, j):
            b, g = body_groups(n)
            for part, src in ((0, k_hi), (1, k_lo), (2, k_hi)):
                sp.dma_start(kp[j][part * HD:(part + 1) * HD].rearrange("d (n s) -> d n s", n=UPB).bitcast(F32),
                             src.rearrange("(n g) d s -> n g d s", g=GROUPS)[bass.ds(b * UPB, UPB), bass.ds(g + j, 1)]
                             .rearrange("n o d s -> (o d) n s").bitcast(F32)
                             ).then_inc(k_in[j], 16)

        def load_v(sp, n, j):
            b, g = body_groups(n)
            sp.dma_start(v1[j][:, :, 0:HD],
                         v_in[bass.ds(b * SEQ, SEQ), bass.ds((g + j) * HD, HD)].rearrange("(t p) d -> p t d", p=P)
                         ).then_inc(v_in_s[j], 16)

        def first_chunk(u):
            return u // UNITS * BODY_CHUNKS + chunk0[u % UNITS]

        slots, rows, first = interleave(STEPS, CHUNKS)

        def chunks_in(u, last):
            return [(w + u - u % UPB, c) for step in slots[u % UPB] for slot in step for w, c in slot
                    if not (last and w + u - u % UPB >= UNITS)]

        def rows_in(u, last):
            ahead = u // UPB * (BODY_CHUNKS // 2)
            return {s: (w + u - u % UPB, count + ahead) for s, (w, count) in rows[u % UPB].items()
                    if not (last and w + u - u % UPB >= UNITS)}

        def loop_bodies(eng, body):
            with eng.Fori(0, BODIES - 1) as n:
                body(n, False)
            body(BODIES - 1, True)

        @block.sync
        def _(sp):
            for i in range(2):
                sp.sem_inc(row_in[i], CREDIT)
                sp.sem_inc(o_stored[i], CREDIT)
            sp.dma_start(idn[:], ident).then_inc(consts_in, 16)
            sp.dma_start(mask_f[:], masks).then_inc(consts_in, 16)


            def stage_weights(n):
                sp.dma_start(staged_d[:], w_dense[bass.ds(n * P, P), :]).then_inc(w_staged, 16)
                sp.dma_start(staged_a[:], w_all[bass.ds(n * P, P), :]).then_inc(w_staged, 16)

            def store_split(n):
                for k in range(2):
                    sp.dma_start(wa[k][bass.ds(n, 1)].rearrange("o p n -> (o p) n").bitcast(F32),
                                 wa_sb[k][:].bitcast(F32)).then_inc(wa_stored, 16)

            def put_row(u, n):
                sp.wait_ge(row_done, n * UNITS + u + 1 + CREDIT)
                sp.dma_start(qp[u % 4][3 * HD:3 * HD + 1].bitcast(F32), max_row[u % 2][:].bitcast(F32)
                             ).then_inc(row_in[u % 2], 16)

            def store_o(n, u):
                sp.wait_ge(o_done, (n * UNITS + u + 1) * 2 + CREDIT)
                b, g = body_groups(n)
                blk = (b * UPB + u % UPB) * GROUPS + g + u // UPB
                for hh in range(2):
                    for dst, first, size in ((o_out, 0, HD), (sum_out, HD, 1)):
                        sp.dma_start(dst[bass.ds(blk, 1)].rearrange("o (i h d) s -> h (o d) i s", i=2, h=2)[hh],
                                     o_sb[u % 2][hh * 2 * HD + first:hh * 2 * HD + first + size]
                                     ).then_inc(o_stored[u % 2], 16)

            load_q(sp, 0, 0)
            load_v(sp, 0, 0)
            load_q(sp, 0, 1)
            load_q(sp, 0, 2)
            load_k(sp, 0, 1)
            load_v(sp, 0, 1)
            for what, unit, _ in first:
                if what == "row":
                    put_row(unit, 0)
            stage_weights(0)
            sp.dma_start(context.bd[:], b_dense.partition_broadcast(P)).then_inc(context.consts_in, 16)
            sp.dma_start(context.bb[:], b_base.partition_broadcast(P)).then_inc(context.consts_in, 16)
            sp.dma_start(context.rev[:], rev_index.partition_broadcast(P)).then_inc(context.consts_in, 16)
            sp.dma_start(context.b_lora[:], b_lora).then_inc(context.consts_in, 16)

            def body(n, last):
                for u in range(UNITS):
                    if not (last and u + 3 >= UNITS):
                        sp.wait_ge(scores_done, (n * BODY_STEPS + step0[u]) * QPG + CREDIT)
                        load_q(sp, n + (u + 3) // UNITS, (u + 3) % UNITS)
                    if u == UPB and not last:
                        sp.wait_ge(pv_done, (n * BODY_STEPS + step0[UPB]) * 2 + CREDIT)
                        load_k(sp, n + 1, 0)
                        load_v(sp, n + 1, 0)
                    if u > 0:
                        store_o(n, u - 1)
                    if last and u == UNITS - 1:
                        sp.wait_ge(context.inverted, 1)
                        sp.dma_start(context.inverse_of[0], context.sums[:]).then_inc(context.inverse_kept, 16)
                        sp.wait_ge(context.inverse_kept, 16)
                        for t in range(2):
                            context.load(sp, 0, t)
                    if last and u == UNITS - 3:
                        for i in range(2):
                            sp.wait_ge(o_stored[i], CREDIT + BODIES // 2 * UNITS // 2 * 64)
                        sp.dma_start(context.sums[:], context.sums_of[0]).then_inc(context.sums_in, 16)
                    if u == UPB - 1:
                        sp.wait_ge(w_low, (n + 1) * 2)
                        store_split(n)
                        if not last:
                            stage_weights(n + 1)
                    for unit, _ in rows_in(u, last).values():
                        put_row(unit, n)
                store_o(n, UNITS - 1)
                if not last:
                    load_k(sp, n + 1, 1)
                    load_v(sp, n + 1, 1)

            loop_bodies(sp, body)
            sp.wait_ge(context.inverse_kept, 16)
            sp.wait_ge(context.consts_in, 64)
            for i in range(2):
                sp.wait_ge(o_stored[i], CREDIT + BODIES * UNITS // 2 * 64)
            sp.wait_ge(wa_stored, CREDIT + BODIES * 32)

        @block.gpsimd
        def _(pool):
            pool.sem_inc(wa_stored, CREDIT)
            for j in range(2):
                pool.memset(v1[j][:, :, HD:2 * HD], 1.0).then_inc(ones_set, 1)
            pool.wait_ge(ones_set, 2)
            for j in range(2):
                pool.memset(kp[j][3 * HD:3 * HD + 1, :].bitcast(F32), 1.0).then_inc(ones_set, 1)
            pool.wait_ge(ones_set, 4)

            def split_low(n):
                pool.wait_ge(w_high, n * 2 + 1)
                pool.tensor_tensor(wd[1][:, bass.ds(n, 1), :].rearrange("p o n -> p (o n)"), staged_d[:],
                                   wd[0][:, bass.ds(n, 1), :].rearrange("p o n -> p (o n)").bitcast(F32),
                                   ALU.subtract).then_inc(w_low, 1)
                pool.wait_ge(w_high, n * 2 + 2)
                pool.wait_ge(wa_stored, n * 32 + CREDIT)
                pool.tensor_tensor(wa_sb[1][:], staged_a[:], wa_sb[0][:].bitcast(F32), ALU.subtract
                                   ).then_inc(w_low, 1)

            def body(n, last):
                for u in range(UNITS):
                    for s, (key, start, mid, end) in enumerate(STEPS[u % UPB]):
                        step = step0[u] + s
                        if (u, s) == (1, 1):
                            split_low(n)
                        if (key, start, mid, end) not in fixes[u % UPB]:
                            continue
                        for h in range(QPG):
                            pool.wait_ge(exp_done, (n * BODY_STEPS + step) * QPG + h + 1)
                            pool.sem_inc(passed, 1)
                            p = probs[step % 2][h]
                            if key >= (u % UPB) * TPG:
                                pool.affine_select(out=p[:, start:start + P], in_=p[:, start:start + P],
                                                   compare_op=ALU.is_ge, fill=0.0, base=0,
                                                   pattern=[[1, P]], channel_multiplier=-1
                                                   ).then_inc(fix_done, 1)
                            else:
                                pool.affine_select(out=p[:, mid:end], in_=p[:, mid:end],
                                                   compare_op=ALU.is_ge, fill=0.0, base=-BLOCK,
                                                   pattern=[[0, end - mid]], channel_multiplier=1
                                                   ).then_inc(fix_done, 1)

            loop_bodies(pool, body)
            context.low(pool, 0, 0)

        @block.scalar
        def _(act):
            act.sem_inc(row_done, CREDIT)
            act.sem_inc(o_done, CREDIT)
            load_k(act, 0, 0)
            def row(u, n, bank):
                act.wait_ge(rowt_done, n * UNITS + u + 1)
                act.wait_ge(row_in[u % 2], (n * (UNITS // 2) + u // 2) * 16 + CREDIT)
                act.activation(max_row[u % 2][:], ps_max[bank][0:QPG * TPG, 0:P], ACT.Copy
                               ).then_inc(row_done, 1)

            def out(u, n, i):
                act.wait_ge(pv_done, (n * BODY_STEPS + step0[u + 1]) * 2 - 1 + i + CREDIT)
                if i == 0:
                    act.wait_ge(o_stored[u % 2], (n * (UNITS // 2) + u // 2) * 64 + CREDIT)
                act.activation(o_sb[u % 2][:, i, :], ps_o[i][:], ACT.Copy).then_inc(o_done, 1)

            for what, unit, count in first:
                if what == "row":
                    row(unit, 0, count % 2)

            def split_high(n, which):
                act.wait_ge(w_staged, (n + 1) * 32)
                if which == 0:
                    act.activation(wd[0][:, bass.ds(n, 1), :].rearrange("p o n -> p (o n)"), staged_d[:],
                                   ACT.Copy).then_inc(w_high, 1)
                else:
                    act.wait_ge(wa_stored, n * 32 + CREDIT)
                    act.activation(wa_sb[0][:], staged_a[:], ACT.Copy).then_inc(w_high, 1)

            def body(n, last):
                for u in range(UNITS):
                    turned = rows_in(u, last)
                    for s, (key, start, mid, end) in enumerate(STEPS[u % UPB]):
                        step = step0[u] + s
                        for h in range(QPG):
                            if h % 2 == 0:
                                act.wait_ge(pv_done, (n * BODY_STEPS + step - 2) * 2 + h // 2 + 1 + CREDIT)
                            act.wait_ge(scores_done, (n * BODY_STEPS + step) * QPG + h + 1 + CREDIT)
                            act.activation(probs[step % 2][h][:, start:end], ps_s[h][:, start:end],
                                           ACT.Exp).then_inc(exp_done, 1)
                            if h == 0 and s - 1 in turned:
                                unit, count = turned[s - 1]
                                row(unit, n, count % 2)
                            if u == 1 and s in (1, 2) and h == 1:
                                split_high(n, s - 1)
                            if s == 0 and u > 0 and h % 2:
                                out(u - 1, n, h // 2)
                out(UNITS - 1, n, 0)
                out(UNITS - 1, n, 1)
                if last:
                    context.high(act, 0, 0)

            loop_bodies(act, body)

        @block.vector
        def _(dve):
            dve.sem_inc(reduced, CREDIT)
            dve.sem_inc(neg_done, CREDIT)
            dve.wait_ge(consts_in, 32)
            dve.tensor_copy(idn_bf[:], idn[:]).then_inc(consts_bf, 1)
            dve.tensor_copy(mask_bf[:], mask_f[:]).then_inc(consts_bf, 1)

            def maxima(u, n, c):
                if c == 0:
                    dve.wait_ge(neg_done, n * UNITS + u + CREDIT)
                chunk_n = n * BODY_CHUNKS + first_chunk(u)
                tl, h, seg = CHUNKS[u % UPB][c]
                width = bank_width((u % UPB) * TPG + tl, seg)
                dve.wait_ge(chunk_done, chunk_n + c + 1)
                dve.reduce_max(part_max[:, h * TPG + tl, seg:seg + 1], ps_max[c % 2][:, 0:width],
                               AX.X).then_inc(reduced, 1)
                if c == NCH[u % UPB] - 1:
                    n_seg = len(max_segments((u % UPB) * TPG))
                    dve.wait_ge(reduced, chunk_n + c + 1 + CREDIT)
                    dve.wait_ge(row_done, n * UNITS + u - 1 + CREDIT)
                    dve.tensor_reduce(neg_max[u % 2][:], part_max[:, :, 0:n_seg], AX.X, ALU.max,
                                      negate=True).then_inc(neg_done, 1)

            for what, unit, c in first:
                if what == "chunk":
                    maxima(unit, 0, c)

            def body(n, last):
                for u in range(UNITS):
                    for unit, c in chunks_in(u, last):
                        maxima(unit, n, c)
                    if last and u == UNITS - 2:
                        dve.wait_ge(context.sums_in, 16)
                        dve.reciprocal(context.sums[:], context.sums[:]).then_inc(context.inverted, 1)

            loop_bodies(dve, body)
            dve.sem_inc(context.a_done, CREDIT)
            context.divide(dve, 0, 0)
            context.divide(dve, 0, 1)

        @block.tensor
        def _(pe):
            pe.sem_inc(scores_done, CREDIT)
            pe.sem_inc(pv_done, CREDIT)

            def chunk(u, c, n, row_unit):
                tl, h, seg = CHUNKS[u % UPB][c]
                tile = (u % UPB) * TPG + tl
                segs = max_segments(tile)
                start, width = segs[seg]
                k = kp[(u // UPB) % 2]
                bank = ps_max[c % 2]
                if c == 0:
                    pe.wait_ge(q_in[u % 4], n * 96 + (u // 4 + 1) * 48)
                    if u % UPB == 0:
                        pe.wait_ge(k_in[(u // UPB) % 2], n * 48 + (u // UNITS + 1) * 48)
                if row_unit is not None:
                    pe.wait_ge(row_done, n * UNITS + row_unit + 1 + CREDIT)
                pe.wait_ge(reduced, n * BODY_CHUNKS + first_chunk(u) + c - 1 + CREDIT)
                diag = seg == len(segs) - 1
                edge = tile >= LT and seg == 0 and not edge_is_vertical(tile)
                lhs = qp[u % 4][0:3 * HD, h, tl * P:(tl + 1) * P]
                if seg == 0 and has_vertical(tile):
                    vert = (VERT - 1) * BLOCK
                    step = start - vert
                    rhs = k[0:3 * HD, vert:vert + 2 * step].rearrange("p (a b) -> p a b", a=2)[:, :, 0:BLOCK]
                    mm = pe.matmul(bank[:, 0:2 * BLOCK], lhs, rhs, start=True, stop=not edge)
                    at = BLOCK
                else:
                    mm = pe.matmul(bank[:, 0:width], lhs, k[0:3 * HD, start:start + width],
                                   start=True, stop=not (edge or diag))
                    at = 0
                if edge:
                    mm = pe.matmul(bank[:, at:at + BLOCK], idn_bf[:], mask_bf[:, P:P + BLOCK],
                                   start=False, stop=True)
                if diag:
                    mm = pe.matmul(bank[:, width - P:width], idn_bf[:], mask_bf[:, 0:P],
                                   start=False, stop=True)
                mm.then_inc(chunk_done, 1)

            def turn_row(u, n, count, last):
                pe.wait_ge(neg_done, n * UNITS + u + 1 + CREDIT)
                pe.wait_ge(reduced, n * BODY_CHUNKS + (min(count, BODY_CHUNKS + 1) if last else count)
                           - 1 + CREDIT)
                pe.transpose(ps_max[count % 2][0:QPG * TPG, 0:P], neg_max[u % 2][:], idn[:]
                             ).then_inc(rowt_done, 1)

            def scores(u, s, h, n):
                key, start, mid, end = STEPS[u % UPB][s]
                j, step = (u // UPB) % 2, u // UNITS * BODY_STEPS + step0[u % UNITS] + s
                if s == 0:
                    pe.wait_ge(row_in[u % 2], (n * (UNITS // 2) + u // 2 + 1) * 16 + CREDIT)
                if step > 0:
                    pe.wait_ge(exp_done, (n * BODY_STEPS + step - 1) * QPG + h + 1)
                pe.matmul(ps_s[h][:, start:end], kp[j][0:3 * HD + 1, key * P:(key + 1) * P],
                          qp[u % 4][0:3 * HD + 1, h, start:end], start=True, stop=True
                          ).then_inc(scores_done, 1)

            def weigh_v(u, s, h, n):
                key, start, mid, end = STEPS[u % UPB][s]
                if (key, start, mid, end) in fixes[u % UPB]:
                    before = len([x for x in STEPS[u % UPB][:s] if x in fixes[u % UPB]])
                    pe.wait_ge(fix_done, n * BODY_FIXES + fix0[u] + before * QPG + h + 1)
                pe.wait_ge(exp_done, (n * BODY_STEPS + step0[u] + s) * QPG + h + 1)
                if s == 0:
                    if u % UPB == 0:
                        pe.wait_ge(v_in_s[u // UPB], n * 16 + 16)
                    pe.wait_ge(o_done, (n * UNITS + u - 1) * 2 + h // 2 + 1 + CREDIT)
                rows = slice((h % 2) * 2 * HD, (h % 2 + 1) * 2 * HD)
                mm = pe.matmul(ps_o[h // 2][rows, start:end], v1[(u // UPB) % 2][:, key, :],
                               probs[(step0[u] + s) % 2][h][:, start:end],
                               start=(s == 0), stop=(s == NS[u % UPB] - 1), skip_group_check=True,
                               tile_position=(0, (h % 2) * 2 * HD))
                if h % 2:
                    mm.then_inc(pv_done, 1)

            pe.wait_ge(consts_bf, 2)
            row_unit = None
            for what, unit, c in first:
                if what == "row":
                    turn_row(unit, 0, c, False)
                    row_unit = unit
                else:
                    chunk(unit, c, 0, row_unit)
                    row_unit = None
            pe.wait_ge(ones_set, 4)
            for h in range(QPG):
                scores(0, 0, h, 0)
            row_before = row_unit

            def body(n, last):
                row_unit = row_before
                for u in range(UNITS):
                    turned = rows_in(u, last)
                    for s in range(NS[u % UPB]):
                        for half in range(2):
                            for h in (half * 2, half * 2 + 1):
                                if s + 1 < NS[u % UPB]:
                                    scores(u, s + 1, h, n)
                                elif not (last and u + 1 == UNITS):
                                    scores(u + 1, 0, h, n)
                                if h == 0 and s in turned:
                                    row_unit = turned[s][0]
                                    turn_row(row_unit, n, turned[s][1], last)
                                row_unit = chunks(u, slots[u % UPB][s][half * 3 + h % 2], n, last, row_unit)
                            weigh_v(u, s, half * 2, n)
                            weigh_v(u, s, half * 2 + 1, n)
                            row_unit = chunks(u, slots[u % UPB][s][half * 3 + 2], n, last, row_unit)
                assert last or row_unit == row_before

            def chunks(u, some, n, last, row_unit):
                for w, c in some:
                    unit = w + u - u % UPB
                    if not (last and unit >= UNITS):
                        chunk(unit, c, n, row_unit)
                        row_unit = None
                return row_unit

            loop_bodies(pe, body)
            context.dense(pe, 0, 0, 0, 2 * 3 * KC)


def finish(nc, wd, wa_in, x, context, out):
    with ExitStack() as ctx:
        sb = lambda name, shape, dt=F32: ctx.enter_context(nc.sbuf_tensor(name, shape, dt))
        ps = lambda name, width=512: ctx.enter_context(nc.psum_tensor(name, [P, width], F32))
        sem = lambda name: ctx.enter_context(nc.semaphore(name))
        two = lambda name, shape: [sb(f"{name}{i}", shape) for i in range(2)]

        idn, bd, bb, b_lora, rev = context.ident, context.bd, context.bb, context.b_lora, context.rev
        minus_half = sb("minus_half_f", [P, 1])
        wa = [sb(f"wa_{k}", [P, KC, WA], F32R) for k in ("hi", "lo")]
        ps_d, a_done, dense_done = context.ps_d, context.a_done, context.dense_done
        x1 = two("x1_", [P, HID])
        a_sb = sb("a_sb", [P, HID])
        xn2 = sb("xn2", [P, HID])
        x2_hi, x2_lo = sb("x2_hi", [P, KC, P], F32R), sb("x2_lo", [P, KC, P], F32R)
        f_sb = sb("f_sb", [P, HID])
        stats = [two(f"stats{k}_", [P, 2, 6]) for k in range(3)]
        mean_var = [two(f"mean_var{k}_", [P, 2]) for k in range(3)]
        var_eps = [two(f"var_eps{k}_", [P, 1]) for k in range(3)]
        rstd = [two(f"rstd{k}_", [P, 1]) for k in range(3)]
        shift = [two(f"shift{k}_", [P, 1]) for k in range(3)]
        logits, top, first, second = (two(f"{k}_", [P, EXPERTS]) for k in ("logits", "top", "first", "second"))
        score, best = two("score", [P, EXPERTS]), two("best", [P, 1])
        gap, expo, half, w1, w2 = (two(f"{k}_", [P, 1]) for k in ("gap", "expo", "half", "w1", "w2"))
        comb, hw, hw_t = two("comb", [P, EXPERTS]), two("hw", [P, ER]), two("hw_t", [P, P])
        ps_f = ps("ps_f", HID)
        ps_x = [ps(f"ps_x{i}") for i in range(2)]
        ps_ra, ps_h = ps("ps_ra"), ps("ps_h")

        passed = sem("passed_f")
        half_set = sem("half_set")
        x_loaded = [sem(f"x_loaded{i}") for i in range(2)]
        out_stored = sem("out_stored")
        wa_loaded = [sem(f"wa_loaded{i}") for i in range(3)]
        eps_done = [sem(f"eps_done{k}") for k in range(3)]
        rstd_done = [sem(f"rstd_done{k}") for k in range(3)]
        shift_done = [sem(f"shift_done{k}") for k in range(3)]
        y_done = sem("y_done")
        x1_done = sem("x1_done")
        xn2_done = sem("xn2_done")
        x2_turned = sem("x2_turned")
        x2_hi_done = sem("x2_hi_done")
        x2_lo_done = sem("x2_lo_done")
        ra_done = sem("ra_done")
        gap_done = sem("gap_done")
        expo_done = sem("expo_done")
        hw_done = sem("hw_done")
        hwt_turned = sem("hwt_turned")
        hwt_done = sem("hwt_done")
        ffn_done = sem("ffn_done")
        f_done = sem("f_done")
        z_done = sem("z_done")
        out_done = sem("out_done")
        chain = sem("chain")
        chain_first = sem("chain_first")

        NT = NTG * TPG

        def loop_tiles(eng, body):
            with eng.Fori(0, NTG - 1) as n:
                for t in range(TPG):
                    body(n, t, NT)
            for t in range(TPG):
                body(NTG - 1, t, TPG - 1 - t)

        WA_BLOCKS = (slice(0, RA_COLS), slice(RA_COLS, RA_COLS + HALF_COLS), slice(RA_COLS + HALF_COLS, WA))

        block = ctx.enter_context(nc.Block())

        @block.sync
        def _(sp):
            def load_x(n, t):
                n, t = n + t // TPG, t % TPG
                sp.dma_start(x1[t % 2][:], x[bass.ds((n * TPG + t) * P, P), :]).then_inc(x_loaded[t % 2], 16)

            def load_wa(i):
                for k in range(2):
                    sp.dma_start(wa[k][:, :, WA_BLOCKS[i]].bitcast(F32),
                                 wa_in[k][:, :, WA_BLOCKS[i]].rearrange("k p n -> p k n").bitcast(F32)
                                 ).then_inc(wa_loaded[i], 16)

            load_x(0, 0)
            sp.wait_ge(context.lo_done, 1)
            context.load(sp, 0, 2)
            sp.dma_start(context.sums[:], context.sums_of[1]).then_inc(context.sums_in, 16)
            load_wa(0)
            load_x(0, 1)
            load_wa(1)
            load_wa(2)
            sp.wait_ge(context.inverted, 2)
            sp.dma_start(context.inverse_of[1], context.sums[:]).then_inc(context.inverse_kept, 16)
            sp.wait_ge(context.inverse_kept, 32)

            def body(n, t, rest):
                if rest >= 3:
                    sp.wait_ge(context.lo_done, n * TPG + t + 2)
                    context.load(sp, n, t + 3)
                sp.wait_ge(out_done, n * TPG + t + 1)
                sp.dma_start(out[bass.ds((n * TPG + t) * P, P), :], f_sb[:]).then_inc(out_stored, 16)
                if rest >= 2:
                    load_x(n, t + 2)

            loop_tiles(sp, body)
            sp.wait_ge(out_stored, CREDIT + NT * 16)

        @block.gpsimd
        def _(pool):
            pool.sem_inc(out_stored, CREDIT)
            pool.memset(minus_half[:], -0.5).then_inc(half_set, 1)
            pool.wait_ge(half_set, 1)

            def root(k, n, t):
                n, i = n + t // TPG, t % 2
                pool.wait_ge(eps_done[k], n * TPG + t % TPG + 1)
                pool.tensor_tensor(rstd[k][i][:], var_eps[k][i][:], minus_half[:], ALU.pow
                                   ).then_inc(rstd_done[k], 1)

            context.low(pool, 0, 1)
            root(0, 0, 0)
            root(1, 0, 0)

            def body(n, t, rest):
                if rest >= 2:
                    context.low(pool, n, t + 2)
                if rest >= 1:
                    root(0, n, t + 1)
                    root(1, n, t + 1)
                root(2, n, t)
                pool.wait_ge(z_done, n * TPG + t + 1)
                pool.tensor_tensor(f_sb[:], f_sb[:], x1[t % 2][:], ALU.add).then_inc(out_done, 1)

            loop_tiles(pool, body)

        @block.scalar
        def _(act):
            act.sem_inc(hwt_done, CREDIT)

            def affine(k, buf, n, t, done):
                n, i = n + t // TPG, t % 2
                act.wait_ge(shift_done[k], n * TPG + t % TPG + 1)
                act.activation(buf[:], buf[:], ACT.Identity, bias=shift[k][i][:],
                               scale=rstd[k][i][:]).then_inc(done, 1)

            context.high(act, 0, 1)
            affine(0, a_sb, 0, 0, y_done)

            def body(n, t, rest):
                i = t % 2
                for half_ in range(2):
                    act.wait_ge(x2_turned, (n * TPG + t) * 2 + half_ + 1)
                    act.activation(x2_hi[:, half_ * 4:half_ * 4 + 4, :],
                                   ps_x[half_][:].rearrange("p (k s) -> p k s", k=4), ACT.Copy
                                   ).then_inc(x2_hi_done, 1)
                if rest >= 2:
                    context.high(act, n, t + 2)
                act.wait_ge(gap_done, n * TPG + t + 1)
                act.activation(expo[i][:], gap[i][:], ACT.Exp).then_inc(expo_done, 1)
                act.wait_ge(hwt_turned, n * TPG + t + 1)
                act.activation(hw_t[i][:], ps_h[:, 0:P], ACT.Copy).then_inc(hwt_done, 1)
                if rest >= 1:
                    affine(0, a_sb, n, t + 1, y_done)
                affine(2, f_sb, n, t, z_done)

            loop_tiles(act, body)

        @block.vector
        def _(dve):
            dve.sem_inc(f_done, CREDIT)
            dve.sem_inc(x2_lo_done, CREDIT)
            count = [0]

            def link(ins, n):
                ins.then_inc(chain if n is not None else chain_first, 1)
                count[0] += 1
                if n is None:
                    dve.wait_ge(chain_first, count[0])
                else:
                    dve.wait_ge(chain, n * LINKS_PER_BODY + count[0])

            def norm_stats(k, src, i, n):
                dve.bn_stats(stats[k][i][:, 0, :], src[:, 0:512])
                link(dve.bn_stats(stats[k][i][:, 1, :], src[:, 512:1024]), n)
                dve.sem_inc(passed, 1)
                link(dve.bn_aggr(mean_var[k][i][:], stats[k][i][:].rearrange("p a b -> p (a b)")), n)
                dve.tensor_scalar(var_eps[k][i][:], mean_var[k][i][:, 1:2], EPS, None, ALU.add
                                  ).then_inc(eps_done[k], 1)

            def norm_shift(k, i, tile):
                dve.wait_ge(rstd_done[k], tile + 1)
                dve.scalar_tensor_tensor(shift[k][i][:], mean_var[k][i][:, 0:1], -1.0, rstd[k][i][:],
                                         op0=ALU.mult, op1=ALU.mult).then_inc(shift_done[k], 1)

            def evacuate_dense(n, t):
                n, t = n + t // TPG, t % TPG
                dve.wait_ge(dense_done, n * TPG + t + 1)
                dve.wait_ge(x1_done, n * TPG + t + CREDIT)
                dve.tensor_tensor(a_sb[:], ps_d[:], bd[:], ALU.add).then_inc(a_done, 1)

            def attention_norms(n, t, links):
                n, t = n + t // TPG, t % TPG
                i, tile = t % 2, n * TPG + t
                dve.wait_ge(a_done, tile + 1 + CREDIT)
                norm_stats(0, a_sb, i, links)
                norm_shift(0, i, tile)
                dve.wait_ge(y_done, tile + 1)
                dve.wait_ge(x_loaded[i], (n * 2 + t // 2 + 1) * 16)
                dve.tensor_tensor(x1[i][:], a_sb[:], x1[i][:], ALU.add).then_inc(x1_done, 1)
                dve.wait_ge(x1_done, tile + 1 + CREDIT)
                norm_stats(1, x1[i], i, links)
                dve.wait_ge(rstd_done[1], tile + 1)
                dve.tensor_scalar(xn2[:], x1[i][:], mean_var[1][i][:, 0:1], rstd[1][i][:],
                                  ALU.subtract, ALU.mult).then_inc(xn2_done, 1)

            def router(n, t):
                i = t % 2
                dve.wait_ge(ra_done, n * TPG + t + 1)
                link(dve.tensor_copy(logits[i][:], ps_ra[:, 0:EXPERTS]), n)
                dve.sem_inc(passed, 1)
                link(dve.max(top[i][:], logits[i][:]), n)

                def one_hot(dst, values, value):
                    link(dve.scalar_tensor_tensor(score[i][:], values, value, rev[:],
                                                  op0=ALU.is_equal, op1=ALU.mult), n)
                    link(dve.reduce_max(best[i][:], score[i][:], AX.X), n)
                    link(dve.tensor_scalar(dst[i][:], score[i][:], best[i][:], None, ALU.is_equal), n)

                one_hot(first, logits[i][:], top[i][:, 0:1])
                link(dve.scalar_tensor_tensor(logits[i][:], first[i][:], -3.0e38, logits[i][:],
                                              op0=ALU.mult, op1=ALU.add), n)
                one_hot(second, logits[i][:], top[i][:, 1:2])
                dve.tensor_tensor(gap[i][:], top[i][:, 1:2], top[i][:, 0:1], ALU.subtract
                                  ).then_inc(gap_done, 1)
                dve.wait_ge(expo_done, n * TPG + t + 1)
                link(dve.tensor_scalar(half[i][:], expo[i][:], 1.0, 0.5, ALU.add, ALU.mult), n)
                link(dve.reciprocal(w1[i][:], half[i][:]), n)
                link(dve.tensor_tensor(w2[i][:], w1[i][:], expo[i][:], ALU.mult), n)
                link(dve.tensor_scalar(comb[i][:], first[i][:], w1[i][:], None, ALU.mult), n)
                link(dve.scalar_tensor_tensor(comb[i][:], second[i][:], w2[i][:], comb[i][:],
                                              op0=ALU.mult, op1=ALU.add), n)
                dve.tensor_tensor(hw[i][:].rearrange("p (e r) -> p e r", r=RANK),
                                  ps_ra[:, EXPERTS:EXPERTS + ER].rearrange("p (e r) -> p e r", r=RANK),
                                  comb[i][:].unsqueeze(2).to_broadcast([P, EXPERTS, RANK]),
                                  ALU.mult).then_inc(hw_done, 1)

            def ffn_norm(n, t):
                i, tile = t % 2, n * TPG + t
                dve.wait_ge(ffn_done, tile + 1)
                dve.wait_ge(out_stored, tile * 16 + CREDIT)
                dve.tensor_tensor(f_sb[:, 0:HEAD_COLS].rearrange("p (b n) -> p b n", b=2),
                                  ps_f[:].rearrange("p (b n) -> p b n", b=2)[:, :, 0:HALF_COLS],
                                  bb[:, 0:HEAD_COLS].rearrange("p (b n) -> p b n", b=2), ALU.add)
                dve.tensor_tensor(f_sb[:, HEAD_COLS:HID], ps_ra[:, RA:RA_COLS], bb[:, HEAD_COLS:HID],
                                  ALU.add).then_inc(f_done, 1)
                dve.wait_ge(f_done, tile + 1 + CREDIT)
                norm_stats(2, f_sb, i, n)
                norm_shift(2, i, tile)

            LINKS_PER_BODY = TPG * (3 * 2 + 14)
            dve.sem_inc(x1_done, CREDIT)
            evacuate_dense(0, 0)
            attention_norms(0, 0, None)
            dve.wait_ge(context.sums_in, 32)
            dve.reciprocal(context.sums[:], context.sums[:]).then_inc(context.inverted, 1)

            def body(n, t, rest):
                if t == 0:
                    count[0] = 0
                if rest >= 2:
                    context.divide(dve, n, t + 2)
                for half_ in range(2):
                    dve.wait_ge(x2_hi_done, (n * TPG + t) * 2 + half_ + 1)
                    dve.tensor_tensor(x2_lo[:, half_ * 4:half_ * 4 + 4, :],
                                      ps_x[half_][:].rearrange("p (k s) -> p k s", k=4),
                                      x2_hi[:, half_ * 4:half_ * 4 + 4, :].bitcast(F32), ALU.subtract
                                      ).then_inc(x2_lo_done, 1)
                router(n, t)
                if rest >= 1:
                    evacuate_dense(n, t + 1)
                if rest >= 1:
                    attention_norms(n, t + 1, n)
                ffn_norm(n, t)
                assert t < TPG - 1 or rest == 0 or count[0] == LINKS_PER_BODY, count

            loop_tiles(dve, body)

        @block.tensor
        def _(pe):
            LATE, LATE_HW = 16, 8
            ALL = 3 * KC
            x2_parts = (x2_hi, x2_lo)

            def body(n, t, rest):
                i, tile = t % 2, n * TPG + t
                if rest >= 1:
                    context.dense(pe, n, t + 1, 0, 2 * ALL - LATE)
                pe.wait_ge(xn2_done, tile + 1)
                for half_ in range(2):
                    pe.wait_ge(x2_lo_done, (tile - 1) * 2 + half_ + 1 + CREDIT)
                    for c in range(4):
                        k = half_ * 4 + c
                        mm = pe.transpose(ps_x[half_][:, c * P:(c + 1) * P],
                                          xn2[:, k * P:(k + 1) * P], idn[:])
                    mm.then_inc(x2_turned, 1)
                if rest >= 1:
                    context.dense(pe, n, t + 1, 2 * ALL - LATE, 2 * ALL)
                pe.wait_ge(x2_lo_done, tile * 2 + 2 + CREDIT)
                pe.wait_ge(f_done, tile + CREDIT)
                pe.wait_ge(wa_loaded[0], 32)
                products(pe, ps_ra[:, 0:RA_COLS], x2_parts, wa, WA_BLOCKS[0], 0, ALL, True).then_inc(ra_done, 1)
                pe.wait_ge(wa_loaded[1], 32)
                products(pe, ps_f[:, 0:HALF_COLS], x2_parts, wa, WA_BLOCKS[1], 0, ALL, False)
                pe.wait_ge(wa_loaded[2], 32)
                products(pe, ps_f[:, 512:512 + HALF_COLS], x2_parts, wa, WA_BLOCKS[2], 0, ALL - LATE_HW, False)
                pe.wait_ge(hw_done, tile + 1)
                pe.transpose(ps_h[:, 0:P], hw[i][:], idn[:]).then_inc(hwt_turned, 1)
                products(pe, ps_f[:, 512:512 + HALF_COLS], x2_parts, wa, WA_BLOCKS[2], ALL - LATE_HW, ALL, False)
                pe.wait_ge(hwt_done, tile + 1 + CREDIT)
                for bank, first, width in ((ps_f[:, 0:HALF_COLS], 0, HALF_COLS),
                                           (ps_f[:, 512:512 + HALF_COLS], HALF_COLS, HALF_COLS),
                                           (ps_ra[:, RA:RA_COLS], HEAD_COLS, HID - HEAD_COLS)):
                    mm = pe.matmul(bank, hw_t[i][:], b_lora[:, first:first + width], start=False,
                                   stop=True, skip_group_check=(first == HEAD_COLS))
                mm.then_inc(ffn_done, 1)

            loop_tiles(pe, body)


def build(nc, x, w_qk, b_qk, w_v, b_v, w_dense, b_dense, w_all, b_base, b_lora, rope, ident,
          masks, rev_index, out):
    kept = lambda name, shape, dt: nc.dram_tensor(name, shape, dt, kind="Internal").ap()
    q_hi, q_lo = (kept(f"q_{k}", [NTG * GROUPS, QPG * HD, TG], F32R) for k in ("hi", "lo"))
    k_hi, k_lo = (kept(f"k_{k}", [NTG * GROUPS, HD, TG], F32R) for k in ("hi", "lo"))
    v_all = kept("v_all", [BATCH * SEQ, GROUPS * HD], F32)
    o_all = kept("o_all", [NTG * GROUPS, QPG * HD, TG], F32)
    sums = kept("sums", [NTG * GROUPS, QPG, TG], F32)
    inv_sums = kept("inv_sums", [NTG * GROUPS, QPG, TG], F32)
    k_tiles = [k.rearrange("(a g) d s -> a (g d) s", g=P // HD) for k in (k_hi, k_lo)]

    project(nc, x, w_qk, b_qk, w_v, b_v, rope, ident, q_hi, q_lo, k_tiles[0], k_tiles[1], v_all)
    wa = [kept(f"wa_kept_{k}", [KC, P, WA], F32R) for k in ("hi", "lo")]
    with ExitStack() as ctx:
        wd = [ctx.enter_context(nc.sbuf_tensor(f"wd_{k}", [P, KC, HID], F32R)) for k in ("hi", "lo")]
        context = Context(nc, ctx, o_all, sums, inv_sums, wd)
        attend(nc, masks, ident, q_hi, q_lo, k_hi, k_lo, v_all, o_all, sums, w_dense, w_all, wd, wa,
               b_dense, b_base, b_lora, rev_index, context)
        finish(nc, wd, wa, x, context, out)


def rope_table():
    half = np.arange(0, HD, 2, dtype=np.float32) / np.float32(HD)
    inv_freq = (np.float32(1.0) / np.power(np.float32(1000000.0), half)).astype(np.float32)
    freqs = np.outer(np.arange(SEQ, dtype=np.float32), inv_freq).astype(np.float32)
    emb = np.concatenate([freqs, freqs], axis=-1).astype(np.float64)
    cos, sin = np.cos(emb), np.sin(emb)
    sin[:, :HD // 2] *= -1.0
    table = np.stack([np.tile(cos.T, (P // HD, 1)), np.tile(sin.T, (P // HD, 1))], axis=1)
    table = table.reshape(P, 2, UPB, TG).transpose(2, 0, 1, 3)
    return np.ascontiguousarray(np.tile(table, (BATCH, 1, 1, 1)).astype(np.float32))


def kernel(L0_attn_hidden_states, L0_attn_w_qkv, L0_attn_b_qkv, L0_attn_w_dense, L0_attn_b_dense,
           L0_ffn_W_base, L0_ffn_b_base, L0_ffn_W_router, L0_ffn_A, L0_ffn_B):
    import concourse.bacc as bacc
    from concourse.bass_utils import run_bass_kernel_spmd

    arr = np.asarray
    w = arr(L0_attn_w_qkv).reshape(GROUPS, QPG + 2, HD, HID)
    b = arr(L0_attn_b_qkv).reshape(GROUPS, QPG + 2, HD)
    w_qk = np.concatenate([w[:, :QPG].reshape(-1, HID), w[:, QPG].reshape(-1, HID)]).T
    b_qk = np.concatenate([b[:, :QPG].reshape(-1), b[:, QPG].reshape(-1)]).reshape(QK_TILES, P).T
    w_base = arr(L0_ffn_W_base)
    lora_a = arr(L0_ffn_A).reshape(ER, HID)
    masks = np.zeros((P, P + BLOCK), np.float32)
    masks[:, :P][np.triu_indices(P, 1)] = NEG
    masks[P // 2:, P:] = NEG
    given = {
        "x": arr(L0_attn_hidden_states).reshape(BATCH * SEQ, HID),
        "w_qk": w_qk,
        "b_qk": b_qk,
        "w_v": w[:, QPG + 1].reshape(-1, HID).T,
        "b_v": b[:, QPG + 1].reshape(-1),
        "w_dense": arr(L0_attn_w_dense).T,
        "b_dense": arr(L0_attn_b_dense),
        "w_all": np.concatenate([arr(L0_ffn_W_router), lora_a, w_base[HEAD_COLS:], w_base[:HEAD_COLS]]).T,
        "b_base": arr(L0_ffn_b_base),
        "b_lora": arr(L0_ffn_B).transpose(0, 2, 1).reshape(ER, HID),
        "rope": rope_table(),
        "ident": np.eye(P, dtype=np.float32),
        "masks": masks,
        "rev_index": np.arange(EXPERTS, 0, -1).astype(np.float32),
    }
    given = {k: np.ascontiguousarray(v) for k, v in given.items()}
    nc = bacc.Bacc("TRN2", target_bir_lowering=False, num_devices=1)
    aps = [nc.dram_tensor(f"{k}_dram", v.shape, F32, kind="ExternalInput").ap() for k, v in given.items()]
    out = nc.dram_tensor("out_dram", [BATCH * SEQ, HID], F32, kind="ExternalOutput").ap()
    build(nc, *aps, out)
    result = run_bass_kernel_spmd(nc, [{f"{k}_dram": v for k, v in given.items()}], core_ids=[0])
    return result.results[0]["out_dram"].reshape(BATCH, SEQ, HID)
```
